# Optimizing a Trainium2 kernel written in Bass

```python
import numpy as np
import jax
import jax.numpy as jnp

def _softmax(x, axis=-1):
    return jax.nn.softmax(x, axis=axis)

def _gelu(x):
    return jax.nn.gelu(x, approximate=True)

def _silu(x):
    return jax.nn.silu(x)

def _sigmoid(x):
    return jax.nn.sigmoid(x)

def _layernorm(x, axis=-1, eps=1e-05):
    m = jnp.mean(x, axis=axis, keepdims=True)
    v = jnp.var(x, axis=axis, keepdims=True)
    return (x - m) / jnp.sqrt(v + eps)

def _scatter_add(tgt, idx, src, axis=0):
    return tgt.at[idx].add(src)

def _segment_sum(src, seg, n):
    return jax.ops.segment_sum(src, seg, n)
kernel_name = 'mk_adj_ffn_d2_adj_r2_d2cb08'

def setup_inputs(seed: int=0):
    np.random.seed(seed)
    _w = jnp.asarray

    def _rec_inputs():
        import jax
        import jax.numpy as jnp
        _gk = jax.random.key(seed)
        x = -0.0005207 + 1.001 * jax.random.normal(jax.random.fold_in(_gk, 1), (8, 1024, 128), jnp.float32)
        _a = jax.random.bernoulli(jax.random.fold_in(_gk, 2), 0.00195312, (1024, 1024))
        adj = _a.astype(jnp.int32)
        return (x, adj)
    x, adj = _rec_inputs()

    def _L0_gnn_setup():
        import jax, jax.numpy as jnp
        import numpy as np
        import math
        CHUNK = 128
        NUM_HEADS = 4
        EPS = 1e-05
        key = jax.random.key(seed)
        ks = jax.random.split(key, 12)
        B, N, F = (4, 1024, 128)
        x = jax.random.normal(ks[0], (B, N, F), dtype=jnp.float32)
        adj_matrix = jax.random.randint(ks[1], (N, N), 0, 2, dtype=jnp.int32)
        s = 1.0 / math.sqrt(F)
        Wq = jax.random.normal(ks[2], (F, F), dtype=jnp.float32) * s
        bq = jnp.zeros((F,), dtype=jnp.float32)
        Wk = jax.random.normal(ks[3], (F, F), dtype=jnp.float32) * s
        bk = jnp.zeros((F,), dtype=jnp.float32)
        Wv = jax.random.normal(ks[4], (F, F), dtype=jnp.float32) * s
        bv = jnp.zeros((F,), dtype=jnp.float32)
        Wo = jax.random.normal(ks[5], (F, F), dtype=jnp.float32) * s
        bo = jnp.zeros((F,), dtype=jnp.float32)
        gamma = jnp.ones((F,), dtype=jnp.float32)
        beta = jnp.zeros((F,), dtype=jnp.float32)
        return {'x': x, 'adj_matrix': adj_matrix, 'Wq': Wq, 'bq': bq, 'Wk': Wk, 'bk': bk, 'Wv': Wv, 'bv': bv, 'Wo': Wo, 'bo': bo, 'gamma': gamma, 'beta': beta}
    _L0_gnn_all = _L0_gnn_setup()
    _L0_gnn_in = {k: v for k, v in _L0_gnn_all.items() if k in ('Wq', 'bq', 'Wk', 'bk', 'Wv', 'bv', 'Wo', 'bo', 'gamma', 'beta')}
    del _L0_gnn_all

    def _L0_ffn_setup():
        import jax, jax.numpy as jnp
        import numpy as np
        D_MODEL = 128
        EXPERT_DIM = 256
        NUM_EXPERTS = 8
        TOP_K = 2
        SEQ_LEN = 1024
        BATCH = 2
        key = jax.random.key(seed)
        ks = jax.random.split(key, 8)
        s = 0.02
        x = jax.random.normal(ks[0], (SEQ_LEN, BATCH, D_MODEL), dtype=jnp.float32)
        Wg = jax.random.normal(ks[1], (D_MODEL, NUM_EXPERTS), dtype=jnp.float32) * s
        bg = jax.random.normal(ks[2], (NUM_EXPERTS,), dtype=jnp.float32) * s
        bias = jnp.zeros((NUM_EXPERTS,), dtype=jnp.float32)
        W1 = jax.random.normal(ks[3], (NUM_EXPERTS, D_MODEL, EXPERT_DIM), dtype=jnp.float32) * s
        b1 = jax.random.normal(ks[4], (NUM_EXPERTS, EXPERT_DIM), dtype=jnp.float32) * s
        W2 = jax.random.normal(ks[5], (NUM_EXPERTS, EXPERT_DIM, D_MODEL), dtype=jnp.float32) * s
        b2 = jax.random.normal(ks[6], (NUM_EXPERTS, D_MODEL), dtype=jnp.float32) * s
        return {'x': x, 'Wg': Wg, 'bg': bg, 'bias': bias, 'W1': W1, 'b1': b1, 'W2': W2, 'b2': b2}
    _L0_ffn_all = _L0_ffn_setup()
    _L0_ffn_in = {k: v for k, v in _L0_ffn_all.items() if k in ('Wg', 'bg', 'bias', 'W1', 'b1', 'W2', 'b2')}
    del _L0_ffn_all

    def _L1_gnn_setup():
        import jax, jax.numpy as jnp
        import numpy as np
        ALPHA = 0.2
        MASK_VAL = -9000000000000000.0
        key = jax.random.key(seed)
        k1, k2, k3, k4 = jax.random.split(key, 4)
        B, N, F = (8, 512, 128)
        H, OUT = (4, 128)
        hs = OUT // H
        x = jax.random.normal(k1, (B, N, F), dtype=jnp.float32)
        adj = jax.random.randint(k2, (N, N), 0, 2, dtype=jnp.int32)
        wb = float(np.sqrt(6.0 / (F + hs)))
        ab = float(np.sqrt(6.0 / (H + 2 * hs)))
        W = jax.random.uniform(k3, (H, F, hs), dtype=jnp.float32, minval=-wb, maxval=wb)
        a = jax.random.uniform(k4, (H, 2 * hs), dtype=jnp.float32, minval=-ab, maxval=ab)
        return {'x': x, 'adj': adj, 'W': W, 'a': a}
    _L1_gnn_all = _L1_gnn_setup()
    _L1_gnn_in = {k: v for k, v in _L1_gnn_all.items() if k in ('W', 'a')}
    del _L1_gnn_all

    def _L1_ffn_setup():
        import jax, jax.numpy as jnp
        import numpy as np
        C = 128
        HID = 512
        E = 8
        TEMP = 1.0
        key = jax.random.key(seed)
        ks = jax.random.split(key, 7)
        x = jax.random.normal(ks[0], (8, 8192, C), dtype=jnp.float32)
        W1 = jax.random.normal(ks[1], (C, HID), dtype=jnp.float32) * 0.02
        b1 = jnp.zeros((HID,), dtype=jnp.float32)
        Wg = jax.random.normal(ks[2], (HID, E), dtype=jnp.float32) * 0.02
        bg = jnp.zeros((E,), dtype=jnp.float32)
        Wd = jax.random.normal(ks[3], (E, HID, C), dtype=jnp.float32) * 0.02
        bd = jnp.zeros((E, C), dtype=jnp.float32)
        return {'x': x, 'W1': W1, 'b1': b1, 'Wg': Wg, 'bg': bg, 'Wd': Wd, 'bd': bd}
    _L1_ffn_all = _L1_ffn_setup()
    _L1_ffn_in = {k: v for k, v in _L1_ffn_all.items() if k in ('W1', 'b1', 'Wg', 'bg', 'Wd', 'bd')}
    del _L1_ffn_all
    return {'x': x, 'adj': adj, 'L0_gnn_Wq': _L0_gnn_in['Wq'], 'L0_gnn_bq': _L0_gnn_in['bq'], 'L0_gnn_Wk': _L0_gnn_in['Wk'], 'L0_gnn_bk': _L0_gnn_in['bk'], 'L0_gnn_Wv': _L0_gnn_in['Wv'], 'L0_gnn_bv': _L0_gnn_in['bv'], 'L0_gnn_Wo': _L0_gnn_in['Wo'], 'L0_gnn_bo': _L0_gnn_in['bo'], 'L0_gnn_gamma': _L0_gnn_in['gamma'], 'L0_gnn_beta': _L0_gnn_in['beta'], 'L0_ffn_Wg': _L0_ffn_in['Wg'], 'L0_ffn_bg': _L0_ffn_in['bg'], 'L0_ffn_bias': _L0_ffn_in['bias'], 'L0_ffn_W1': _L0_ffn_in['W1'], 'L0_ffn_b1': _L0_ffn_in['b1'], 'L0_ffn_W2': _L0_ffn_in['W2'], 'L0_ffn_b2': _L0_ffn_in['b2'], 'L1_gnn_W': _L1_gnn_in['W'], 'L1_gnn_a': _L1_gnn_in['a'], 'L1_ffn_W1': _L1_ffn_in['W1'], 'L1_ffn_b1': _L1_ffn_in['b1'], 'L1_ffn_Wg': _L1_ffn_in['Wg'], 'L1_ffn_bg': _L1_ffn_in['bg'], 'L1_ffn_Wd': _L1_ffn_in['Wd'], 'L1_ffn_bd': _L1_ffn_in['bd']}

def reference(x, adj, L0_gnn_Wq, L0_gnn_bq, L0_gnn_Wk, L0_gnn_bk, L0_gnn_Wv, L0_gnn_bv, L0_gnn_Wo, L0_gnn_bo, L0_gnn_gamma, L0_gnn_beta, L0_ffn_Wg, L0_ffn_bg, L0_ffn_bias, L0_ffn_W1, L0_ffn_b1, L0_ffn_W2, L0_ffn_b2, L1_gnn_W, L1_gnn_a, L1_ffn_W1, L1_ffn_b1, L1_ffn_Wg, L1_ffn_bg, L1_ffn_Wd, L1_ffn_bd):
    import jax
    import jax.numpy as jnp

    def _L0_gnn_ref(x, adj_matrix, Wq, bq, Wk, bk, Wv, bv, Wo, bo, gamma, beta):
        import jax, jax.numpy as jnp
        import numpy as np
        import math
        CHUNK = 128
        NUM_HEADS = 4
        EPS = 1e-05
        B, N, Fin = x.shape
        H = NUM_HEADS
        Dout = Wq.shape[0]
        Dh = Dout // H
        Nc = N // CHUNK
        q = (x @ Wq.T + bq).reshape(B, N, H, Dh).transpose(0, 2, 1, 3)
        k = (x @ Wk.T + bk).reshape(B, N, H, Dh).transpose(0, 2, 1, 3)
        v = (x @ Wv.T + bv).reshape(B, N, H, Dh).transpose(0, 2, 1, 3)
        kc = k.reshape(B, H, Nc, CHUNK, Dh)
        vc = v.reshape(B, H, Nc, CHUNK, Dh)
        scores = jnp.einsum('bhnd,bhjcd->bhnjc', q, kc) / jnp.sqrt(jnp.asarray(Dh, dtype=q.dtype))
        scores = jnp.clip(scores, -10.0, 10.0)
        mask = adj_matrix.reshape(N, Nc, CHUNK)[None, None]
        scores = jnp.where(mask == 0, jnp.asarray(-10.0, scores.dtype), scores)
        attn = jax.nn.softmax(scores, axis=-1)
        ctx = jnp.einsum('bhnjc,bhjcd->bhnd', attn, vc)
        ctx = ctx.transpose(0, 2, 1, 3).reshape(B, N, Dout)
        out = ctx @ Wo.T + bo
        out = out + x
        mu = jnp.mean(out, axis=-1, keepdims=True)
        var = jnp.mean(jnp.square(out - mu), axis=-1, keepdims=True)
        out = (out - mu) * jax.lax.rsqrt(var + EPS) * gamma + beta
        return out

    def _L0_ffn_ref(x, Wg, bg, bias, W1, b1, W2, b2):
        import jax, jax.numpy as jnp
        import numpy as np
        D_MODEL = 128
        EXPERT_DIM = 256
        NUM_EXPERTS = 8
        TOP_K = 2
        SEQ_LEN = 1024
        BATCH = 2
        x_flat = x.reshape(-1, D_MODEL)
        gate_logits = x_flat @ Wg + bg + bias
        topk_vals, topk_idx = jax.lax.top_k(gate_logits, TOP_K)
        topk_w = jax.nn.softmax(topk_vals, axis=-1)
        combine = (jax.nn.one_hot(topk_idx, NUM_EXPERTS, dtype=x.dtype) * topk_w[..., None]).sum(axis=1)
        h = jax.nn.relu(jnp.einsum('td,edh->teh', x_flat, W1) + b1)
        y = jnp.einsum('teh,ehd->ted', h, W2) + b2
        out = jnp.einsum('ted,te->td', y, combine)
        return out.reshape(x.shape)

    def _L1_gnn_ref(x, adj, W, a):
        import jax, jax.numpy as jnp
        import numpy as np
        ALPHA = 0.2
        MASK_VAL = -9000000000000000.0
        B, N, _ = x.shape
        H, _, hs = W.shape
        Wh = jnp.einsum('bnf,hfd->bhnd', x, W)
        a1, a2 = (a[:, :hs], a[:, hs:])
        ei = jnp.einsum('bhnd,hd->bhn', Wh, a1)
        ej = jnp.einsum('bhnd,hd->bhn', Wh, a2)
        e = ei[:, :, :, None] + ej[:, :, None, :]
        e = jnp.where(e > 0, e, ALPHA * e)
        e = jnp.where(adj[None, None] > 0, e, MASK_VAL)
        att = jax.nn.softmax(e, axis=-1)
        h = jnp.einsum('bhij,bhjd->bhid', att, Wh)
        h = h.transpose(0, 2, 1, 3).reshape(B, N, H * hs)
        return jax.nn.elu(h)

    def _L1_ffn_ref(x, W1, b1, Wg, bg, Wd, bd):
        import jax, jax.numpy as jnp
        import numpy as np
        C = 128
        HID = 512
        E = 8
        TEMP = 1.0
        orig_shape = x.shape
        xf = x.reshape(-1, orig_shape[-1])
        H = jax.nn.gelu(xf @ W1 + b1, approximate=False)
        probs = jax.nn.softmax((H @ Wg + bg) / TEMP, axis=-1)
        assign = jnp.argmax(probs, axis=-1)
        out = jnp.zeros_like(xf)
        for e in range(Wd.shape[0]):
            y = H @ Wd[e] + bd[e]
            sel = (assign == e)[:, None]
            out = out + jnp.where(sel, probs[:, e:e + 1] * y, 0.0)
        return out.reshape(orig_shape)
    x = x + _L0_gnn_ref(_layernorm(x, axis=-1), adj, L0_gnn_Wq, L0_gnn_bq, L0_gnn_Wk, L0_gnn_bk, L0_gnn_Wv, L0_gnn_bv, L0_gnn_Wo, L0_gnn_bo, L0_gnn_gamma, L0_gnn_beta)
    x = x + _L0_ffn_ref(_layernorm(x, axis=-1), L0_ffn_Wg, L0_ffn_bg, L0_ffn_bias, L0_ffn_W1, L0_ffn_b1, L0_ffn_W2, L0_ffn_b2)
    x = x + _L1_gnn_ref(_layernorm(x, axis=-1), adj, L1_gnn_W, L1_gnn_a)
    x = x + _L1_ffn_ref(_layernorm(x, axis=-1), L1_ffn_W1, L1_ffn_b1, L1_ffn_Wg, L1_ffn_bg, L1_ffn_Wd, L1_ffn_bd)
    return x

_drawn_inputs = setup_inputs


def setup_inputs(seed=0):
    import zlib

    import numpy as np

    out = dict(_drawn_inputs(seed))
    spreads = {'L0_gnn_bq': (0.0, 0.8),
     'L0_gnn_bk': (0.0, 0.8),
     'L0_gnn_bv': (0.0, 0.1),
     'L0_gnn_bo': (0.0, 0.1),
     'L0_gnn_gamma': (1.0, 0.2),
     'L0_gnn_beta': (0.0, 0.1),
     'L0_ffn_bias': (0.0, 0.468),
     'L1_ffn_b1': (0.0, 0.8),
     'L1_ffn_bg': (0.0, 0.8),
     'L1_ffn_bd': (0.0, 0.8)}
    factors = {'L0_ffn_Wg': 2.969,
     'L0_ffn_bg': 8.0,
     'L0_ffn_W1': 3.271,
     'L0_ffn_b1': 8.0,
     'L0_ffn_W2': 2.699,
     'L0_ffn_b2': 6.553,
     'L1_ffn_W1': 7.92,
     'L1_ffn_Wg': 8.0,
     'L1_ffn_Wd': 8.0}
    for name, (base, spread) in spreads.items():
        noise = np.random.default_rng([zlib.crc32(name.encode()), seed]).standard_normal(out[name].shape)
        drawn = base * np.exp(spread * noise) if base else spread * noise
        out[name] = jnp.asarray(drawn.astype(out[name].dtype))
    for name, factor in factors.items():
        out[name] = (out[name] * factor).astype(out[name].dtype)
    return out
```

```python
from contextlib import ExitStack

import concourse.bass as bass
from concourse import mybir
import numpy as np

ALU = mybir.AluOpType
ACT = mybir.ActivationFunctionType
AX = mybir.AxisListType
F32 = mybir.dt.float32
F16 = mybir.dt.float16
BF16 = mybir.dt.bfloat16
I32 = mybir.dt.int32

P = 128
B, N, D = 8, 1024, 128
H, HS = 4, 32
E = 8
C = N // P
EPS = 1e-5
CLIP = 10.0
E_HI = float(np.float32(np.exp(CLIP)))
E_LO = float(np.float32(np.exp(-CLIP)))
SCALE = float(HS) ** -0.5
SLOPE = 0.2


class Steps:

    def __init__(self, eng, sem, base=0):
        self.eng, self.sem, self.base, self.n = eng, sem, base, 0

    def did(self, ins):
        self.n += 1
        ins.then_inc(self.sem, 1)
        return ins

    def wait(self):
        self.eng.wait_ge(self.sem, self.base + self.n)


def halves(ap):
    return [ap[:, 0:512], ap[:, 512:1024]]


COMBINE = 7


def combine_stats(nc, steps, stats, mean, var_eps, tmp):
    ms, ds, vs = tmp[:, 0], tmp[:, 1], tmp[:, 2]
    tt, stt = nc.vector.tensor_tensor, nc.vector.scalar_tensor_tensor
    steps.did(tt(ms, stats[:, :, 1], stats[:, :, 4], ALU.add))
    steps.did(tt(ds, stats[:, :, 1], stats[:, :, 4], ALU.subtract))
    steps.did(tt(vs, stats[:, :, 2], stats[:, :, 5], ALU.add))
    steps.wait()
    steps.did(nc.vector.tensor_scalar(mean, ms, 0.5, None, ALU.mult))
    steps.did(stt(out=ds, in0=ds, scalar=0.25, in1=ds, op0=ALU.mult, op1=ALU.mult))
    steps.did(nc.vector.tensor_scalar(vs, vs, 1.0 / D, EPS, ALU.mult, ALU.add))
    steps.wait()
    steps.did(tt(var_eps, vs, ds, ALU.add))


class Core:

    def __init__(self, nc, ctx, t):
        self.nc, self.ctx, self.t = nc, ctx, t
        sb = self.sb
        self.x = sb("x_res", [P, B * C, D], F32)
        self.bound = sb("bound", [P, C, N], F32)
        self.lone = sb("lone", [P, N], F32)
        self.lone16 = sb("lone16", [P, N], BF16)
        self.ident = sb("ident_sb", [P, P], F32)
        self.ident16 = sb("ident16", [P, P], BF16)
        self.ones = sb("ones", [P, HS], F32)
        self.minus_half = sb("minus_half", [P, B * C], F32)
        self.mv = sb("mv", [P, B * C, 2], F32)
        self.var_eps = sb("var_eps", [P, B * C], F32)
        self.rstd = sb("rstd", [P, B * C], F32)
        self.wo_bias = sb("wo_bias", [P, D], F32)
        self.gamma = sb("gamma_sb", [P, D], F32)
        self.beta = sb("beta_sb", [P, D], F32)
        self.w0 = sb("w0", [P, 4, D], F32)
        self.bqkv = sb("bqkv", [P, 3], F32)
        self.arena = sb("arena", [P, ARENA // 4], F32)
        self.ps = ctx.enter_context(nc.psum_tensor("ps", [P, 8, 512], F32))

    def sb(self, name, shape, dt):
        return self.ctx.enter_context(self.nc.sbuf_tensor(name, shape, dt))

    def sem(self, name):
        return self.ctx.enter_context(self.nc.semaphore(name))

    def dram(self, name, shape, dt):
        return self.nc.dram_tensor(name, shape, dt).ap()

    def bank2(self, k):
        return self.ps[:, k:k + 2, :].rearrange("p a n -> p (a n)")


class Arena:

    def __init__(self, core):
        self.core, self.at = core, 0

    def take(self, shape, dt=F32):
        size = 2 if dt in (F16, BF16) else 4
        words = int(np.prod(shape)) * size // 4
        ap = self.core.arena[:, self.at:self.at + words]
        self.at += words
        assert self.at * 4 <= ARENA, self.at * 4
        if dt != F32:
            ap = ap.bitcast(dt)
        if len(shape) == 1:
            return ap
        names = "abcd"[:len(shape)]
        sizes = {n: s for n, s in zip(names, shape)}
        return ap.rearrange(f"p ({' '.join(names)}) -> p {' '.join(names)}", **sizes)


ARENA = 129 * 1024 + 768


def tile_rows(dram):
    return dram.rearrange("(n p) f -> p n f", p=P)


def setup(k, scr):
    nc, t = k.nc, k.t
    a = Arena(k)
    adj = a.take([C, N], I32)
    code = a.take([C, N], BF16)
    nonzero = a.take([C, N], BF16)
    edge = a.take([C, N], BF16)
    ones16 = a.take([P], BF16)
    bv_cols = a.take([P])
    bo_rows = a.take([D])

    adj_loaded = [k.sem(f"adj_loaded{i}") for i in range(C)]
    x_loaded = k.sem("x_loaded")
    weights_loaded = k.sem("weights_loaded")
    code_ready = k.sem("code_ready")
    turned = k.sem("turned")
    masks_ready = k.sem("masks_ready")
    counted = k.sem("counted")
    consts_ready = k.sem("consts_ready")
    bias_made = k.sem("bias_made")
    edge_stored = k.sem("edge_stored")
    stats_done = k.sem("s_stats_done")
    mv_done = k.sem("s_mv_done")
    stats = a.take([B * C, 6])
    n_weights = 11
    xt = tile_rows(t["x"].rearrange("b n f -> (b n) f"))
    adj_t = tile_rows(t["adj"])

    with nc.Block() as block:
        @block.sync
        def _(sp):
            for i in range(C):
                sp.dma_start(adj[:, i, :], adj_t[:, i, :]).then_inc(adj_loaded[i], 16)
            for b in range(B):
                sp.dma_start(k.x[:, b * C:(b + 1) * C, :], xt[:, b * C:(b + 1) * C, :]).then_inc(x_loaded, 16)
            sp.wait_ge(masks_ready, 2 * C)
            sp.dma_start(scr.edge, edge).then_inc(edge_stored, 16)
            sp.wait_ge(edge_stored, 16)

        @block.scalar
        def _(act):
            loads = [(k.ident[:], t["ident"])]
            loads += [(k.w0[:, i, :], t[w]) for i, w in enumerate(("L0_gnn_WqT", "L0_gnn_WkT", "L0_gnn_WvT", "L0_gnn_WoT"))]
            loads += [(k.bqkv[:, i:i + 1], t[w].rearrange("(p o) -> p o", o=1))
                      for i, w in enumerate(("L0_gnn_bq", "L0_gnn_bk", "L0_gnn_bv"))]
            loads += [(dst, t[w].rearrange("(o f) -> o f", o=1).to_broadcast([P, D]))
                      for dst, w in ((bo_rows, "L0_gnn_bo"), (k.gamma[:], "L0_gnn_gamma"), (k.beta[:], "L0_gnn_beta"))]
            assert len(loads) == n_weights
            for dst, src in loads:
                act.dma_start(dst, src).then_inc(weights_loaded, 16)

        @block.gpsimd
        def _(pool):
            nc.gpsimd.memset(k.ones[:], 1.0)
            nc.gpsimd.memset(ones16, 1.0)
            nc.gpsimd.memset(k.minus_half[:], -0.5).then_inc(consts_ready, 1)
            pool.wait_ge(consts_ready, 1)
            pool.wait_ge(mv_done, B * C + 1)
            nc.gpsimd.tensor_tensor(k.rstd[:], k.var_eps[:], k.minus_half[:], ALU.pow)

        @block.vector
        def _(dve):
            dve.wait_ge(weights_loaded, 16 * n_weights)
            nc.vector.tensor_copy(k.ident16[:], k.ident[:])
            nc.vector.tensor_copy(bv_cols, k.bqkv[:, 2:3].to_broadcast([P, P])).then_inc(code_ready, 1)
            for i in range(C):
                dve.wait_ge(adj_loaded[i], 16)
                nc.vector.tensor_scalar(nonzero[:, i, :], adj[:, i, :], 0.0, None, ALU.not_equal).then_inc(code_ready, 1)
                dve.wait_ge(code_ready, 2 * i + 2)
                nc.vector.scalar_tensor_tensor(out=code[:, i, :], in0=adj[:, i, :], scalar=0.0, in1=nonzero[:, i, :],
                                               op0=ALU.is_gt, op1=ALU.add).then_inc(code_ready, 1)
            for c in range(C):
                flags = k.ps[:, c % 4, :].bitcast(BF16)
                dve.wait_ge(turned, c + 1)
                nc.vector.tensor_scalar(edge[:, c, :], flags, 1.5, None, ALU.is_ge).then_inc(masks_ready, 1)
                nc.vector.tensor_scalar(k.bound[:, c, :], flags, 1.0, E_HI, ALU.min, ALU.mult).then_inc(masks_ready, 1)
            for c in range(C):
                dve.wait_ge(masks_ready, 2 * C + c)
                nc.vector.tensor_scalar(k.bound[:, c, :], k.bound[:, c, :], E_LO, None, ALU.max).then_inc(masks_ready, 1)
            dve.wait_ge(counted, 1)
            nc.vector.tensor_scalar(k.lone[:], k.bank2(6), 0.0, None, ALU.is_equal).then_inc(masks_ready, 1)
            dve.wait_ge(masks_ready, 3 * C + 1)
            nc.vector.tensor_copy(k.lone16[:], k.lone[:])
            dve.wait_ge(bias_made, 1)
            nc.vector.scalar_tensor_tensor(out=k.wo_bias[:], in0=k.ps[:, 4, 0:D], scalar=float(C), in1=bo_rows,
                                           op0=ALU.mult, op1=ALU.add)
            dve.wait_ge(x_loaded, 16 * B)
            for i in range(B * C):
                nc.vector.bn_stats(stats[:, i, :], k.x[:, i, :]).then_inc(stats_done, 1)
            for i in range(B * C):
                dve.wait_ge(stats_done, i + 1)
                nc.vector.bn_aggr(k.mv[:, i, :], stats[:, i, :]).then_inc(mv_done, 1)
            dve.wait_ge(mv_done, B * C)
            nc.vector.tensor_scalar(k.var_eps[:], k.mv[:, :, 1], EPS, None, ALU.add).then_inc(mv_done, 1)

        @block.tensor
        def _(pe):
            pe.wait_ge(code_ready, 2 * C + 1)
            for c in range(C):
                if c >= 4:
                    pe.wait_ge(masks_ready, 2 * (c - 3))
                flags = k.ps[:, c % 4, :].bitcast(BF16)
                for i in range(C):
                    last = nc.tensor.transpose(flags[:, i * P:(i + 1) * P], code[:, i, c * P:(c + 1) * P], k.ident16[:])
                last.then_inc(turned, 1)
            pe.wait_ge(consts_ready, 1)
            nc.tensor.matmul(k.ps[:, 4, 0:D], bv_cols, k.w0[:, 3, :], start=True, stop=True).then_inc(bias_made, 1)
            pe.wait_ge(masks_ready, 2 * C)
            for half in range(2):
                for c in range(C):
                    last = nc.tensor.matmul(k.ps[:, 6 + half, :], ones16, edge[:, c, half * 512:(half + 1) * 512],
                                            start=(c == 0), stop=(c == C - 1))
            last.then_inc(counted, 1)


class Scratch:

    def __init__(self, k):
        self.parts = k.dram("qk_parts", [B, 4, P, N], F16)
        self.v = k.dram("v_rows", [B, P, N], F32)
        self.xb = k.dram("x_bias", [B, P, N], F32)
        self.den = k.dram("den_rows", [2, H, N], F32)
        self.rec = k.dram("rec_rows", [2, H, N], F32)
        self.edge = k.dram("edge_rows", [P, C, N], BF16)
        self.xnT = k.dram("xn_turned", [B, P, N], F32)
        self.combT = k.dram("expert_weights", [B * C, E, P], F32)
        self.gv = k.dram("gat_values", [B, 2, P, N], F32)
        self.gs = k.dram("gat_small", [B, P, C * H + D], F32)
        self.grow = k.dram("gat_rows", [B, H * N], F32)
        self.gden = k.dram("gat_den", [2, H, N], F32)
        self.grec = k.dram("gat_rec", [2, H, N], F32)


def rows_of(k, b):
    return [k.x[:, bass.ds(b * C + i, 1), :].rearrange("p o f -> p (o f)") for i in range(C)]


def qkv(k, scr):
    nc = k.nc
    a = Arena(k)
    xn = a.take([2, C, D])
    xnT = a.take([2, N])
    xb = a.take([2, C, D])
    parts = a.take([2, 4, N], F16)
    v = a.take([2, N])
    mean = a.take([2, C])
    rstd = a.take([2, C])

    xn_done, turned, xnT_done, proj_done, high_done, low_done, v_copied, xb_done, small_done = [
        k.sem(f"q_{s}") for s in ("xn_done", "turned", "xnT_done", "proj_done", "high_done", "low_done", "v_copied",
                                  "xb_done", "small_done")]
    stored = [k.sem(f"q_stored{u}") for u in range(2)]
    STORES = 4

    with nc.Block() as block:
        @block.vector
        def _(dve):
            dve.sem_inc(low_done, 2)
            with dve.Fori(0, B // 2) as pair:
                for u in range(2):
                    b = 2 * pair + u
                    rows = rows_of(k, b)
                    nc.vector.tensor_copy(mean[:, u, :], k.mv[:, bass.ds(b * C, C), 0]).then_inc(small_done, 1)
                    nc.vector.tensor_copy(rstd[:, u, :], k.rstd[:, bass.ds(b * C, C)]).then_inc(small_done, 1)
                    dve.wait_ge(small_done, 2 * b + 2)
                    dve.wait_ge(turned, b + 1)
                    dve.wait_ge(xb_done, b + 1)
                    for i in range(C):
                        nc.vector.tensor_scalar(xn[:, u, i, :], rows[i], mean[:, u, i:i + 1], rstd[:, u, i:i + 1],
                                                ALU.subtract, ALU.mult).then_inc(xn_done, 1)
                    for j in range(2):
                        dve.wait_ge(high_done, 2 * b + j + 1)
                        nc.vector.scalar_tensor_tensor(
                            out=parts[:, u, 2 * j + 1, :], in0=k.bank2(2 + 2 * j), scalar=k.bqkv[:, j:j + 1],
                            in1=parts[:, u, 2 * j, :], op0=ALU.add, op1=ALU.subtract).then_inc(low_done, 1)

        @block.tensor
        def _(pe):
            pe.sem_inc(turned, 2)
            pe.sem_inc(proj_done, 6)
            with pe.Fori(0, B // 2) as pair:
                for u in range(2):
                    b = 2 * pair + u
                    pe.wait_ge(xn_done, (b + 1) * C)
                    pe.wait_ge(xnT_done, b + 1)
                    for i in range(C):
                        last = nc.tensor.transpose(k.bank2(0)[:, i * P:(i + 1) * P], xn[:, u, i, :], k.ident[:])
                    last.then_inc(turned, 1)
                    pe.wait_ge(xnT_done, b + 2)
                    for j in range(2):
                        pe.wait_ge(low_done, 2 * b + j + 1)
                        for half in range(2):
                            last = nc.tensor.matmul(k.ps[:, 2 + 2 * j + half, :], k.w0[:, j, :],
                                                    halves(xnT[:, u, :])[half], start=True, stop=True)
                        last.then_inc(proj_done, 1)
                    pe.wait_ge(v_copied, b + 1)
                    for i in range(C):
                        last = nc.tensor.matmul(k.bank2(6)[:, i * P:(i + 1) * P], xnT[:, u, i * P:(i + 1) * P],
                                                k.w0[:, 2, :], start=True, stop=True)
                    last.then_inc(proj_done, 1)

        @block.scalar
        def _(act):
            act.sem_inc(xnT_done, 1)
            act.sem_inc(v_copied, 1)
            with act.Fori(0, B // 2) as pair:
                for u in range(2):
                    b = 2 * pair + u
                    act.wait_ge(turned, b + 3)
                    act.wait_ge(proj_done, 3 * b + 3)
                    nc.scalar.copy(xnT[:, u, :], k.bank2(0)).then_inc(xnT_done, 1)
                    act.wait_ge(stored[u], 16 * STORES * (pair + 1))
                    for j in range(2):
                        act.wait_ge(proj_done, 3 * b + 7 + j)
                        nc.scalar.activation(parts[:, u, 2 * j, :], k.bank2(2 + 2 * j), ACT.Identity,
                                             bias=k.bqkv[:, j:j + 1]).then_inc(high_done, 1)
                    act.wait_ge(proj_done, 3 * b + 9)
                    nc.scalar.copy(v[:, u, :], k.bank2(6)).then_inc(v_copied, 1)

        @block.gpsimd
        def _(pool):
            pool.sem_inc(xb_done, 2)
            with pool.Fori(0, B // 2) as pair:
                for u in range(2):
                    b = 2 * pair + u
                    pool.wait_ge(xn_done, (b + 1) * C)
                    pool.wait_ge(stored[u], 16 * STORES * (pair + 1))
                    nc.gpsimd.tensor_tensor(xb[:, u, :, :], xn[:, u, :, :],
                                            k.wo_bias[:].unsqueeze(1).to_broadcast([P, C, D]), ALU.add).then_inc(xb_done, 1)

        @block.sync
        def _(sp):
            for u in range(2):
                sp.sem_inc(stored[u], 16 * STORES)
            with sp.Fori(0, B // 2) as pair:
                for u in range(2):
                    b = 2 * pair + u
                    at = bass.ds(b, 1)
                    sp.wait_ge(low_done, 2 * b + 4)
                    for j in range(2):
                        sp.dma_start(scr.parts[at, 2 * j:2 * j + 2].rearrange("o r p t -> p (o r) t"),
                                     parts[:, u, 2 * j:2 * j + 2, :]).then_inc(stored[u], 16)
                    sp.wait_ge(v_copied, b + 2)
                    sp.dma_start(scr.v[at].rearrange("o p t -> (o p) t"), v[:, u, :]).then_inc(stored[u], 16)
                    sp.wait_ge(xb_done, b + 3)
                    sp.dma_start(scr.xb[at].rearrange("o p t -> (o p) t"),
                                 xb[:, u, :, :].rearrange("p c f -> p (c f)")).then_inc(stored[u], 16)
            for u in range(2):
                sp.wait_ge(stored[u], 16 * STORES * (B // 2 + 1))


class Peeled:

    @staticmethod
    def run(eng, body, last):
        body(0, 0, 0)
        with eng.Fori(0, (B - 2) // 2) as pair:
            body(2 * pair + 1, 1, pair)
            body(2 * pair + 2, 0, pair + 1)
        body(B - 1, (B - 1) % 2, (B - 1) // 2)
        last()

    @staticmethod
    def back(b, u, c, lag):
        if c >= lag:
            return b, u, c - lag
        return None if is_first(b) else (b - 1, 1 - u, c - lag + C)

    @staticmethod
    def tail(lag):
        return [(B - 1, (B - 1) % 2, c) for c in range(C - lag, C)]


def is_first(b):
    return isinstance(b, int) and b == 0


def attention0(k, scr):
    nc = k.nc
    a = Arena(k)
    qs = a.take([2, H, N], F16)
    ks = a.take([2, H, N], F16)
    v = a.take([2, N])
    xb = a.take([N])
    e = a.take([H, N])
    pm = a.take([8, N])
    ctx = a.take([4, N])
    den = a.take([N])
    r_in = a.take([HS])
    r_out = a.take([HS])
    r_rows = a.take([N])
    y = a.take([C, D])
    stats = a.take([C, 6])
    mean = a.take([C])
    tmp = a.take([3, C])
    ve = a.take([C])
    rs = a.take([C])

    loaded = [k.sem(f"a_loaded{u}") for u in range(2)]
    (score_done, exp_done, clip_done, pv_done, copied, recip_done, ctx_done, o_done, den_stored, den_loaded,
     rec_stored, rec_loaded, xb_loaded, y_added, y_done, pow_done, res_done) = [
        k.sem(f"a_{s}") for s in ("score_done", "exp_done", "clip_done", "pv_done", "copied", "recip_done", "ctx_done",
                                  "o_done", "den_stored", "den_loaded", "rec_stored", "rec_loaded", "xb_loaded",
                                  "y_added", "y_done", "pow_done", "res_done")]
    LOADS = 4 + 4 + 1
    RECIP_LAG, CTX_LAG, O_LAG = 2, 3, 4
    Y_AFTER = 4
    VAR = C + COMBINE
    Y_STEPS = VAR + C
    back, tail = Peeled.back, Peeled.tail

    with nc.Block() as block:
        @block.sync
        def _(sp):
            sp.sem_inc(den_stored, 16)

            def load(b, u):
                at = bass.ds(b, 1)
                for r in range(4):
                    for dst, j in ((qs, r // 2), (ks, 2 + r % 2)):
                        sp.dma_start(dst[r * HS:(r + 1) * HS, u, :, :],
                                     scr.parts[at, j].rearrange("o (h d) t -> d (o h) t", h=H)).then_inc(loaded[u], 16)
                sp.dma_start(v[:, u, :], scr.v[at].rearrange("o p t -> (o p) t")).then_inc(loaded[u], 16)

            def store_den(b, u, c):
                g = C * b + c
                sp.wait_ge(copied, 2 * g + 3)
                sp.dma_start(scr.den[c % 2], den[0:P:HS, :]).then_inc(den_stored, 16)

            def load_den(b, u, c):
                g = C * b + c
                sp.wait_ge(den_stored, 16 * g + 32)
                sp.dma_start(r_in[:], scr.den[c % 2].rearrange("h (a t) -> (h a) t", t=HS)).then_inc(den_loaded, 16)

            def store_rec(b, u, c):
                g = C * b + c
                sp.wait_ge(recip_done, g + 1)
                sp.dma_start(scr.rec[c % 2].rearrange("h (a t) -> (h a) t", t=HS), r_out[:]).then_inc(rec_stored, 16)

            def load_rec(b, u, c):
                g = C * b + c
                sp.wait_ge(rec_stored, 16 * g + 16)
                for h in range(H):
                    sp.dma_start(r_rows[h * HS:(h + 1) * HS, :],
                                 scr.rec[c % 2, h:h + 1, :].to_broadcast([HS, N])).then_inc(rec_loaded, 16)

            def round_trip(g, before):
                if g:
                    store_den(*g)
                if before:
                    store_rec(*before)
                if g:
                    load_den(*g)
                if before:
                    load_rec(*before)

            def body(b, u, _):
                if is_first(b):
                    load(0, 0)
                    load(1, 1)
                for c in range(C):
                    round_trip(back(b, u, c, 1), back(b, u, c, 2))
                    if c == 0 and not isinstance(b, int):
                        sp.wait_ge(pv_done, C * b + 2)
                        load(b + 1, 1 - u)
                    if c == 1 and not is_first(b):
                        sp.wait_ge(y_added, b)
                        sp.dma_start(xb[:, :], scr.xb[bass.ds(b - 1, 1)].rearrange("o p t -> (o p) t")).then_inc(xb_loaded, 16)

            def last():
                g6, g7 = tail(2)
                round_trip(g7, g6)
                round_trip(None, g7)
                sp.wait_ge(y_added, B)
                sp.dma_start(xb[:, :], scr.xb[B - 1]).then_inc(xb_loaded, 16)

            Peeled.run(sp, body, last)

        @block.tensor
        def _(pe):
            pe.sem_inc(pv_done, 2)
            pe.sem_inc(o_done, 4)

            def scores(b, u, half_b, c):
                if c == 0:
                    pe.wait_ge(loaded[u], 16 * LOADS * (half_b + 1))
                for h in range(H):
                    for half in range(2):
                        pe.wait_ge(exp_done, 64 * b + 8 * c + 2 * h + half + 1)
                        nc.tensor.matmul(k.ps[:, half, :], ks[:, u, h, c * P:(c + 1) * P], halves(qs[:, u, h, :])[half],
                                         start=True, stop=True).then_inc(score_done, 1)

            def values(b, u, c):
                g = C * b + c
                pe.wait_ge(copied, 2 * g + 2)
                pe.wait_ge(clip_done, 4 * g + 8)
                for half in range(2):
                    for bank in (2, 4):
                        for h in range(H):
                            lhsT = v[:, u, c * P + h * HS:c * P + (h + 1) * HS] if bank == 2 else k.ones[:]
                            last = nc.tensor.matmul(
                                k.ps[h * HS:(h + 1) * HS, bank + half, :], lhsT,
                                halves(pm[:, 4 * (c % 2) + h, :])[half], start=True, stop=True)
                last.then_inc(pv_done, 1)

            def project(b, u, c):
                pe.wait_ge(ctx_done, C * b + c + 1)
                if c == 0:
                    pe.wait_ge(y_added, b + 1)
                for i in range(C):
                    last = nc.tensor.matmul(k.bank2(6)[:, i * P:(i + 1) * P], ctx[:, c % 4, i * P:(i + 1) * P],
                                            k.w0[:, 3, :], start=(c == 0 and i % 4 == 0), stop=(c == C - 1),
                                            skip_group_check=True)
                last.then_inc(o_done, 1)

            def body(b, u, half_b):
                for c in range(C):
                    scores(b, u, half_b, c)
                    if g := back(b, u, c, 1):
                        values(*g)
                    if g := back(b, u, c, O_LAG):
                        project(*g)

            def last():
                values(*tail(1)[0])
                for g in tail(O_LAG):
                    project(*g)

            Peeled.run(pe, body, last)

        @block.scalar
        def _(act):
            act.sem_inc(exp_done, 2)
            act.sem_inc(copied, 2)

            def copy(b, u, c):
                g = C * b + c
                act.wait_ge(pv_done, g + 3)
                act.wait_ge(den_stored, 16 * g + 16)
                nc.scalar.copy(den[:, :], k.bank2(4)).then_inc(copied, 1)
                act.wait_ge(o_done, g + 1)
                nc.scalar.copy(ctx[:, c % 4, :], k.bank2(2)).then_inc(copied, 1)

            def body(b, u, _):
                for c in range(C):
                    for h in range(H):
                        act.wait_ge(clip_done, 32 * b + 4 * c + h + 1)
                        for half in range(2):
                            at = 64 * b + 8 * c + 2 * h + half
                            act.wait_ge(score_done, at + 1)
                            nc.scalar.activation(halves(e[:, h, :])[half], k.ps[:, half, :], ACT.Exp,
                                                 scale=SCALE).then_inc(exp_done, 1)
                    if g := back(b, u, c, 1):
                        copy(*g)

            Peeled.run(act, body, lambda: copy(*tail(1)[0]))

        @block.vector
        def _(dve):
            dve.sem_inc(clip_done, 4)
            dve.sem_inc(y_added, 1)

            def clip(b, u, c):
                dve.wait_ge(pv_done, C * b + c + 1)
                for h in range(H):
                    dve.wait_ge(exp_done, 64 * b + 8 * c + 2 * h + 4)
                    nc.vector.scalar_tensor_tensor(out=pm[:, 4 * (c % 2) + h, :], in0=e[:, h, :], scalar=E_LO,
                                                   in1=k.bound[:, c, :], op0=ALU.max, op1=ALU.min).then_inc(clip_done, 1)

            def reciprocal(b, u, c):
                dve.wait_ge(den_loaded, 16 * (C * b + c) + 16)
                nc.vector.reciprocal(r_out[:], r_in[:]).then_inc(recip_done, 1)

            def quotient(b, u, c):
                g = C * b + c
                dve.wait_ge(rec_loaded, 64 * g + 64)
                dve.wait_ge(copied, 2 * g + 4)
                nc.vector.tensor_tensor(ctx[:, c % 4, :], ctx[:, c % 4, :], r_rows[:, :], ALU.mult).then_inc(ctx_done, 1)

            def statistics(b):
                at = Y_STEPS * b
                dve.wait_ge(o_done, C * b + C + 4)
                dve.wait_ge(xb_loaded, 16 * b + 16)
                dve.wait_ge(res_done, 3 * b + 3)
                flat = y[:, :, :].rearrange("p c f -> p (c f)")
                nc.vector.tensor_tensor(flat, k.bank2(6), xb[:, :], ALU.add).then_inc(y_added, 1)
                dve.wait_ge(y_added, b + 2)
                for i in range(C):
                    nc.vector.bn_stats(stats[:, i, :], y[:, i, :]).then_inc(y_done, 1)
                dve.wait_ge(y_done, at + C)
                combine_stats(nc, Steps(dve, y_done, at + C), stats, mean, ve, tmp)

            def normalise(b):
                dve.wait_ge(pow_done, b + 1)
                for i in range(C):
                    nc.vector.tensor_scalar(y[:, i, :], y[:, i, :], mean[:, i:i + 1], rs[:, i:i + 1],
                                            ALU.subtract, ALU.mult).then_inc(y_done, 1)

            def body(b, u, _):
                for c in range(C):
                    clip(b, u, c)
                    if g := back(b, u, c, CTX_LAG):
                        quotient(*g)
                    if g := back(b, u, c, RECIP_LAG):
                        reciprocal(*g)
                    if c == Y_AFTER and not is_first(b):
                        statistics(b - 1)
                    if c == Y_AFTER + 1 and not is_first(b):
                        normalise(b - 1)

            def last():
                g5, g6, g7 = tail(CTX_LAG)
                quotient(*g5)
                reciprocal(*g6)
                quotient(*g6)
                reciprocal(*g7)
                quotient(*g7)
                statistics(B - 1)
                normalise(B - 1)

            Peeled.run(dve, body, last)

        @block.gpsimd
        def _(pool):
            pool.sem_inc(res_done, 3)
            gamma, beta = [w[:].unsqueeze(1).to_broadcast([P, C, D]) for w in (k.gamma, k.beta)]
            with pool.Fori(0, B) as b:
                pool.wait_ge(y_done, Y_STEPS * b + VAR)
                nc.gpsimd.tensor_tensor(rs[:], ve[:], k.minus_half[:, 0:C], ALU.pow).then_inc(pow_done, 1)
                pool.wait_ge(y_done, Y_STEPS * b + Y_STEPS)
                nc.gpsimd.tensor_tensor(y[:, :, :], y[:, :, :], gamma, ALU.mult).then_inc(res_done, 1)
                pool.wait_ge(res_done, 3 * b + 4)
                nc.gpsimd.tensor_tensor(y[:, :, :], y[:, :, :], beta, ALU.add).then_inc(res_done, 1)
                pool.wait_ge(res_done, 3 * b + 5)
                x = k.x[:, bass.ds(b * C, C), :]
                nc.gpsimd.tensor_tensor(x, x, y[:, :, :], ALU.add).then_inc(res_done, 1)


def layer_norm(k, scr, name):
    nc = k.nc
    a = Arena(k)
    stats = a.take([B * C, 6])
    tmp = a.take([3, B * C])
    xn = a.take([2, C, D])
    xnT = a.take([2, N])
    mean = a.take([2, C])
    rstd = a.take([2, C])
    stats_done, var_done, pow_done, small_done, xn_done, turned, xnT_done = [
        k.sem(f"{name}_{s}") for s in ("stats_done", "var_done", "pow_done", "small_done", "xn_done", "turned", "xnT_done")]
    stored = [k.sem(f"{name}_stored{u}") for u in range(2)]
    means = k.mv[:, :, 0]

    with nc.Block() as block:
        @block.vector
        def _(dve):
            for i in range(B * C):
                nc.vector.bn_stats(stats[:, i, :], k.x[:, i, :]).then_inc(stats_done, 1)
            dve.wait_ge(stats_done, B * C)
            combine_stats(nc, Steps(dve, var_done), stats, means, k.var_eps[:], tmp)
            dve.wait_ge(pow_done, 1)
            with dve.Fori(0, B // 2) as pair:
                for u in range(2):
                    b = 2 * pair + u
                    rows = rows_of(k, b)
                    nc.vector.tensor_copy(mean[:, u, :], k.mv[:, bass.ds(b * C, C), 0]).then_inc(small_done, 1)
                    nc.vector.tensor_copy(rstd[:, u, :], k.rstd[:, bass.ds(b * C, C)]).then_inc(small_done, 1)
                    dve.wait_ge(small_done, 2 * b + 2)
                    dve.wait_ge(turned, b + 1)
                    for i in range(C):
                        nc.vector.tensor_scalar(xn[:, u, i, :], rows[i], mean[:, u, i:i + 1], rstd[:, u, i:i + 1],
                                                ALU.subtract, ALU.mult).then_inc(xn_done, 1)

        @block.gpsimd
        def _(pool):
            pool.wait_ge(var_done, COMBINE)
            nc.gpsimd.tensor_tensor(k.rstd[:], k.var_eps[:], k.minus_half[:], ALU.pow).then_inc(pow_done, 1)

        @block.tensor
        def _(pe):
            pe.sem_inc(turned, 2)
            with pe.Fori(0, B // 2) as pair:
                for u in range(2):
                    b = 2 * pair + u
                    pe.wait_ge(xnT_done, b + 1)
                    pe.wait_ge(xn_done, (b + 1) * C)
                    for i in range(C):
                        last = nc.tensor.transpose(k.bank2(2 * u)[:, i * P:(i + 1) * P], xn[:, u, i, :], k.ident[:])
                    last.then_inc(turned, 1)

        @block.scalar
        def _(act):
            act.sem_inc(xnT_done, 2)
            with act.Fori(0, B // 2) as pair:
                for u in range(2):
                    b = 2 * pair + u
                    act.wait_ge(stored[u], 16 * (pair + 1))
                    act.wait_ge(turned, b + 3)
                    nc.scalar.copy(xnT[:, u, :], k.bank2(2 * u)).then_inc(xnT_done, 1)

        @block.sync
        def _(sp):
            for u in range(2):
                sp.sem_inc(stored[u], 16)
            with sp.Fori(0, B // 2) as pair:
                for u in range(2):
                    b = 2 * pair + u
                    sp.wait_ge(xnT_done, b + 3)
                    sp.dma_start(scr.xnT[bass.ds(b, 1)].rearrange("o p t -> (o p) t"), xnT[:, u, :]).then_inc(stored[u], 16)
            for u in range(2):
                sp.wait_ge(stored[u], 16 * (B // 2 + 1))


def gat_factors(k, scr):
    nc, t = k.nc, k.t
    a = Arena(k)
    xnT = a.take([2, N])
    wide = a.take([D + 2 * H])
    prod = a.take([2, D])
    a12 = a.take([2, D])
    e = a.take([2, C, 3 * H])
    top = a.take([2, 2 * H])
    tops = a.take([2, 2 * H])
    u8 = a.take([2, C, 2 * H])
    spread = a.take([2, H])
    r1 = a.take([2, C, H])
    f = a.take([2, C * H])
    r = a.take([2, H, C])
    rT = a.take([2, P])
    xsum = a.take([2, 1])
    small = a.take([2, C * H + D])
    g = small[:, :, 0:C * H]
    v = a.take([2, N])
    fb = a.take([2, N])

    w_loaded, w_ready = k.sem("g_w_loaded"), k.sem("g_w_ready")
    loaded = [k.sem(f"g_loaded{u}") for u in range(2)]
    stored = [k.sem(f"g_stored{u}") for u in range(2)]
    top_seen = k.sem("g_top_seen")
    wh_done, step, reduced, exp_done, v_done, turned, r_copied, fb_done = [
        k.sem(f"g_{s}") for s in ("wh_done", "step", "reduced", "exp_done", "v_done", "turned", "r_copied", "fb_done")]
    STORES = 4
    E_READY, U_READY, R_READY = 4, 6, 9
    STEPS = 11

    def ps(u):
        return k.ps[:, 4 * u:4 * u + 4, :].rearrange("p a n -> p (a n)").rearrange("p (c n) -> p c n", n=256)

    with nc.Block() as block:
        @block.sync
        def _(sp):
            for u in range(2):
                sp.sem_inc(stored[u], 16 * STORES)
            sp.dma_start(wide[:, 0:D], t["L1_gnn_Wc"]).then_inc(w_loaded, 16)
            for i in range(2):
                sp.dma_start(a12[:, i, :].rearrange("p (h d) -> p h d", h=H),
                             t["L1_gnn_a"][:, HS * (1 - i):HS * (2 - i)].rearrange("(o h) d -> o h d", o=1)
                             .to_broadcast([P, H, HS])).then_inc(w_loaded, 16)
            for u in range(2):
                sp.dma_start(xnT[:, u, :], scr.xnT[u]).then_inc(loaded[u], 16)
            def store(b, u):
                at = bass.ds(b, 1)
                sp.wait_ge(v_done, b + 3)
                sp.dma_start(scr.gv[at, 0].rearrange("o p n -> (o p) n"), v[:, u, :]).then_inc(stored[u], 16)
                sp.wait_ge(fb_done, b + 1)
                sp.dma_start(scr.gv[at, 1].rearrange("o p n -> (o p) n"), fb[:, u, :]).then_inc(stored[u], 16)
                sp.wait_ge(r_copied, b + 3)
                sp.dma_start(scr.gs[at].rearrange("o p n -> (o p) n"), small[:, u, :]).then_inc(stored[u], 16)
                sp.dma_start(scr.grow[at].rearrange("o (q t) -> (o q) t", t=P), rT[0:C * H, u, :]).then_inc(stored[u], 16)

            with sp.Fori(0, B // 2 - 1) as pair:
                for u in range(2):
                    b = 2 * pair + u
                    store(b, u)
                    sp.dma_start(xnT[:, u, :], scr.xnT[bass.ds(b + 2, 1)].rearrange("o p t -> (o p) t")).then_inc(loaded[u], 16)
            for u in range(2):
                store(B - 2 + u, u)
            for u in range(2):
                sp.wait_ge(stored[u], 16 * STORES * (B // 2 + 1))

        @block.tensor
        def _(pe):
            pe.wait_ge(w_ready, 4)
            with pe.Fori(0, B // 2) as pair:
                for u in range(2):
                    b = 2 * pair + u
                    pe.wait_ge(loaded[u], 16 * (pair + 1))
                    pe.wait_ge(v_done, b + 1)
                    pe.wait_ge(r_copied, b + 1)
                    for i in range(C):
                        last = nc.tensor.matmul(ps(u)[:, i, 0:D + 2 * H], xnT[:, u, i * P:(i + 1) * P], wide[:],
                                                start=True, stop=True)
                    last.then_inc(wh_done, 1)
                    pe.wait_ge(exp_done, 3 * b + 3)
                    pe.wait_ge(v_done, b + 3)
                    nc.tensor.transpose(k.ps[0:C * H, 4 * u, 0:P],
                                        r[:, u].rearrange("p h c -> p (h c)"), k.ident[:]).then_inc(turned, 1)

        @block.vector
        def _(dve):
            dve.sem_inc(v_done, 2)
            dve.wait_ge(w_loaded, 48)
            for i in range(2):
                nc.vector.tensor_tensor(prod[:, i, :], wide[:, 0:D], a12[:, i, :], ALU.mult).then_inc(w_ready, 1)
            for i in range(2):
                dve.wait_ge(w_ready, i + 1)
                nc.vector.tensor_reduce(wide[:, D + i * H:D + (i + 1) * H], prod[:, i, :].rearrange("p (h d) -> p h d", h=H),
                                        AX.X, ALU.add).then_inc(w_ready, 1)
            with dve.Fori(0, B // 2) as pair:
                for u in range(2):
                    b = 2 * pair + u
                    s = Steps(dve, step, STEPS * b)
                    dve.wait_ge(wh_done, b + 1)
                    dve.wait_ge(stored[u], 16 * STORES * (pair + 1))
                    s.did(nc.vector.tensor_copy(e[:, u, :, 0:H], ps(u)[:, :, D:D + H]))
                    s.did(nc.vector.tensor_copy(e[:, u, :, 2 * H:3 * H], ps(u)[:, :, D + H:D + 2 * H]))
                    s.did(nc.vector.tensor_scalar(e[:, u, :, H:2 * H], ps(u)[:, :, D:D + H], -1.0, None, ALU.mult))
                    s.wait()
                    s.did(nc.vector.tensor_reduce(top[:, u, :], e[:, u, :, 0:2 * H].rearrange("p c q -> p q c"),
                                                  AX.X, ALU.max))
                    assert s.n == E_READY
                    dve.wait_ge(reduced, b + 1)
                    s.did(nc.vector.tensor_tensor(u8[:, u], e[:, u, :, 0:2 * H],
                                                  tops[:, u, :].unsqueeze(1).to_broadcast([P, C, 2 * H]), ALU.subtract))
                    s.did(nc.vector.tensor_tensor(spread[:, u, :], tops[:, u, 0:H], tops[:, u, H:2 * H], ALU.add))
                    assert s.n == U_READY
                    s.did(nc.vector.tensor_tensor(r1[:, u], e[:, u, :, 2 * H:3 * H],
                                                  tops[:, u, 0:H].unsqueeze(1).to_broadcast([P, C, H]), ALU.add))
                    s.wait()
                    s.did(nc.vector.scalar_tensor_tensor(out=r1[:, u], in0=r1[:, u], scalar=0.0,
                                                         in1=spread[:, u, :].unsqueeze(1).to_broadcast([P, C, H]),
                                                         op0=ALU.max, op1=ALU.subtract))
                    s.wait()
                    s.did(nc.vector.tensor_scalar(r1[:, u], r1[:, u], 0.0, None, ALU.min))
                    assert s.n == R_READY
                    s.did(nc.vector.tensor_reduce(xsum[:, u, :], xnT[:, u, :], AX.X, ALU.add))
                    s.wait()
                    s.did(nc.vector.tensor_scalar(small[:, u, C * H:C * H + D], wide[:, 0:D], xsum[:, u, 0:1], None, ALU.mult))
                    assert s.n == STEPS
                    dve.wait_ge(exp_done, 3 * b + 1)
                    nc.vector.tensor_tensor(v[:, u, :].rearrange("p (c h d) -> p c h d", c=C, h=H),
                                            ps(u)[:, :, 0:D].rearrange("p c (h d) -> p c h d", h=H),
                                            f[:, u, :].rearrange("p (c h) -> p c h", h=H).unsqueeze(3).to_broadcast([P, C, H, HS]),
                                            ALU.mult).then_inc(v_done, 1)

        @block.gpsimd
        def _(pool):
            with pool.Fori(0, B // 2) as pair:
                for u in range(2):
                    b = 2 * pair + u
                    pool.wait_ge(step, STEPS * b + E_READY)
                    pool.sem_inc(top_seen, 1)
                    nc.gpsimd.partition_all_reduce(tops[:, u, :], top[:, u, :], P, bass.bass_isa.ReduceOp.max).then_inc(reduced, 1)

        @block.scalar
        def _(act):
            act.sem_inc(r_copied, 2)
            with act.Fori(0, B // 2) as pair:
                for u in range(2):
                    b = 2 * pair + u
                    act.wait_ge(step, STEPS * b + U_READY)
                    nc.scalar.activation(f[:, u, :].rearrange("p (c h) -> p c h", h=H), u8[:, u, :, 0:H],
                                         ACT.Exp).then_inc(exp_done, 1)
                    nc.scalar.activation(g[:, u, :].rearrange("p (c h) -> p c h", h=H), u8[:, u, :, H:2 * H],
                                         ACT.Exp, scale=1.0 - SLOPE).then_inc(exp_done, 1)
                    act.wait_ge(step, STEPS * b + R_READY)
                    nc.scalar.activation(r[:, u].rearrange("p h c -> p c h"), r1[:, u], ACT.Exp,
                                         scale=1.0 - SLOPE).then_inc(exp_done, 1)
                    act.wait_ge(exp_done, 3 * b + 1)
                    nc.scalar.copy(fb[:, u, :].rearrange("p (q d) -> p q d", d=HS),
                                   f[:, u, :].unsqueeze(2).to_broadcast([P, C * H, HS])).then_inc(fb_done, 1)
                    act.wait_ge(turned, b + 1)
                    nc.scalar.copy(rT[0:C * H, u, :], k.ps[0:C * H, 4 * u, 0:P]).then_inc(r_copied, 1)


def attention1(k, scr):
    nc = k.nc
    a = Arena(k)
    edge = k.bound[:, 0:C // 2, :].bitcast(BF16).rearrange("p a n -> p (a n)").rearrange("p (c n) -> p c n", c=C)
    rows = a.take([2, H, N])
    v = a.take([2, N])
    fb = a.take([2, N])
    small = a.take([2, C * H + D])
    pm = a.take([8, N])
    ctx = a.take([N])
    den = a.take([N])
    r_rows = a.take([N])
    low = a.take([N])
    r_in = a.take([HS])
    r_out = a.take([HS])
    tens = a.take([P], BF16)

    edge_loaded, tens_ready = k.sem("h_edge_loaded"), k.sem("h_tens_ready")
    loaded = [k.sem(f"h_loaded{u}") for u in range(2)]
    (w_done, pv_done, copied, recip_done, quot_done, low_done, exp_done, elu_done, turned, added,
     den_stored, den_loaded, rec_stored, rec_loaded) = [
        k.sem(f"h_{s}") for s in ("w_done", "pv_done", "copied", "recip_done", "quot_done", "low_done", "exp_done",
                                  "elu_done", "turned", "added", "den_stored", "den_loaded", "rec_stored", "rec_loaded")]
    LOADS = 4
    U_LAST = (B - 1) % 2
    RECIP_AT, QUOT_AT, ELU_AT, ADD_AT = 1, 3, 4, 5

    with nc.Block() as block:
        @block.sync
        def _(sp):
            sp.sem_inc(den_stored, 16)
            sp.dma_start(edge, scr.edge).then_inc(edge_loaded, 16)

            def load(b, u):
                at = bass.ds(b, 1)
                sp.dma_start(rows[:, u, :, :].rearrange("p h n -> p (h n)"),
                             scr.grow[at].to_broadcast([P, H * N])).then_inc(loaded[u], 16)
                sp.dma_start(v[:, u, :], scr.gv[at, 0].rearrange("o p n -> (o p) n")).then_inc(loaded[u], 16)
                sp.dma_start(fb[:, u, :], scr.gv[at, 1].rearrange("o p n -> (o p) n")).then_inc(loaded[u], 16)
                sp.dma_start(small[:, u, :], scr.gs[at].rearrange("o p n -> (o p) n")).then_inc(loaded[u], 16)

            def reciprocals(b, u):
                sp.wait_ge(copied, 2 * b + 1)
                sp.dma_start(scr.gden[u], den[0:P:HS, :]).then_inc(den_stored, 16)
                sp.wait_ge(den_stored, 16 * b + 32)
                sp.dma_start(r_in[:], scr.gden[u].rearrange("h (a t) -> (h a) t", t=HS)).then_inc(den_loaded, 16)
                sp.wait_ge(recip_done, b + 1)
                sp.dma_start(scr.grec[u].rearrange("h (a t) -> (h a) t", t=HS), r_out[:]).then_inc(rec_stored, 16)
                sp.wait_ge(rec_stored, 16 * b + 16)
                for h in range(H):
                    sp.dma_start(r_rows[h * HS:(h + 1) * HS, :],
                                 scr.grec[u, h:h + 1, :].to_broadcast([HS, N])).then_inc(rec_loaded, 16)

            def body(b, u, _):
                if is_first(b):
                    load(0, 0)
                    load(1, 1)
                    return
                if not isinstance(b, int):
                    sp.wait_ge(pv_done, C * b + 2)
                    load(b + 1, 1 - u)
                reciprocals(b - 1, 1 - u)

            Peeled.run(sp, body, lambda: reciprocals(B - 1, U_LAST))

        @block.gpsimd
        def _(pool):
            nc.gpsimd.memset(tens, float(C)).then_inc(tens_ready, 1)

        @block.tensor
        def _(pe):
            pe.sem_inc(pv_done, 2)
            pe.sem_inc(turned, 1)
            pe.wait_ge(tens_ready, 1)

            def values(b, u, half_b, c):
                if c == 0:
                    pe.wait_ge(loaded[u], 16 * LOADS * (half_b + 1))
                    pe.wait_ge(added, b + 1)
                    for half in range(2):
                        nc.tensor.matmul(k.ps[:, 4 * u + half, :], small[:, u, C * H:C * H + D], halves(k.lone[:])[half],
                                         start=True, stop=False, skip_group_check=True)
                        nc.tensor.matmul(k.ps[:, 4 * u + 2 + half, :], tens, halves(k.lone16[:])[half],
                                         start=True, stop=False, skip_group_check=True)
                pe.wait_ge(w_done, 4 * (C * b + c) + 4)
                for half in range(2):
                    for bank, w in ((0, v), (2, fb)):
                        for h in range(H):
                            last = nc.tensor.matmul(
                                k.ps[h * HS:(h + 1) * HS, 4 * u + bank + half, :],
                                w[:, u, c * P + h * HS:c * P + (h + 1) * HS], halves(pm[:, 4 * (c % 2) + h, :])[half],
                                start=False, stop=(c == C - 1), skip_group_check=True)
                last.then_inc(pv_done, 1)

            def turn(b, u):
                pe.wait_ge(elu_done, b + 1)
                for i in range(C):
                    last = nc.tensor.transpose(k.bank2(4 * u)[:, i * P:(i + 1) * P], ctx[:, i * P:(i + 1) * P], k.ident[:])
                last.then_inc(turned, 1)

            def body(b, u, half_b):
                for c in range(C):
                    values(b, u, half_b, c)
                    if c == ELU_AT and not is_first(b):
                        turn(b - 1, 1 - u)

            Peeled.run(pe, body, lambda: turn(B - 1, U_LAST))

        @block.vector
        def _(dve):
            dve.sem_inc(added, 2)
            dve.wait_ge(edge_loaded, 16)

            def weights(b, u, half_b, c):
                if c == 0:
                    dve.wait_ge(loaded[u], 16 * LOADS * (half_b + 1))
                dve.wait_ge(pv_done, C * b + c + 1)
                for h in range(H):
                    nc.vector.scalar_tensor_tensor(out=pm[:, 4 * (c % 2) + h, :], in0=rows[:, u, h, :],
                                                   scalar=small[:, u, c * H + h:c * H + h + 1], in1=edge[:, c, :],
                                                   op0=ALU.max, op1=ALU.mult).then_inc(w_done, 1)

            def reciprocal(b):
                dve.wait_ge(den_loaded, 16 * b + 16)
                nc.vector.reciprocal(r_out[:], r_in[:]).then_inc(recip_done, 1)

            def quotient(b):
                dve.wait_ge(copied, 2 * b + 2)
                dve.wait_ge(rec_loaded, 64 * b + 64)
                nc.vector.tensor_tensor(ctx[:], ctx[:], r_rows[:], ALU.mult).then_inc(quot_done, 1)
                dve.wait_ge(quot_done, b + 1)
                nc.vector.tensor_scalar(low[:], ctx[:], 0.0, None, ALU.min).then_inc(low_done, 1)

            def elu(b):
                dve.wait_ge(exp_done, b + 1)
                nc.vector.scalar_tensor_tensor(out=ctx[:], in0=low[:], scalar=-1.0, in1=ctx[:],
                                               op0=ALU.add, op1=ALU.max).then_inc(elu_done, 1)

            def add(b, u):
                dve.wait_ge(turned, b + 2)
                x = k.x[:, bass.ds(b * C, C), :].rearrange("p c f -> p (c f)")
                nc.vector.tensor_tensor(x, k.bank2(4 * u), x, ALU.add).then_inc(added, 1)

            def body(b, u, half_b):
                for c in range(C):
                    weights(b, u, half_b, c)
                    if not is_first(b):
                        if c == RECIP_AT:
                            reciprocal(b - 1)
                        if c == QUOT_AT:
                            quotient(b - 1)
                        if c == ELU_AT:
                            elu(b - 1)
                        if c == ADD_AT:
                            add(b - 1, 1 - u)

            def last():
                reciprocal(B - 1)
                quotient(B - 1)
                elu(B - 1)
                add(B - 1, U_LAST)

            Peeled.run(dve, body, last)

        @block.scalar
        def _(act):
            def finish(b, u):
                act.wait_ge(pv_done, C * b + C + 2)
                act.wait_ge(den_stored, 16 * b + 16)
                nc.scalar.copy(den[:], k.bank2(4 * u + 2)).then_inc(copied, 1)
                act.wait_ge(turned, b + 1)
                nc.scalar.copy(ctx[:], k.bank2(4 * u)).then_inc(copied, 1)
                act.wait_ge(low_done, b + 1)
                nc.scalar.activation(low[:], low[:], ACT.Exp).then_inc(exp_done, 1)

            with act.Fori(0, B // 2) as pair:
                for u in range(2):
                    finish(2 * pair + u, u)


def gate0(k, scr):
    nc, t = k.nc, k.t
    a = Arena(k)
    T = B * C
    xnT = a.take([2, N])
    wg = a.take([E])
    bg = a.take([E])
    bias = a.take([E])
    key = a.take([E])
    l = a.take([T, E])
    hot = a.take([2, T, E])
    at = a.take([T, E])
    top = a.take([2, T])
    pick = a.take([T])
    w = a.take([2, T])
    comb = a.take([T, E])
    combT = a.take([T * E])

    w_loaded, logits_done, key_ready, step, exp_done, turned, copied, stored = [
        k.sem(f"t_{s}") for s in ("w_loaded", "logits_done", "key_ready", "step", "exp_done", "turned", "copied", "stored")]
    loaded = [k.sem(f"t_loaded{u}") for u in range(2)]
    lane = lambda ap: ap.unsqueeze(1).to_broadcast([P, T, E])
    per = lambda ap: ap.unsqueeze(2).to_broadcast([P, T, E])
    DIFF_READY, COMB_READY = 14, 20

    with nc.Block() as block:
        @block.sync
        def _(sp):
            sp.dma_start(wg, t["L0_ffn_Wg"]).then_inc(w_loaded, 16)
            for dst, n in ((bg, "L0_ffn_bg"), (bias, "L0_ffn_bias")):
                sp.dma_start(dst, t[n].rearrange("(o e) -> o e", o=1).to_broadcast([P, E])).then_inc(w_loaded, 16)
            for b in range(B):
                if b >= 2:
                    sp.wait_ge(logits_done, b - 1)
                sp.dma_start(xnT[:, b % 2, :], scr.xnT[b]).then_inc(loaded[b % 2], 16)
            sp.wait_ge(copied, 1)
            sp.dma_start(scr.combT.rearrange("(q i) e t -> (i e) q t", i=P // E),
                         combT.rearrange("p (q t) -> p q t", t=P)).then_inc(stored, 16)
            sp.wait_ge(stored, 16)

        @block.tensor
        def _(pe):
            pe.wait_ge(w_loaded, 48)
            for b in range(B):
                pe.wait_ge(loaded[b % 2], 16 * (b // 2 + 1))
                for i in range(C):
                    last = nc.tensor.matmul(k.ps[:, 7, (b * C + i) * E:(b * C + i + 1) * E],
                                            xnT[:, b % 2, i * P:(i + 1) * P], wg, start=True, stop=True)
                last.then_inc(logits_done, 1)
            pe.wait_ge(step, COMB_READY)
            flat = comb.rearrange("p n e -> p (n e)")
            for q in range(T * E // P):
                last = nc.tensor.transpose(k.ps[:, 6, q * P:(q + 1) * P], flat[:, q * P:(q + 1) * P], k.ident[:])
            last.then_inc(turned, 1)

        @block.gpsimd
        def _(pool):
            for e in range(E):
                last = nc.gpsimd.memset(key[:, e:e + 1], float(E - e))
            last.then_inc(key_ready, 1)

        @block.scalar
        def _(act):
            act.wait_ge(step, DIFF_READY)
            nc.scalar.activation(w[:, 1, :], pick, ACT.Exp).then_inc(exp_done, 1)
            act.wait_ge(turned, 1)
            nc.scalar.copy(combT, k.ps[:, 6, :]).then_inc(copied, 1)

        @block.vector
        def _(dve):
            s = Steps(dve, step)
            tt, stt, ts = nc.vector.tensor_tensor, nc.vector.scalar_tensor_tensor, nc.vector.tensor_scalar
            dve.wait_ge(w_loaded, 48)
            dve.wait_ge(key_ready, 1)
            dve.wait_ge(logits_done, B)
            s.did(tt(l, k.ps[:, 7, :].rearrange("p (n e) -> p n e", e=E), lane(bg), ALU.add))
            s.wait()
            s.did(tt(l, l, lane(bias), ALU.add))
            for j in range(2):
                s.wait()
                s.did(nc.vector.tensor_reduce(top[:, j, :], l, AX.X, ALU.max))
                s.wait()
                s.did(tt(at, l, per(top[:, j, :]), ALU.is_equal))
                s.wait()
                s.did(tt(at, at, lane(key), ALU.mult))
                s.wait()
                s.did(nc.vector.tensor_reduce(pick, at, AX.X, ALU.max))
                s.wait()
                s.did(tt(hot[:, j], at, per(pick), ALU.is_equal))
                if j == 0:
                    s.wait()
                    s.did(stt(out=l, in0=hot[:, 0], scalar=-3e38, in1=l, op0=ALU.mult, op1=ALU.add))
            s.wait()
            s.did(tt(pick, top[:, 1, :], top[:, 0, :], ALU.subtract))
            assert s.n == DIFF_READY
            dve.wait_ge(exp_done, 1)
            s.did(ts(w[:, 0, :], w[:, 1, :], 1.0, None, ALU.add))
            s.wait()
            s.did(nc.vector.reciprocal(w[:, 0, :], w[:, 0, :]))
            s.wait()
            s.did(tt(w[:, 1, :], w[:, 1, :], w[:, 0, :], ALU.mult))
            s.did(tt(comb, hot[:, 0], per(w[:, 0, :]), ALU.mult))
            s.wait()
            s.did(tt(at, hot[:, 1], per(w[:, 1, :]), ALU.mult))
            s.wait()
            s.did(tt(comb, comb, at, ALU.add))
            assert s.n == COMB_READY


def ffn0(k, scr):
    nc, t = k.nc, k.t
    a = Arena(k)
    HID = 256
    K = E * HID // P
    PER = HID // P
    w1 = a.take([E, HID])
    w2 = a.take([K, D])
    b1 = a.take([K])
    b2 = a.take([D])
    xnT = a.take([2, N])
    wt = a.take([2, C, E, P])
    wt8 = a.take([2, C, P])
    h = a.take([2, N])
    hw = a.take([2, N])
    outT = a.take([N])

    w_loaded, zeroed, h_made, h_done, hw_done, used, outT_done, turned, added = [
        k.sem(f"e_{s}") for s in ("w_loaded", "zeroed", "h_made", "h_done", "hw_done", "used", "outT_done", "turned", "added")]
    loaded = [k.sem(f"e_loaded{u}") for u in range(2)]
    LOADS = 3

    with nc.Block() as block:
        @block.sync
        def _(sp):
            sp.dma_start(w1, t["L0_ffn_W1"].rearrange("e d h -> d e h")).then_inc(w_loaded, 16)
            sp.dma_start(b1, t["L0_ffn_b1T"]).then_inc(w_loaded, 16)
            sp.wait_ge(zeroed, 1)

            def load(b, u):
                at = bass.ds(b, 1)
                sp.dma_start(xnT[:, u, :], scr.xnT[at].rearrange("o p t -> (o p) t")).then_inc(loaded[u], 16)
                sp.dma_start(wt[:, u, :, :, :], scr.combT[bass.ds(b * C, C)].rearrange("(o c) e t -> o c e t", o=1)
                             .to_broadcast([P, C, E, P])).then_inc(loaded[u], 16)
                sp.dma_start(wt8[0:E, u, :, :], scr.combT[bass.ds(b * C, C)].rearrange("c e t -> e c t")).then_inc(loaded[u], 16)

            load(0, 0)
            sp.dma_start(w2, t["L0_ffn_W2"].rearrange("e (j p) d -> p (e j) d", p=P)).then_inc(w_loaded, 16)
            sp.dma_start(b2[0:E, :], t["L0_ffn_b2"]).then_inc(w_loaded, 16)
            load(1, 1)
            with sp.Fori(0, B // 2 - 1) as pair:
                for u in range(2):
                    b = 2 * pair + u
                    sp.wait_ge(outT_done, b + 2)
                    load(b + 2, u)

        @block.gpsimd
        def _(pool):
            nc.gpsimd.memset(b2, 0.0)
            nc.gpsimd.memset(wt8, 0.0).then_inc(zeroed, 1)

        @block.tensor
        def _(pe):
            pe.sem_inc(used, 2)
            pe.wait_ge(w_loaded, 16 * 4)

            def hidden(b, u, j):
                pe.wait_ge(h_done, K * b + j + 1)
                for half in range(2):
                    last = nc.tensor.matmul(k.ps[:, 2 * (j % 2) + half, :], w1[:, j // PER, (j % PER) * P:(j % PER + 1) * P],
                                            halves(xnT[:, u, :])[half], start=True, stop=True)
                last.then_inc(h_made, 1)

            def second(b, u, j):
                pe.wait_ge(hw_done, K * b + j + 3)
                if j == 0:
                    pe.wait_ge(outT_done, b + 1)
                for half in range(2):
                    last = nc.tensor.matmul(k.ps[:, 4 + half, :], w2[:, j, :], halves(hw[:, j % 2, :])[half],
                                            start=(j == 0), stop=False, skip_group_check=True)
                last.then_inc(used, 1)

            with pe.Fori(0, B // 2) as pair:
                for u in range(2):
                    b = 2 * pair + u
                    pe.wait_ge(loaded[u], 16 * LOADS * (pair + 1))
                    hidden(b, u, 0)
                    hidden(b, u, 1)
                    for j in range(2, K):
                        second(b, u, j - 2)
                        hidden(b, u, j)
                    second(b, u, K - 2)
                    second(b, u, K - 1)
                    for half in range(2):
                        last = nc.tensor.matmul(k.ps[:, 4 + half, :], b2, halves(wt8[:, u].rearrange("p c t -> p (c t)"))[half],
                                                start=False, stop=True, skip_group_check=True)
                    last.then_inc(turned, 1)
                    pe.wait_ge(outT_done, b + 2)
                    pe.wait_ge(added, b + 1)
                    for i in range(C):
                        last = nc.tensor.transpose(k.bank2(6)[:, i * P:(i + 1) * P], outT[:, i * P:(i + 1) * P], k.ident[:])
                    last.then_inc(turned, 1)

        @block.scalar
        def _(act):
            act.sem_inc(h_done, 2)
            act.sem_inc(outT_done, 1)
            act.wait_ge(w_loaded, 16 * 4)
            with act.Fori(0, B // 2) as pair:
                for u in range(2):
                    b = 2 * pair + u
                    for j in range(K):
                        act.wait_ge(h_made, K * b + j + 1)
                        act.wait_ge(hw_done, K * b + j + 1)
                        nc.scalar.activation(h[:, j % 2, :], k.bank2(2 * (j % 2)), ACT.Relu, bias=b1[:, j:j + 1]).then_inc(h_done, 1)
                    act.wait_ge(turned, 2 * b + 1)
                    nc.scalar.copy(outT, k.bank2(4)).then_inc(outT_done, 1)

        @block.vector
        def _(dve):
            dve.sem_inc(hw_done, 2)
            dve.sem_inc(added, 1)
            with dve.Fori(0, B // 2) as pair:
                for u in range(2):
                    b = 2 * pair + u
                    dve.wait_ge(loaded[u], 16 * LOADS * (pair + 1))
                    for j in range(K):
                        dve.wait_ge(h_done, K * b + j + 3)
                        dve.wait_ge(used, K * b + j + 1)
                        nc.vector.tensor_tensor(hw[:, j % 2, :].rearrange("p (c t) -> p c t", t=P),
                                                h[:, j % 2, :].rearrange("p (c t) -> p c t", t=P),
                                                wt[:, u, :, j // PER, :], ALU.mult).then_inc(hw_done, 1)
                    dve.wait_ge(turned, 2 * b + 2)
                    x = k.x[:, bass.ds(b * C, C), :].rearrange("p c f -> p (c f)")
                    nc.vector.tensor_tensor(x, k.bank2(6), x, ALU.add).then_inc(added, 1)


def ffn1(k, scr, out):
    nc, t = k.nc, k.t
    a = Arena(k)
    HID = 512
    K = HID // P
    w1 = a.take([HID])
    b1 = a.take([K])
    wg = a.take([K, E])
    wd = a.take([K, E * D])
    bg = a.take([E])
    bd = a.take([E * D])
    key = a.take([E])
    xnT = a.take([2, N])
    h = a.take([2, K, N])
    l = a.take([2, C, E])
    at = a.take([C, E])
    top = a.take([C])
    pick = a.take([C])
    total = a.take([C])
    w = a.take([C, E])
    y = a.take([2, E * D])
    pickd = a.take([2, D])

    w_loaded, key_ready, h_made, h_done, logits_done, y_made, step, exp_done, y_free, ystep, hot_free = [
        k.sem(f"f_{s}") for s in ("w_loaded", "key_ready", "h_made", "h_done", "logits_done", "y_made", "step",
                                  "exp_done", "y_free", "ystep", "hot_free")]
    loaded = [k.sem(f"f_loaded{u}") for u in range(2)]
    stored = k.sem("f_stored")
    lane = lambda ap: ap.unsqueeze(1).to_broadcast([P, C, E])
    per = lambda ap: ap.unsqueeze(2).to_broadcast([P, C, E])
    DIFF_READY, STEPS = 3, 10
    YSTEPS = 4 * C
    out_rows = tile_rows(out.rearrange("b n f -> (b n) f"))

    with nc.Block() as block:
        @block.sync
        def _(sp):
            def load(b, u):
                sp.dma_start(xnT[:, u, :], scr.xnT[bass.ds(b, 1)].rearrange("o p t -> (o p) t")).then_inc(loaded[u], 16)

            sp.dma_start(w1, t["L1_ffn_W1"]).then_inc(w_loaded, 16)
            sp.dma_start(b1, t["L1_ffn_b1T"]).then_inc(w_loaded, 16)
            load(0, 0)
            load(1, 1)
            sp.dma_start(wg, t["L1_ffn_Wg"].rearrange("(j p) e -> p j e", p=P)).then_inc(w_loaded, 16)
            for e in range(E):
                sp.dma_start(wd[:, :, e * D:(e + 1) * D], t["L1_ffn_Wd"][e].rearrange("(j p) d -> p j d", p=P)).then_inc(w_loaded, 16)
            sp.dma_start(bg, t["L1_ffn_bg"].rearrange("(o e) -> o e", o=1).to_broadcast([P, E])).then_inc(w_loaded, 16)
            sp.dma_start(bd, t["L1_ffn_bd"].rearrange("(o e) d -> o (e d)", o=1).to_broadcast([P, E * D])).then_inc(w_loaded, 16)
            with sp.Fori(0, B // 2 - 1) as pair:
                for u in range(2):
                    b = 2 * pair + u
                    sp.wait_ge(h_made, K * b + K)
                    load(b + 2, u)
                    sp.wait_ge(ystep, YSTEPS * b + YSTEPS)
                    sp.dma_start(out_rows[:, bass.ds(b * C, C), :], k.x[:, bass.ds(b * C, C), :]).then_inc(stored, 16)
            for b in range(B - 2, B):
                sp.wait_ge(ystep, YSTEPS * b + YSTEPS)
                sp.dma_start(out_rows[:, b * C:(b + 1) * C, :], k.x[:, b * C:(b + 1) * C, :]).then_inc(stored, 16)
            sp.wait_ge(stored, 16 * B)

        @block.tensor
        def _(pe):
            pe.wait_ge(w_loaded, 16 * (5 + E))
            with pe.Fori(0, B // 2) as pair:
                for u in range(2):
                    b = 2 * pair + u
                    pe.wait_ge(loaded[u], 16 * (pair + 1))
                    for j in range(K):
                        pe.wait_ge(h_done, K * b + j + 1)
                        for half in range(2):
                            last = nc.tensor.matmul(k.ps[:, half, :], w1[:, j * P:(j + 1) * P],
                                                    halves(xnT[:, u, :])[half], start=True, stop=True)
                        last.then_inc(h_made, 1)
                    pe.wait_ge(h_done, K * b + K + 1)
                    pe.wait_ge(step, STEPS * b + 1)
                    for i in range(C):
                        for j in range(K):
                            last = nc.tensor.matmul(k.ps[:, 6, i * E:(i + 1) * E], h[:, u, j, i * P:(i + 1) * P],
                                                    wg[:, j, :], start=(j == 0), stop=(j == K - 1))
                    last.then_inc(logits_done, 1)
                    for i in range(C):
                        pe.wait_ge(y_free, C * b + i + 1)
                        for half in range(2):
                            for j in range(K):
                                last = nc.tensor.matmul(k.ps[:, 2 + 2 * (i % 2) + half, :], h[:, u, j, i * P:(i + 1) * P],
                                                        halves(wd[:, j, :])[half], start=(j == 0), stop=(j == K - 1))
                        last.then_inc(y_made, 1)

        @block.gpsimd
        def _(pool):
            for e in range(E):
                last = nc.gpsimd.memset(key[:, e:e + 1], float(E - e))
            last.then_inc(key_ready, 1)

        @block.scalar
        def _(act):
            act.sem_inc(h_done, 1)
            act.wait_ge(w_loaded, 16 * (5 + E))
            with act.Fori(0, B // 2) as pair:
                for u in range(2):
                    b = 2 * pair + u
                    for j in range(K):
                        act.wait_ge(h_made, K * b + j + 1)
                        nc.scalar.activation(h[:, u, j, :], k.bank2(0), ACT.Gelu, bias=b1[:, j:j + 1]).then_inc(h_done, 1)
                    act.wait_ge(step, STEPS * b + DIFF_READY + 1)
                    nc.scalar.activation(l[:, 1], l[:, 0], ACT.Exp).then_inc(exp_done, 1)

        @block.vector
        def _(dve):
            tt, ts, red = nc.vector.tensor_tensor, nc.vector.tensor_scalar, nc.vector.tensor_reduce
            dve.sem_inc(step, 1)
            dve.sem_inc(y_free, 2)
            dve.wait_ge(w_loaded, 16 * (5 + E))
            dve.wait_ge(key_ready, 1)
            with dve.Fori(0, B // 2) as pair:
                for u in range(2):
                    b = 2 * pair + u
                    s = Steps(dve, step, STEPS * b + 1)
                    dve.wait_ge(logits_done, b + 1)
                    s.did(tt(l[:, 0], k.ps[:, 6, 0:C * E].rearrange("p (c e) -> p c e", e=E), lane(bg), ALU.add))
                    s.wait()
                    s.did(red(top, l[:, 0], AX.X, ALU.max))
                    s.wait()
                    s.did(tt(l[:, 0], l[:, 0], per(top), ALU.subtract))
                    assert s.n == DIFF_READY
                    s.wait()
                    s.did(ts(at, l[:, 0], 0.0, None, ALU.is_ge))
                    s.wait()
                    s.did(tt(at, at, lane(key), ALU.mult))
                    s.wait()
                    s.did(red(pick, at, AX.X, ALU.max))
                    s.wait()
                    s.did(tt(w, at, per(pick), ALU.is_equal))
                    dve.wait_ge(exp_done, b + 1)
                    s.did(red(total, l[:, 1], AX.X, ALU.add))
                    s.wait()
                    s.did(nc.vector.reciprocal(total, total))
                    s.wait()
                    s.did(tt(w, w, per(total), ALU.mult))
                    assert s.n == STEPS
                    s.wait()
                    rows = rows_of(k, b)
                    for i in range(C):
                        at_y = Steps(dve, ystep, YSTEPS * b + 4 * i)
                        dve.wait_ge(y_made, C * b + i + 1)
                        at_y.did(tt(y[:, i % 2, :], k.bank2(2 + 2 * (i % 2)), bd, ALU.add))
                        at_y.wait()
                        y3 = y[:, i % 2, :].rearrange("p (e d) -> p e d", e=E)
                        at_y.did(tt(y3, y3, w[:, i, :].unsqueeze(2).to_broadcast([P, E, D]), ALU.mult))
                        dve.sem_inc(y_free, 1)
                        at_y.wait()
                        at_y.did(red(pickd[:, i % 2, :], y3.rearrange("p e d -> p d e"), AX.X, ALU.add))
                        at_y.wait()
                        at_y.did(tt(rows[i], rows[i], pickd[:, i % 2, :], ALU.add))


def build(nc, t, out):
    with ExitStack() as ctx:
        k = Core(nc, ctx, t)
        scr = Scratch(k)
        setup(k, scr)
        qkv(k, scr)
        attention0(k, scr)
        layer_norm(k, scr, "n2")
        gate0(k, scr)
        ffn0(k, scr)
        layer_norm(k, scr, "n3")
        gat_factors(k, scr)
        attention1(k, scr)
        layer_norm(k, scr, "n4")
        ffn1(k, scr, out)


def layouts(inputs):
    a = {n: np.ascontiguousarray(np.asarray(v)) for n, v in inputs.items()}
    for n in ("L0_gnn_Wq", "L0_gnn_Wk", "L0_gnn_Wv", "L0_gnn_Wo"):
        a[n + "T"] = np.ascontiguousarray(a.pop(n).T)
    a["L1_gnn_Wc"] = np.ascontiguousarray(a.pop("L1_gnn_W").transpose(1, 0, 2).reshape(D, D))
    a["L0_ffn_b1T"] = np.ascontiguousarray(a.pop("L0_ffn_b1").reshape(-1, P).T)
    a["L1_ffn_b1T"] = np.ascontiguousarray(a.pop("L1_ffn_b1").reshape(-1, P).T)
    a["ident"] = np.eye(P, dtype=np.float32)
    return a


def kernel(**inputs):
    import concourse.bacc as bacc
    from concourse.bass_utils import run_bass_kernel_spmd

    nc = bacc.Bacc("TRN2", target_bir_lowering=False, num_devices=1)
    arrays = layouts(inputs)
    t = {n: nc.dram_tensor(n, a.shape, mybir.dt.from_np(a.dtype), kind="ExternalInput").ap() for n, a in arrays.items()}
    out = nc.dram_tensor("out", (B, N, D), F32, kind="ExternalOutput").ap()
    build(nc, t, out)
    r = run_bass_kernel_spmd(nc, [arrays], core_ids=[0])
    return r.results[0]["out"]
```

```python
from contextlib import ExitStack

import concourse.bass as bass
from concourse import mybir
import numpy as np

ALU = mybir.AluOpType
ACT = mybir.ActivationFunctionType
AX = mybir.AxisListType
F32 = mybir.dt.float32
F16 = mybir.dt.float16
BF16 = mybir.dt.bfloat16
I32 = mybir.dt.int32

P = 128
B, N, D = 8, 1024, 128
H, HS = 4, 32
E = 8
C = N // P
EPS = 1e-5
CLIP = 10.0
E_HI = float(np.float32(np.exp(CLIP)))
E_LO = float(np.float32(np.exp(-CLIP)))
SCALE = float(HS) ** -0.5
SLOPE = 0.2


class Steps:

    def __init__(self, eng, sem, base=0):
        self.eng, self.sem, self.base, self.n = eng, sem, base, 0

    def did(self, ins):
        self.n += 1
        ins.then_inc(self.sem, 1)
        return ins

    def wait(self):
        self.eng.wait_ge(self.sem, self.base + self.n)


def halves(ap):
    return [ap[:, 0:512], ap[:, 512:1024]]


COMBINE = 7


def combine_stats(nc, steps, stats, mean, var_eps, tmp):
    ms, ds, vs = tmp[:, 0], tmp[:, 1], tmp[:, 2]
    tt, stt = nc.vector.tensor_tensor, nc.vector.scalar_tensor_tensor
    steps.did(tt(ms, stats[:, :, 1], stats[:, :, 4], ALU.add))
    steps.did(tt(ds, stats[:, :, 1], stats[:, :, 4], ALU.subtract))
    steps.did(tt(vs, stats[:, :, 2], stats[:, :, 5], ALU.add))
    steps.wait()
    steps.did(nc.vector.tensor_scalar(mean, ms, 0.5, None, ALU.mult))
    steps.did(stt(out=ds, in0=ds, scalar=0.25, in1=ds, op0=ALU.mult, op1=ALU.mult))
    steps.did(nc.vector.tensor_scalar(vs, vs, 1.0 / D, EPS, ALU.mult, ALU.add))
    steps.wait()
    steps.did(tt(var_eps, vs, ds, ALU.add))


class Core:

    def __init__(self, nc, ctx, t):
        self.nc, self.ctx, self.t = nc, ctx, t
        sb = self.sb
        self.x = sb("x_res", [P, B * C, D], F32)
        self.bound = sb("bound", [P, C, N], F32)
        self.lone = sb("lone", [P, N], BF16)
        self.ident = sb("ident_sb", [P, P], F32)
        self.ident16 = sb("ident16", [P, P], BF16)
        self.ones = sb("ones", [P, HS], F32)
        self.minus_half = sb("minus_half", [P, B * C], F32)
        self.mv = sb("mv", [P, B * C, 2], F32)
        self.var_eps = sb("var_eps", [P, B * C], F32)
        self.rstd = sb("rstd", [P, B * C], F32)
        self.wo_bias = sb("wo_bias", [P, D], F32)
        self.gamma = sb("gamma_sb", [P, D], F32)
        self.beta = sb("beta_sb", [P, D], F32)
        self.w0 = sb("w0", [P, 4, D], F32)
        self.bqkv = sb("bqkv", [P, 3], F32)
        self.arena = sb("arena", [P, ARENA // 4], F32)
        self.ps = ctx.enter_context(nc.psum_tensor("ps", [P, 8, 512], F32))

    def sb(self, name, shape, dt):
        return self.ctx.enter_context(self.nc.sbuf_tensor(name, shape, dt))

    def sem(self, name):
        return self.ctx.enter_context(self.nc.semaphore(name))

    def dram(self, name, shape, dt):
        return self.nc.dram_tensor(name, shape, dt).ap()

    def bank2(self, k):
        return self.ps[:, k:k + 2, :].rearrange("p a n -> p (a n)")


class Arena:

    def __init__(self, core):
        self.core, self.at = core, 0

    def take(self, shape, dt=F32):
        size = 2 if dt in (F16, BF16) else 4
        words = int(np.prod(shape)) * size // 4
        ap = self.core.arena[:, self.at:self.at + words]
        self.at += words
        assert self.at * 4 <= ARENA, self.at * 4
        if dt != F32:
            ap = ap.bitcast(dt)
        if len(shape) == 1:
            return ap
        names = "abcd"[:len(shape)]
        sizes = {n: s for n, s in zip(names, shape)}
        return ap.rearrange(f"p ({' '.join(names)}) -> p {' '.join(names)}", **sizes)


ARENA = 133 * 1024 + 768


def tile_rows(dram):
    return dram.rearrange("(n p) f -> p n f", p=P)


def setup(k, scr):
    nc, t = k.nc, k.t
    a = Arena(k)
    adj = a.take([C, N], I32)
    code = a.take([C, N], BF16)
    nonzero = a.take([C, N], BF16)
    edge = a.take([C, N], BF16)
    ones16 = a.take([P], BF16)
    bv_cols = a.take([P])
    bo_rows = a.take([D])

    adj_loaded = [k.sem(f"adj_loaded{i}") for i in range(C)]
    x_loaded = k.sem("x_loaded")
    weights_loaded = k.sem("weights_loaded")
    code_ready = k.sem("code_ready")
    turned = k.sem("turned")
    masks_ready = k.sem("masks_ready")
    counted = k.sem("counted")
    consts_ready = k.sem("consts_ready")
    bias_made = k.sem("bias_made")
    edge_stored = k.sem("edge_stored")
    stats_done = k.sem("s_stats_done")
    mv_done = k.sem("s_mv_done")
    stats = a.take([B * C, 6])
    n_weights = 11
    xt = tile_rows(t["x"].rearrange("b n f -> (b n) f"))
    adj_t = tile_rows(t["adj"])

    with nc.Block() as block:
        @block.sync
        def _(sp):
            for i in range(C):
                sp.dma_start(adj[:, i, :], adj_t[:, i, :]).then_inc(adj_loaded[i], 16)
            for b in range(B):
                sp.dma_start(k.x[:, b * C:(b + 1) * C, :], xt[:, b * C:(b + 1) * C, :]).then_inc(x_loaded, 16)
            sp.wait_ge(masks_ready, 2 * C)
            sp.dma_start(scr.edge, edge).then_inc(edge_stored, 16)
            sp.wait_ge(edge_stored, 16)

        @block.scalar
        def _(act):
            loads = [(k.ident[:], t["ident"])]
            loads += [(k.w0[:, i, :], t[w]) for i, w in enumerate(("L0_gnn_WqT", "L0_gnn_WkT", "L0_gnn_WvT", "L0_gnn_WoT"))]
            loads += [(k.bqkv[:, i:i + 1], t[w].rearrange("(p o) -> p o", o=1))
                      for i, w in enumerate(("L0_gnn_bq", "L0_gnn_bk", "L0_gnn_bv"))]
            loads += [(dst, t[w].rearrange("(o f) -> o f", o=1).to_broadcast([P, D]))
                      for dst, w in ((bo_rows, "L0_gnn_bo"), (k.gamma[:], "L0_gnn_gamma"), (k.beta[:], "L0_gnn_beta"))]
            assert len(loads) == n_weights
            for dst, src in loads:
                act.dma_start(dst, src).then_inc(weights_loaded, 16)

        @block.gpsimd
        def _(pool):
            nc.gpsimd.memset(k.ones[:], 1.0)
            nc.gpsimd.memset(ones16, 1.0)
            nc.gpsimd.memset(k.minus_half[:], -0.5).then_inc(consts_ready, 1)
            pool.wait_ge(consts_ready, 1)
            pool.wait_ge(mv_done, B * C + 1)
            nc.gpsimd.tensor_tensor(k.rstd[:], k.var_eps[:], k.minus_half[:], ALU.pow)

        @block.vector
        def _(dve):
            dve.wait_ge(weights_loaded, 16 * n_weights)
            nc.vector.tensor_copy(k.ident16[:], k.ident[:])
            nc.vector.tensor_copy(bv_cols, k.bqkv[:, 2:3].to_broadcast([P, P])).then_inc(code_ready, 1)
            for i in range(C):
                dve.wait_ge(adj_loaded[i], 16)
                nc.vector.tensor_scalar(nonzero[:, i, :], adj[:, i, :], 0.0, None, ALU.not_equal).then_inc(code_ready, 1)
                dve.wait_ge(code_ready, 2 * i + 2)
                nc.vector.scalar_tensor_tensor(out=code[:, i, :], in0=adj[:, i, :], scalar=0.0, in1=nonzero[:, i, :],
                                               op0=ALU.is_gt, op1=ALU.add).then_inc(code_ready, 1)
            for c in range(C):
                flags = k.ps[:, c % 4, :].bitcast(BF16)
                dve.wait_ge(turned, c + 1)
                nc.vector.tensor_scalar(edge[:, c, :], flags, 1.5, None, ALU.is_ge).then_inc(masks_ready, 1)
                nc.vector.tensor_scalar(k.bound[:, c, :], flags, 1.0, E_HI, ALU.min, ALU.mult).then_inc(masks_ready, 1)
            for c in range(C):
                dve.wait_ge(masks_ready, 2 * C + c)
                nc.vector.tensor_scalar(k.bound[:, c, :], k.bound[:, c, :], E_LO, None, ALU.max).then_inc(masks_ready, 1)
            dve.wait_ge(counted, 1)
            nc.vector.tensor_scalar(k.lone[:], k.bank2(6), 0.0, None, ALU.is_equal).then_inc(masks_ready, 1)
            dve.wait_ge(bias_made, 1)
            nc.vector.scalar_tensor_tensor(out=k.wo_bias[:], in0=k.ps[:, 4, 0:D], scalar=float(C), in1=bo_rows,
                                           op0=ALU.mult, op1=ALU.add)
            dve.wait_ge(x_loaded, 16 * B)
            for i in range(B * C):
                nc.vector.bn_stats(stats[:, i, :], k.x[:, i, :]).then_inc(stats_done, 1)
            for i in range(B * C):
                dve.wait_ge(stats_done, i + 1)
                nc.vector.bn_aggr(k.mv[:, i, :], stats[:, i, :]).then_inc(mv_done, 1)
            dve.wait_ge(mv_done, B * C)
            nc.vector.tensor_scalar(k.var_eps[:], k.mv[:, :, 1], EPS, None, ALU.add).then_inc(mv_done, 1)

        @block.tensor
        def _(pe):
            pe.wait_ge(code_ready, 2 * C + 1)
            for c in range(C):
                if c >= 4:
                    pe.wait_ge(masks_ready, 2 * (c - 3))
                flags = k.ps[:, c % 4, :].bitcast(BF16)
                for i in range(C):
                    last = nc.tensor.transpose(flags[:, i * P:(i + 1) * P], code[:, i, c * P:(c + 1) * P], k.ident16[:])
                last.then_inc(turned, 1)
            pe.wait_ge(consts_ready, 1)
            nc.tensor.matmul(k.ps[:, 4, 0:D], bv_cols, k.w0[:, 3, :], start=True, stop=True).then_inc(bias_made, 1)
            pe.wait_ge(masks_ready, 2 * C)
            for half in range(2):
                for c in range(C):
                    last = nc.tensor.matmul(k.ps[:, 6 + half, :], ones16, edge[:, c, half * 512:(half + 1) * 512],
                                            start=(c == 0), stop=(c == C - 1))
            last.then_inc(counted, 1)


class Scratch:

    def __init__(self, k):
        self.parts = k.dram("qk_parts", [B, 4, P, N], F16)
        self.v = k.dram("v_rows", [B, P, N], F32)
        self.xb = k.dram("x_bias", [B, P, N], F32)
        self.den = k.dram("den_rows", [2, H, N], F32)
        self.rec = k.dram("rec_rows", [2, H, N], F32)
        self.edge = k.dram("edge_rows", [P, C, N], BF16)
        self.xnT = k.dram("xn_turned", [B, P, N], F32)
        self.gv = k.dram("gat_values", [B, 2, P, N], F32)
        self.gs = k.dram("gat_small", [B, P, C * H + D], F32)
        self.grow = k.dram("gat_rows", [B, H * N], F32)
        self.gden = k.dram("gat_den", [2, H, N], F32)
        self.grec = k.dram("gat_rec", [2, H, N], F32)


def rows_of(k, b):
    return [k.x[:, bass.ds(b * C + i, 1), :].rearrange("p o f -> p (o f)") for i in range(C)]


def qkv(k, scr):
    nc = k.nc
    a = Arena(k)
    xn = a.take([2, C, D])
    xnT = a.take([2, N])
    xb = a.take([2, C, D])
    parts = a.take([2, 4, N], F16)
    v = a.take([2, N])
    mean = a.take([2, C])
    rstd = a.take([2, C])

    xn_done, turned, xnT_done, proj_done, high_done, low_done, v_copied, xb_done, small_done = [
        k.sem(f"q_{s}") for s in ("xn_done", "turned", "xnT_done", "proj_done", "high_done", "low_done", "v_copied",
                                  "xb_done", "small_done")]
    stored = [k.sem(f"q_stored{u}") for u in range(2)]
    STORES = 4

    with nc.Block() as block:
        @block.vector
        def _(dve):
            dve.sem_inc(low_done, 2)
            with dve.Fori(0, B // 2) as pair:
                for u in range(2):
                    b = 2 * pair + u
                    rows = rows_of(k, b)
                    nc.vector.tensor_copy(mean[:, u, :], k.mv[:, bass.ds(b * C, C), 0]).then_inc(small_done, 1)
                    nc.vector.tensor_copy(rstd[:, u, :], k.rstd[:, bass.ds(b * C, C)]).then_inc(small_done, 1)
                    dve.wait_ge(small_done, 2 * b + 2)
                    dve.wait_ge(turned, b + 1)
                    dve.wait_ge(xb_done, b + 1)
                    for i in range(C):
                        nc.vector.tensor_scalar(xn[:, u, i, :], rows[i], mean[:, u, i:i + 1], rstd[:, u, i:i + 1],
                                                ALU.subtract, ALU.mult).then_inc(xn_done, 1)
                    for j in range(2):
                        dve.wait_ge(high_done, 2 * b + j + 1)
                        nc.vector.scalar_tensor_tensor(
                            out=parts[:, u, 2 * j + 1, :], in0=k.bank2(2 + 2 * j), scalar=k.bqkv[:, j:j + 1],
                            in1=parts[:, u, 2 * j, :], op0=ALU.add, op1=ALU.subtract).then_inc(low_done, 1)

        @block.tensor
        def _(pe):
            pe.sem_inc(turned, 2)
            pe.sem_inc(proj_done, 6)
            with pe.Fori(0, B // 2) as pair:
                for u in range(2):
                    b = 2 * pair + u
                    pe.wait_ge(xn_done, (b + 1) * C)
                    pe.wait_ge(xnT_done, b + 1)
                    for i in range(C):
                        last = nc.tensor.transpose(k.bank2(0)[:, i * P:(i + 1) * P], xn[:, u, i, :], k.ident[:])
                    last.then_inc(turned, 1)
                    pe.wait_ge(xnT_done, b + 2)
                    for j in range(2):
                        pe.wait_ge(low_done, 2 * b + j + 1)
                        for half in range(2):
                            last = nc.tensor.matmul(k.ps[:, 2 + 2 * j + half, :], k.w0[:, j, :],
                                                    halves(xnT[:, u, :])[half], start=True, stop=True)
                        last.then_inc(proj_done, 1)
                    pe.wait_ge(v_copied, b + 1)
                    for i in range(C):
                        last = nc.tensor.matmul(k.bank2(6)[:, i * P:(i + 1) * P], xnT[:, u, i * P:(i + 1) * P],
                                                k.w0[:, 2, :], start=True, stop=True)
                    last.then_inc(proj_done, 1)

        @block.scalar
        def _(act):
            act.sem_inc(xnT_done, 1)
            act.sem_inc(v_copied, 1)
            with act.Fori(0, B // 2) as pair:
                for u in range(2):
                    b = 2 * pair + u
                    act.wait_ge(turned, b + 3)
                    act.wait_ge(proj_done, 3 * b + 3)
                    nc.scalar.copy(xnT[:, u, :], k.bank2(0)).then_inc(xnT_done, 1)
                    act.wait_ge(stored[u], 16 * STORES * (pair + 1))
                    for j in range(2):
                        act.wait_ge(proj_done, 3 * b + 7 + j)
                        nc.scalar.activation(parts[:, u, 2 * j, :], k.bank2(2 + 2 * j), ACT.Identity,
                                             bias=k.bqkv[:, j:j + 1]).then_inc(high_done, 1)
                    act.wait_ge(proj_done, 3 * b + 9)
                    nc.scalar.copy(v[:, u, :], k.bank2(6)).then_inc(v_copied, 1)

        @block.gpsimd
        def _(pool):
            pool.sem_inc(xb_done, 2)
            with pool.Fori(0, B // 2) as pair:
                for u in range(2):
                    b = 2 * pair + u
                    pool.wait_ge(xn_done, (b + 1) * C)
                    pool.wait_ge(stored[u], 16 * STORES * (pair + 1))
                    nc.gpsimd.tensor_tensor(xb[:, u, :, :], xn[:, u, :, :],
                                            k.wo_bias[:].unsqueeze(1).to_broadcast([P, C, D]), ALU.add).then_inc(xb_done, 1)

        @block.sync
        def _(sp):
            for u in range(2):
                sp.sem_inc(stored[u], 16 * STORES)
            with sp.Fori(0, B // 2) as pair:
                for u in range(2):
                    b = 2 * pair + u
                    at = bass.ds(b, 1)
                    sp.wait_ge(low_done, 2 * b + 4)
                    for j in range(2):
                        sp.dma_start(scr.parts[at, 2 * j:2 * j + 2].rearrange("o r p t -> p (o r) t"),
                                     parts[:, u, 2 * j:2 * j + 2, :]).then_inc(stored[u], 16)
                    sp.wait_ge(v_copied, b + 2)
                    sp.dma_start(scr.v[at].rearrange("o p t -> (o p) t"), v[:, u, :]).then_inc(stored[u], 16)
                    sp.wait_ge(xb_done, b + 3)
                    sp.dma_start(scr.xb[at].rearrange("o p t -> (o p) t"),
                                 xb[:, u, :, :].rearrange("p c f -> p (c f)")).then_inc(stored[u], 16)
            for u in range(2):
                sp.wait_ge(stored[u], 16 * STORES * (B // 2 + 1))


class Peeled:

    @staticmethod
    def run(eng, body, last):
        body(0, 0, 0)
        with eng.Fori(0, (B - 2) // 2) as pair:
            body(2 * pair + 1, 1, pair)
            body(2 * pair + 2, 0, pair + 1)
        body(B - 1, (B - 1) % 2, (B - 1) // 2)
        last()

    @staticmethod
    def back(b, u, c, lag):
        if c >= lag:
            return b, u, c - lag
        return None if is_first(b) else (b - 1, 1 - u, c - lag + C)

    @staticmethod
    def tail(lag):
        return [(B - 1, (B - 1) % 2, c) for c in range(C - lag, C)]


def is_first(b):
    return isinstance(b, int) and b == 0


def attention0(k, scr):
    nc = k.nc
    a = Arena(k)
    qs = a.take([2, H, N], F16)
    ks = a.take([2, H, N], F16)
    v = a.take([2, N])
    xb = a.take([N])
    e = a.take([H, N])
    pm = a.take([8, N])
    ctx = a.take([4, N])
    den = a.take([N])
    r_in = a.take([HS])
    r_out = a.take([HS])
    r_rows = a.take([2, N])
    ctx_sum = a.take([2, N])
    y = a.take([C, D])
    stats = a.take([C, 6])
    mean = a.take([C])
    tmp = a.take([3, C])
    ve = a.take([C])
    rs = a.take([C])

    loaded = [k.sem(f"a_loaded{u}") for u in range(2)]
    (score_done, exp_done, clip_done, pv_done, copied, recip_done, summed, o_done, den_stored, den_loaded,
     rec_stored, rec_loaded, xb_loaded, y_added, y_done, pow_done, res_done) = [
        k.sem(f"a_{s}") for s in ("score_done", "exp_done", "clip_done", "pv_done", "copied", "recip_done", "summed",
                                  "o_done", "den_stored", "den_loaded", "rec_stored", "rec_loaded", "xb_loaded",
                                  "y_added", "y_done", "pow_done", "res_done")]
    LOADS = 4 + 4 + 1
    RECIP_LAG = 2
    PROJECT_AT = 5
    VAR = C + COMBINE
    Y_STEPS = VAR + C
    back, tail = Peeled.back, Peeled.tail

    with nc.Block() as block:
        @block.sync
        def _(sp):
            sp.sem_inc(den_stored, 16)

            def load(b, u, r):
                at = bass.ds(b, 1)
                if r == H:
                    sp.dma_start(v[:, u, :], scr.v[at].rearrange("o p t -> (o p) t")).then_inc(loaded[u], 16)
                    return
                for dst, j in ((qs, r // 2), (ks, 2 + r % 2)):
                    sp.dma_start(dst[r * HS:(r + 1) * HS, u, :, :],
                                 scr.parts[at, j].rearrange("o (h d) t -> d (o h) t", h=H)).then_inc(loaded[u], 16)

            def store_den(b, u, c):
                g = C * b + c
                sp.wait_ge(copied, 2 * g + 3)
                sp.dma_start(scr.den[c % 2], den[0:P:HS, :]).then_inc(den_stored, 16)

            def load_den(b, u, c):
                g = C * b + c
                sp.wait_ge(den_stored, 16 * g + 32)
                sp.dma_start(r_in[:], scr.den[c % 2].rearrange("h (a t) -> (h a) t", t=HS)).then_inc(den_loaded, 16)

            def store_rec(b, u, c):
                g = C * b + c
                sp.wait_ge(recip_done, g + 1)
                sp.dma_start(scr.rec[c % 2].rearrange("h (a t) -> (h a) t", t=HS), r_out[:]).then_inc(rec_stored, 16)

            def load_rec(b, u, c):
                g = C * b + c
                sp.wait_ge(rec_stored, 16 * g + 16)
                for h in range(H):
                    sp.dma_start(r_rows[h * HS:(h + 1) * HS, c % 2, :],
                                 scr.rec[c % 2, h:h + 1, :].to_broadcast([HS, N])).then_inc(rec_loaded, 16)

            def round_trip(g, before):
                if g:
                    store_den(*g)
                if before:
                    store_rec(*before)
                if g:
                    load_den(*g)
                if before:
                    load_rec(*before)

            def body(b, u, _):
                if is_first(b):
                    for u_next in range(2):
                        for r in range(H + 1):
                            load(u_next, u_next, r)
                for c in range(C):
                    round_trip(back(b, u, c, 1), back(b, u, c, 2))
                    if 1 <= c <= H + 1 and not isinstance(b, int):
                        if c == 1:
                            sp.wait_ge(pv_done, 2 * C * b + 4)
                        load(b + 1, 1 - u, c - 1)
                    if c == 1 and not is_first(b):
                        sp.wait_ge(y_added, b)
                        sp.dma_start(xb[:, :], scr.xb[bass.ds(b - 1, 1)].rearrange("o p t -> (o p) t")).then_inc(xb_loaded, 16)

            def last():
                g6, g7 = tail(2)
                round_trip(g7, g6)
                round_trip(None, g7)
                sp.wait_ge(y_added, B)
                sp.dma_start(xb[:, :], scr.xb[B - 1]).then_inc(xb_loaded, 16)

            Peeled.run(sp, body, last)

        @block.tensor
        def _(pe):
            pe.sem_inc(o_done, 2)
            pe.sem_inc(pv_done, 4)

            def scores(b, u, half_b, c, h):
                if c == 0 and h == 0:
                    pe.wait_ge(loaded[u], 16 * LOADS * (half_b + 1))
                pe.wait_ge(exp_done, 4 * (C * b + c) + h + 1)
                for half in range(2):
                    last = nc.tensor.matmul(k.ps[:, 6 * (h % 2) + half, :], ks[:, u, h, c * P:(c + 1) * P],
                                            halves(qs[:, u, h, :])[half], start=True, stop=True)
                last.then_inc(score_done, 1)

            def values(b, u, c, part):
                g = C * b + c
                pe.wait_ge(copied, 2 * g + 1 + part)
                if part == 1 and c == PROJECT_AT - 1 and not is_first(b):
                    pe.wait_ge(y_added, b + 1)
                if part == 0:
                    pe.wait_ge(clip_done, 4 * g + 8)
                for half in range(2):
                    for h in range(H):
                        lhsT = k.ones[:] if part == 0 else v[:, u, c * P + h * HS:c * P + (h + 1) * HS]
                        last = nc.tensor.matmul(
                            k.ps[h * HS:(h + 1) * HS, 4 - 2 * part + half, :], lhsT,
                            halves(pm[:, 4 * (c % 2) + h, :])[half], start=True, stop=True)
                last.then_inc(pv_done, 1)

            def project(b, u):
                pe.wait_ge(summed, 2 * C * b + 2 * C + 8)
                for i in range(C):
                    last = nc.tensor.matmul(k.bank2(2)[:, i * P:(i + 1) * P], ctx_sum[:, u, i * P:(i + 1) * P],
                                            k.w0[:, 3, :], start=True, stop=True)
                last.then_inc(o_done, 1)

            def body(b, u, half_b):
                for c in range(C):
                    scores(b, u, half_b, c, 0)
                    scores(b, u, half_b, c, 1)
                    if g := back(b, u, c, 1):
                        values(*g, 0)
                    scores(b, u, half_b, c, 2)
                    scores(b, u, half_b, c, 3)
                    if c == PROJECT_AT and not is_first(b):
                        pe.wait_ge(copied, 2 * C * b + 2 * PROJECT_AT)
                        project(b - 1, 1 - u)
                    if g := back(b, u, c, 1):
                        values(*g, 1)

            def last():
                for part in range(2):
                    values(*tail(1)[0], part)
                pe.wait_ge(copied, 2 * C * B + 2)
                project(B - 1, (B - 1) % 2)

            Peeled.run(pe, body, last)

        @block.scalar
        def _(act):
            act.sem_inc(exp_done, 2)
            act.sem_inc(copied, 2)

            def copy_den(b, u, c):
                g = C * b + c
                act.wait_ge(pv_done, 2 * g + 5)
                act.wait_ge(den_stored, 16 * g + 16)
                nc.scalar.copy(den[:, :], k.bank2(4)).then_inc(copied, 1)

            def copy_ctx(b, u, c):
                g = C * b + c
                act.wait_ge(pv_done, 2 * g + 6)
                act.wait_ge(summed, 2 * g + 2)
                nc.scalar.copy(ctx[:, c % 4, :], k.bank2(2)).then_inc(copied, 1)

            def body(b, u, _):
                for c in range(C):
                    for h in range(H):
                        if h == 2 and (g := back(b, u, c, 2)):
                            copy_ctx(*g)
                        at = 4 * (C * b + c) + h
                        act.wait_ge(clip_done, at + 1)
                        act.wait_ge(score_done, at + 1)
                        nc.scalar.activation(e[:, h, :], k.bank2(6 * (h % 2)), ACT.Exp, scale=SCALE).then_inc(exp_done, 1)
                    if g := back(b, u, c, 1):
                        copy_den(*g)

            def last():
                g6, g7 = tail(2)
                copy_ctx(*g6)
                copy_den(*g7)
                copy_ctx(*g7)

            Peeled.run(act, body, last)

        @block.vector
        def _(dve):
            dve.sem_inc(clip_done, 4)
            dve.sem_inc(y_added, 1)

            def clip(b, u, c, h):
                if h == 0:
                    dve.wait_ge(pv_done, 2 * (C * b + c) + 2)
                dve.wait_ge(exp_done, 4 * (C * b + c) + h + 3)
                nc.vector.scalar_tensor_tensor(out=pm[:, 4 * (c % 2) + h, :], in0=e[:, h, :], scalar=E_LO,
                                               in1=k.bound[:, c, :], op0=ALU.max, op1=ALU.min).then_inc(clip_done, 1)

            def reciprocal(b, u, c):
                dve.wait_ge(summed, 2 * (C * b + c) + 5)
                dve.wait_ge(den_loaded, 16 * (C * b + c) + 16)
                nc.vector.reciprocal(r_out[:], r_in[:]).then_inc(recip_done, 1)

            def add(b):
                dve.wait_ge(xb_loaded, 16 * b + 16)
                dve.wait_ge(res_done, 3 * b + 3)
                dve.wait_ge(o_done, b + 3)
                nc.vector.tensor_tensor(y[:, :, :].rearrange("p c f -> p (c f)"), k.bank2(2), xb[:, :],
                                        ALU.add).then_inc(y_added, 1)

            def statistics(b, h):
                if h == 0:
                    dve.wait_ge(y_added, b + 2)
                for i in range(2 * h, 2 * h + 2):
                    nc.vector.bn_stats(stats[:, i, :], y[:, i, :]).then_inc(y_done, 1)
                if h == H - 1:
                    dve.wait_ge(y_done, Y_STEPS * b + C)
                    combine_stats(nc, Steps(dve, y_done, Y_STEPS * b + C), stats, mean, ve, tmp)

            def normalise(b, h):
                if h == 0:
                    dve.wait_ge(pow_done, b + 1)
                for i in range(2 * h, 2 * h + 2):
                    nc.vector.tensor_scalar(y[:, i, :], y[:, i, :], mean[:, i:i + 1], rs[:, i:i + 1],
                                            ALU.subtract, ALU.mult).then_inc(y_done, 1)

            def body(b, u, _):
                for c in range(C):
                    for h in range(H):
                        clip(b, u, c, h)
                        if h == 2 and (g := back(b, u, c, RECIP_LAG)):
                            reciprocal(*g)
                        if not is_first(b):
                            if c == PROJECT_AT and h == 3:
                                add(b - 1)
                            if c == PROJECT_AT + 1:
                                statistics(b - 1, h)
                            if c == PROJECT_AT + 2:
                                normalise(b - 1, h)

            def last():
                for g in tail(RECIP_LAG):
                    reciprocal(*g)
                add(B - 1)
                for h in range(H):
                    statistics(B - 1, h)
                for h in range(H):
                    normalise(B - 1, h)

            Peeled.run(dve, body, last)

        @block.gpsimd
        def _(pool):
            pool.sem_inc(summed, 8)
            pool.sem_inc(res_done, 3)
            gamma, beta = [w[:].unsqueeze(1).to_broadcast([P, C, D]) for w in (k.gamma, k.beta)]

            def quotient(b, u, c):
                g = C * b + c
                pool.wait_ge(rec_loaded, 64 * g + 64)
                pool.wait_ge(copied, 2 * g + 4)
                if c == 0:
                    pool.wait_ge(o_done, b + 1)
                    nc.gpsimd.tensor_tensor(ctx_sum[:, u, :], ctx[:, 0, :], r_rows[:, 0, :], ALU.mult).then_inc(summed, 2)
                    return
                nc.gpsimd.tensor_tensor(ctx[:, c % 4, :], ctx[:, c % 4, :], r_rows[:, c % 2, :], ALU.mult).then_inc(summed, 1)
                pool.wait_ge(summed, 2 * g + 9)
                nc.gpsimd.tensor_tensor(ctx_sum[:, u, :], ctx_sum[:, u, :], ctx[:, c % 4, :], ALU.add).then_inc(summed, 1)

            def power(b):
                pool.wait_ge(y_done, Y_STEPS * b + VAR)
                nc.gpsimd.tensor_tensor(rs[:], ve[:], k.minus_half[:, 0:C], ALU.pow).then_inc(pow_done, 1)

            def residual(b):
                pool.wait_ge(y_done, Y_STEPS * b + Y_STEPS)
                nc.gpsimd.tensor_tensor(y[:, :, :], y[:, :, :], gamma, ALU.mult).then_inc(res_done, 1)
                pool.wait_ge(res_done, 3 * b + 4)
                nc.gpsimd.tensor_tensor(y[:, :, :], y[:, :, :], beta, ALU.add).then_inc(res_done, 1)
                pool.wait_ge(res_done, 3 * b + 5)
                x = k.x[:, bass.ds(b * C, C), :]
                nc.gpsimd.tensor_tensor(x, x, y[:, :, :], ALU.add).then_inc(res_done, 1)

            def body(b, u, _):
                for c in range(C):
                    quotient(b, u, c)
                    if c == 3 and not is_first(b):
                        power(b - 1)
                    if c == 4 and not is_first(b):
                        residual(b - 1)

            def last():
                power(B - 1)
                residual(B - 1)

            Peeled.run(pool, body, last)


def layer_norm(k, scr, name):
    nc = k.nc
    a = Arena(k)
    stats = a.take([B * C, 6])
    tmp = a.take([3, B * C])
    xn = a.take([2, C, D])
    xnT = a.take([2, N])
    mean = a.take([2, C])
    rstd = a.take([2, C])
    stats_done, var_done, pow_done, small_done, xn_done, turned, xnT_done = [
        k.sem(f"{name}_{s}") for s in ("stats_done", "var_done", "pow_done", "small_done", "xn_done", "turned", "xnT_done")]
    stored = [k.sem(f"{name}_stored{u}") for u in range(2)]
    means = k.mv[:, :, 0]

    with nc.Block() as block:
        @block.vector
        def _(dve):
            for i in range(B * C):
                nc.vector.bn_stats(stats[:, i, :], k.x[:, i, :]).then_inc(stats_done, 1)
            dve.wait_ge(stats_done, B * C)
            combine_stats(nc, Steps(dve, var_done), stats, means, k.var_eps[:], tmp)
            dve.wait_ge(pow_done, 1)
            with dve.Fori(0, B // 2) as pair:
                for u in range(2):
                    b = 2 * pair + u
                    rows = rows_of(k, b)
                    nc.vector.tensor_copy(mean[:, u, :], k.mv[:, bass.ds(b * C, C), 0]).then_inc(small_done, 1)
                    nc.vector.tensor_copy(rstd[:, u, :], k.rstd[:, bass.ds(b * C, C)]).then_inc(small_done, 1)
                    dve.wait_ge(small_done, 2 * b + 2)
                    dve.wait_ge(turned, b + 1)
                    for i in range(C):
                        nc.vector.tensor_scalar(xn[:, u, i, :], rows[i], mean[:, u, i:i + 1], rstd[:, u, i:i + 1],
                                                ALU.subtract, ALU.mult).then_inc(xn_done, 1)

        @block.gpsimd
        def _(pool):
            pool.wait_ge(var_done, COMBINE)
            nc.gpsimd.tensor_tensor(k.rstd[:], k.var_eps[:], k.minus_half[:], ALU.pow).then_inc(pow_done, 1)

        @block.tensor
        def _(pe):
            pe.sem_inc(turned, 2)
            with pe.Fori(0, B // 2) as pair:
                for u in range(2):
                    b = 2 * pair + u
                    pe.wait_ge(xnT_done, b + 1)
                    pe.wait_ge(xn_done, (b + 1) * C)
                    for i in range(C):
                        last = nc.tensor.transpose(k.bank2(2 * u)[:, i * P:(i + 1) * P], xn[:, u, i, :], k.ident[:])
                    last.then_inc(turned, 1)

        @block.scalar
        def _(act):
            act.sem_inc(xnT_done, 2)
            with act.Fori(0, B // 2) as pair:
                for u in range(2):
                    b = 2 * pair + u
                    act.wait_ge(stored[u], 16 * (pair + 1))
                    act.wait_ge(turned, b + 3)
                    nc.scalar.copy(xnT[:, u, :], k.bank2(2 * u)).then_inc(xnT_done, 1)

        @block.sync
        def _(sp):
            for u in range(2):
                sp.sem_inc(stored[u], 16)
            with sp.Fori(0, B // 2) as pair:
                for u in range(2):
                    b = 2 * pair + u
                    sp.wait_ge(xnT_done, b + 3)
                    sp.dma_start(scr.xnT[bass.ds(b, 1)].rearrange("o p t -> (o p) t"), xnT[:, u, :]).then_inc(stored[u], 16)
            for u in range(2):
                sp.wait_ge(stored[u], 16 * (B // 2 + 1))


def gat_factors(k, scr):
    nc, t = k.nc, k.t
    a = Arena(k)
    xnT = a.take([2, N])
    wide = a.take([D + 2 * H])
    prod = a.take([2, D])
    a12 = a.take([2, D])
    e = a.take([2, C, 3 * H])
    top = a.take([2, 2 * H])
    tops = a.take([2, 2 * H])
    u8 = a.take([2, C, 2 * H])
    spread = a.take([2, H])
    r1 = a.take([2, C, H])
    f = a.take([2, C * H])
    r = a.take([2, H, C])
    rT = a.take([2, P])
    xsum = a.take([2, 1])
    small = a.take([2, C * H + D])
    g = small[:, :, 0:C * H]
    v = a.take([2, N])
    fb = a.take([2, N])

    w_loaded, w_ready = k.sem("g_w_loaded"), k.sem("g_w_ready")
    loaded = [k.sem(f"g_loaded{u}") for u in range(2)]
    stored = [k.sem(f"g_stored{u}") for u in range(2)]
    top_seen = k.sem("g_top_seen")
    wh_done, step, reduced, exp_done, v_done, turned, r_copied, fb_done = [
        k.sem(f"g_{s}") for s in ("wh_done", "step", "reduced", "exp_done", "v_done", "turned", "r_copied", "fb_done")]
    STORES = 4
    E_READY, U_READY, R_READY = 4, 6, 9
    STEPS = 11

    def ps(u):
        return k.ps[:, 4 * u:4 * u + 4, :].rearrange("p a n -> p (a n)").rearrange("p (c n) -> p c n", n=256)

    with nc.Block() as block:
        @block.sync
        def _(sp):
            for u in range(2):
                sp.sem_inc(stored[u], 16 * STORES)
            sp.dma_start(wide[:, 0:D], t["L1_gnn_Wc"]).then_inc(w_loaded, 16)
            for i in range(2):
                sp.dma_start(a12[:, i, :].rearrange("p (h d) -> p h d", h=H),
                             t["L1_gnn_a"][:, HS * (1 - i):HS * (2 - i)].rearrange("(o h) d -> o h d", o=1)
                             .to_broadcast([P, H, HS])).then_inc(w_loaded, 16)
            for u in range(2):
                sp.dma_start(xnT[:, u, :], scr.xnT[u]).then_inc(loaded[u], 16)
            def store(b, u):
                at = bass.ds(b, 1)
                sp.wait_ge(v_done, b + 3)
                sp.dma_start(scr.gv[at, 0].rearrange("o p n -> (o p) n"), v[:, u, :]).then_inc(stored[u], 16)
                sp.wait_ge(fb_done, b + 1)
                sp.dma_start(scr.gv[at, 1].rearrange("o p n -> (o p) n"), fb[:, u, :]).then_inc(stored[u], 16)
                sp.wait_ge(r_copied, b + 3)
                sp.dma_start(scr.gs[at].rearrange("o p n -> (o p) n"), small[:, u, :]).then_inc(stored[u], 16)
                sp.dma_start(scr.grow[at].rearrange("o (q t) -> (o q) t", t=P), rT[0:C * H, u, :]).then_inc(stored[u], 16)

            with sp.Fori(0, B // 2 - 1) as pair:
                for u in range(2):
                    b = 2 * pair + u
                    store(b, u)
                    sp.dma_start(xnT[:, u, :], scr.xnT[bass.ds(b + 2, 1)].rearrange("o p t -> (o p) t")).then_inc(loaded[u], 16)
            for u in range(2):
                store(B - 2 + u, u)
            for u in range(2):
                sp.wait_ge(stored[u], 16 * STORES * (B // 2 + 1))

        @block.tensor
        def _(pe):
            pe.wait_ge(w_ready, 4)
            with pe.Fori(0, B // 2) as pair:
                for u in range(2):
                    b = 2 * pair + u
                    pe.wait_ge(loaded[u], 16 * (pair + 1))
                    pe.wait_ge(v_done, b + 1)
                    pe.wait_ge(r_copied, b + 1)
                    for i in range(C):
                        last = nc.tensor.matmul(ps(u)[:, i, 0:D + 2 * H], xnT[:, u, i * P:(i + 1) * P], wide[:],
                                                start=True, stop=True)
                    last.then_inc(wh_done, 1)
                    pe.wait_ge(exp_done, 3 * b + 3)
                    pe.wait_ge(v_done, b + 3)
                    nc.tensor.transpose(k.ps[0:C * H, 4 * u, 0:P],
                                        r[:, u].rearrange("p h c -> p (h c)"), k.ident[:]).then_inc(turned, 1)

        @block.vector
        def _(dve):
            dve.sem_inc(v_done, 2)
            dve.wait_ge(w_loaded, 48)
            for i in range(2):
                nc.vector.tensor_tensor(prod[:, i, :], wide[:, 0:D], a12[:, i, :], ALU.mult).then_inc(w_ready, 1)
            for i in range(2):
                dve.wait_ge(w_ready, i + 1)
                nc.vector.tensor_reduce(wide[:, D + i * H:D + (i + 1) * H], prod[:, i, :].rearrange("p (h d) -> p h d", h=H),
                                        AX.X, ALU.add).then_inc(w_ready, 1)
            with dve.Fori(0, B // 2) as pair:
                for u in range(2):
                    b = 2 * pair + u
                    s = Steps(dve, step, STEPS * b)
                    dve.wait_ge(wh_done, b + 1)
                    dve.wait_ge(stored[u], 16 * STORES * (pair + 1))
                    s.did(nc.vector.tensor_copy(e[:, u, :, 0:H], ps(u)[:, :, D:D + H]))
                    s.did(nc.vector.tensor_copy(e[:, u, :, 2 * H:3 * H], ps(u)[:, :, D + H:D + 2 * H]))
                    s.did(nc.vector.tensor_scalar(e[:, u, :, H:2 * H], ps(u)[:, :, D:D + H], -1.0, None, ALU.mult))
                    s.wait()
                    s.did(nc.vector.tensor_reduce(top[:, u, :], e[:, u, :, 0:2 * H].rearrange("p c q -> p q c"),
                                                  AX.X, ALU.max))
                    assert s.n == E_READY
                    dve.wait_ge(reduced, b + 1)
                    s.did(nc.vector.tensor_tensor(u8[:, u], e[:, u, :, 0:2 * H],
                                                  tops[:, u, :].unsqueeze(1).to_broadcast([P, C, 2 * H]), ALU.subtract))
                    s.did(nc.vector.tensor_tensor(spread[:, u, :], tops[:, u, 0:H], tops[:, u, H:2 * H], ALU.add))
                    assert s.n == U_READY
                    s.did(nc.vector.tensor_tensor(r1[:, u], e[:, u, :, 2 * H:3 * H],
                                                  tops[:, u, 0:H].unsqueeze(1).to_broadcast([P, C, H]), ALU.add))
                    s.wait()
                    s.did(nc.vector.scalar_tensor_tensor(out=r1[:, u], in0=r1[:, u], scalar=0.0,
                                                         in1=spread[:, u, :].unsqueeze(1).to_broadcast([P, C, H]),
                                                         op0=ALU.max, op1=ALU.subtract))
                    s.wait()
                    s.did(nc.vector.tensor_scalar(r1[:, u], r1[:, u], 0.0, None, ALU.min))
                    assert s.n == R_READY
                    s.did(nc.vector.tensor_reduce(xsum[:, u, :], xnT[:, u, :], AX.X, ALU.add))
                    s.wait()
                    s.did(nc.vector.tensor_scalar(small[:, u, C * H:C * H + D], wide[:, 0:D], xsum[:, u, 0:1], None, ALU.mult))
                    assert s.n == STEPS
                    dve.wait_ge(exp_done, 3 * b + 1)
                    nc.vector.tensor_tensor(v[:, u, :].rearrange("p (c h d) -> p c h d", c=C, h=H),
                                            ps(u)[:, :, 0:D].rearrange("p c (h d) -> p c h d", h=H),
                                            f[:, u, :].rearrange("p (c h) -> p c h", h=H).unsqueeze(3).to_broadcast([P, C, H, HS]),
                                            ALU.mult).then_inc(v_done, 1)

        @block.gpsimd
        def _(pool):
            with pool.Fori(0, B // 2) as pair:
                for u in range(2):
                    b = 2 * pair + u
                    pool.wait_ge(step, STEPS * b + E_READY)
                    pool.sem_inc(top_seen, 1)
                    nc.gpsimd.partition_all_reduce(tops[:, u, :], top[:, u, :], P, bass.bass_isa.ReduceOp.max).then_inc(reduced, 1)

        @block.scalar
        def _(act):
            act.sem_inc(r_copied, 2)
            with act.Fori(0, B // 2) as pair:
                for u in range(2):
                    b = 2 * pair + u
                    act.wait_ge(step, STEPS * b + U_READY)
                    nc.scalar.activation(f[:, u, :].rearrange("p (c h) -> p c h", h=H), u8[:, u, :, 0:H],
                                         ACT.Exp).then_inc(exp_done, 1)
                    nc.scalar.activation(g[:, u, :].rearrange("p (c h) -> p c h", h=H), u8[:, u, :, H:2 * H],
                                         ACT.Exp, scale=1.0 - SLOPE).then_inc(exp_done, 1)
                    act.wait_ge(step, STEPS * b + R_READY)
                    nc.scalar.activation(r[:, u].rearrange("p h c -> p c h"), r1[:, u], ACT.Exp,
                                         scale=1.0 - SLOPE).then_inc(exp_done, 1)
                    act.wait_ge(exp_done, 3 * b + 1)
                    nc.scalar.copy(fb[:, u, :].rearrange("p (q d) -> p q d", d=HS),
                                   f[:, u, :].unsqueeze(2).to_broadcast([P, C * H, HS])).then_inc(fb_done, 1)
                    act.wait_ge(turned, b + 1)
                    nc.scalar.copy(rT[0:C * H, u, :], k.ps[0:C * H, 4 * u, 0:P]).then_inc(r_copied, 1)


def attention1(k, scr):
    nc = k.nc
    a = Arena(k)
    edge = k.bound[:, 0:C // 2, :].bitcast(BF16).rearrange("p a n -> p (a n)").rearrange("p (c n) -> p c n", c=C)
    rows = a.take([2, H, N])
    v = a.take([2, N])
    fb = a.take([2, N])
    small = a.take([2, C * H + D])
    pm = a.take([8, N])
    ctx = a.take([N])
    den = a.take([N])
    r_rows = a.take([N])
    low = a.take([N])
    r_in = a.take([HS])
    r_out = a.take([HS])
    lone32 = a.take([N])
    tens = a.take([P], BF16)

    edge_loaded, tens_ready = k.sem("h_edge_loaded"), k.sem("h_tens_ready")
    loaded = [k.sem(f"h_loaded{u}") for u in range(2)]
    (w_done, pv_done, copied, recip_done, quot_done, low_done, exp_done, elu_done, turned, added,
     den_stored, den_loaded, rec_stored, rec_loaded) = [
        k.sem(f"h_{s}") for s in ("w_done", "pv_done", "copied", "recip_done", "quot_done", "low_done", "exp_done",
                                  "elu_done", "turned", "added", "den_stored", "den_loaded", "rec_stored", "rec_loaded")]
    LOADS = 4
    U_LAST = (B - 1) % 2
    RECIP_AT, QUOT_AT, ELU_AT, ADD_AT = 1, 3, 4, 5

    with nc.Block() as block:
        @block.sync
        def _(sp):
            sp.sem_inc(den_stored, 16)
            sp.dma_start(edge, scr.edge).then_inc(edge_loaded, 16)

            def load(b, u):
                at = bass.ds(b, 1)
                sp.dma_start(rows[:, u, :, :].rearrange("p h n -> p (h n)"),
                             scr.grow[at].to_broadcast([P, H * N])).then_inc(loaded[u], 16)
                sp.dma_start(v[:, u, :], scr.gv[at, 0].rearrange("o p n -> (o p) n")).then_inc(loaded[u], 16)
                sp.dma_start(fb[:, u, :], scr.gv[at, 1].rearrange("o p n -> (o p) n")).then_inc(loaded[u], 16)
                sp.dma_start(small[:, u, :], scr.gs[at].rearrange("o p n -> (o p) n")).then_inc(loaded[u], 16)

            def reciprocals(b, u):
                sp.wait_ge(copied, 2 * b + 1)
                sp.dma_start(scr.gden[u], den[0:P:HS, :]).then_inc(den_stored, 16)
                sp.wait_ge(den_stored, 16 * b + 32)
                sp.dma_start(r_in[:], scr.gden[u].rearrange("h (a t) -> (h a) t", t=HS)).then_inc(den_loaded, 16)
                sp.wait_ge(recip_done, b + 1)
                sp.dma_start(scr.grec[u].rearrange("h (a t) -> (h a) t", t=HS), r_out[:]).then_inc(rec_stored, 16)
                sp.wait_ge(rec_stored, 16 * b + 16)
                for h in range(H):
                    sp.dma_start(r_rows[h * HS:(h + 1) * HS, :],
                                 scr.grec[u, h:h + 1, :].to_broadcast([HS, N])).then_inc(rec_loaded, 16)

            def body(b, u, _):
                if is_first(b):
                    load(0, 0)
                    load(1, 1)
                    return
                if not isinstance(b, int):
                    sp.wait_ge(pv_done, C * b + 2)
                    load(b + 1, 1 - u)
                reciprocals(b - 1, 1 - u)

            Peeled.run(sp, body, lambda: reciprocals(B - 1, U_LAST))

        @block.gpsimd
        def _(pool):
            nc.gpsimd.tensor_copy(lone32, k.lone[:])
            nc.gpsimd.memset(tens, float(C)).then_inc(tens_ready, 1)

        @block.tensor
        def _(pe):
            pe.sem_inc(pv_done, 2)
            pe.sem_inc(turned, 1)
            pe.wait_ge(tens_ready, 1)

            def values(b, u, half_b, c):
                if c == 0:
                    pe.wait_ge(loaded[u], 16 * LOADS * (half_b + 1))
                    pe.wait_ge(added, b + 1)
                    for half in range(2):
                        nc.tensor.matmul(k.ps[:, 4 * u + half, :], small[:, u, C * H:C * H + D], halves(lone32)[half],
                                         start=True, stop=False, skip_group_check=True)
                        nc.tensor.matmul(k.ps[:, 4 * u + 2 + half, :], tens, halves(k.lone[:])[half],
                                         start=True, stop=False, skip_group_check=True)
                pe.wait_ge(w_done, 4 * (C * b + c) + 4)
                for half in range(2):
                    for bank, w in ((0, v), (2, fb)):
                        for h in range(H):
                            last = nc.tensor.matmul(
                                k.ps[h * HS:(h + 1) * HS, 4 * u + bank + half, :],
                                w[:, u, c * P + h * HS:c * P + (h + 1) * HS], halves(pm[:, 4 * (c % 2) + h, :])[half],
                                start=False, stop=(c == C - 1), skip_group_check=True)
                last.then_inc(pv_done, 1)

            def turn(b, u):
                pe.wait_ge(elu_done, b + 1)
                for i in range(C):
                    last = nc.tensor.transpose(k.bank2(4 * u)[:, i * P:(i + 1) * P], ctx[:, i * P:(i + 1) * P], k.ident[:])
                last.then_inc(turned, 1)

            def body(b, u, half_b):
                for c in range(C):
                    values(b, u, half_b, c)
                    if c == ELU_AT and not is_first(b):
                        turn(b - 1, 1 - u)

            Peeled.run(pe, body, lambda: turn(B - 1, U_LAST))

        @block.vector
        def _(dve):
            dve.sem_inc(added, 2)
            dve.wait_ge(edge_loaded, 16)

            def weights(b, u, half_b, c):
                if c == 0:
                    dve.wait_ge(loaded[u], 16 * LOADS * (half_b + 1))
                dve.wait_ge(pv_done, C * b + c + 1)
                for h in range(H):
                    nc.vector.scalar_tensor_tensor(out=pm[:, 4 * (c % 2) + h, :], in0=rows[:, u, h, :],
                                                   scalar=small[:, u, c * H + h:c * H + h + 1], in1=edge[:, c, :],
                                                   op0=ALU.max, op1=ALU.mult).then_inc(w_done, 1)

            def reciprocal(b):
                dve.wait_ge(den_loaded, 16 * b + 16)
                nc.vector.reciprocal(r_out[:], r_in[:]).then_inc(recip_done, 1)

            def quotient(b):
                dve.wait_ge(copied, 2 * b + 2)
                dve.wait_ge(rec_loaded, 64 * b + 64)
                nc.vector.tensor_tensor(ctx[:], ctx[:], r_rows[:], ALU.mult).then_inc(quot_done, 1)
                dve.wait_ge(quot_done, b + 1)
                nc.vector.tensor_scalar(low[:], ctx[:], 0.0, None, ALU.min).then_inc(low_done, 1)

            def elu(b):
                dve.wait_ge(exp_done, b + 1)
                nc.vector.scalar_tensor_tensor(out=ctx[:], in0=low[:], scalar=-1.0, in1=ctx[:],
                                               op0=ALU.add, op1=ALU.max).then_inc(elu_done, 1)

            def add(b, u):
                dve.wait_ge(turned, b + 2)
                x = k.x[:, bass.ds(b * C, C), :].rearrange("p c f -> p (c f)")
                nc.vector.tensor_tensor(x, k.bank2(4 * u), x, ALU.add).then_inc(added, 1)

            def body(b, u, half_b):
                for c in range(C):
                    weights(b, u, half_b, c)
                    if not is_first(b):
                        if c == RECIP_AT:
                            reciprocal(b - 1)
                        if c == QUOT_AT:
                            quotient(b - 1)
                        if c == ELU_AT:
                            elu(b - 1)
                        if c == ADD_AT:
                            add(b - 1, 1 - u)

            def last():
                reciprocal(B - 1)
                quotient(B - 1)
                elu(B - 1)
                add(B - 1, U_LAST)

            Peeled.run(dve, body, last)

        @block.scalar
        def _(act):
            def finish(b, u):
                act.wait_ge(pv_done, C * b + C + 2)
                act.wait_ge(den_stored, 16 * b + 16)
                nc.scalar.copy(den[:], k.bank2(4 * u + 2)).then_inc(copied, 1)
                act.wait_ge(turned, b + 1)
                nc.scalar.copy(ctx[:], k.bank2(4 * u)).then_inc(copied, 1)
                act.wait_ge(low_done, b + 1)
                nc.scalar.activation(low[:], low[:], ACT.Exp).then_inc(exp_done, 1)

            with act.Fori(0, B // 2) as pair:
                for u in range(2):
                    finish(2 * pair + u, u)


class ExpertWeights:

    def __init__(self, layer, hidden, w1, b1, wg, gate_biases, w2, b2):
        self.layer, self.hidden = layer, hidden
        self.w1, self.b1, self.wg, self.gate_biases, self.w2, self.b2 = w1, b1, wg, gate_biases, w2, b2


def experts(k, ex, out=None):
    nc, t = k.nc, k.t
    a = Arena(k)
    T = 4
    TOK = T * P
    UNITS = B * C // T
    K = ex.hidden // P
    ED = E * D
    WS = 64.0
    CHUNK_COLS = ED if ex.layer == 1 else D
    LOGIT_CHUNKS = K if ex.layer == 1 else 1
    SCORES = 3

    w1 = a.take([2, K * P], F16)
    wg = a.take([2, LOGIT_CHUNKS, E], F16)
    w2 = a.take([2, K, CHUNK_COLS], F16)
    b2 = a.take([ED], F16)
    b2_high = a.take([ED], F16)
    pick_rows = a.take([P], F16)
    w32 = a.take([K * CHUNK_COLS])
    w1_32 = a.take([K * P])
    wg32 = a.take([LOGIT_CHUNKS, E])
    b2_32 = a.take([ED])
    b1 = a.take([K])
    bg = a.take([len(ex.gate_biases), E])
    key = a.take([E])

    stats = a.take([T, 6])
    tmp = a.take([3, T])
    mean, ve, rs = a.take([T]), a.take([T]), a.take([T])
    xn = a.take([T, D])
    xT = a.take([2, 2, TOK], F16)
    h32 = a.take([2, TOK])
    h = a.take([2, 2, K, TOK], F16)
    prod = a.take([2, ED])

    l = a.take([T, E])
    expl = a.take([T, E])
    at = a.take([T, E])
    hot = a.take([2, T, E])
    top = a.take([2, T])
    pick = a.take([T])
    q = a.take([2, T])
    w = a.take([T, E])

    (w_loaded, w_high, w_ready, consts, ln_step, pow_done, turned, xhi_done, xlo_done, h_made, h32_done, hi_done, lo_done,
     y_made, prod_done, sum_step, logits_done, gate_step, exp_done, stored) = [
        k.sem(f"m{ex.layer}_{s}") for s in (
            "w_loaded", "w_high", "w_ready", "consts", "ln_step", "pow_done", "turned", "xhi_done", "xlo_done", "h_made",
            "h32_done", "hi_done", "lo_done", "y_made", "prod_done", "sum_step", "logits_done", "gate_step", "exp_done",
            "stored")]
    LN_STEPS = T + COMBINE + T
    DIFF_READY, GATE_STEPS = ((14, 20), (3, 10))[ex.layer]
    SUM_STEPS = 4
    loads = [(w1_32, ex.w1), (b1, ex.b1), (wg32, ex.wg), (b2_32, ex.b2)]
    loads += [(bg[:, i, :], v) for i, v in enumerate(ex.gate_biases)] + ex.w2(w32)
    STEPS = 16
    EVERY = STEPS // K
    lane = lambda ap: ap.unsqueeze(1).to_broadcast([P, T, E])
    per = lambda ap: ap.unsqueeze(2).to_broadcast([P, T, E])

    def rows(m):
        return [k.x[:, bass.ds(T * m + i, 1), :].rearrange("p o f -> p (o f)") for i in range(T)]

    def run(eng, body):
        body(-2, 0, False, False, True)
        body(-1, 1, False, True, True)
        with eng.Fori(0, UNITS // 2 - 1) as pair:
            body(2 * pair, 0, True, True, True)
            body(2 * pair + 1, 1, True, True, True)
        body(UNITS - 2, 0, True, True, False)
        body(UNITS - 1, 1, True, False, False)

    with nc.Block() as block:
        @block.sync
        def _(sp):
            for dst, src in loads:
                sp.dma_start(dst, src).then_inc(w_loaded, 16)
            if out is not None:
                out_rows = tile_rows(out.rearrange("b n f -> (b n) f"))
                with sp.Fori(0, UNITS) as m:
                    sp.wait_ge(sum_step, SUM_STEPS * T * m + SUM_STEPS * (T + 2))
                    sp.dma_start(out_rows[:, bass.ds(T * m, T), :], k.x[:, bass.ds(T * m, T), :]).then_inc(stored, 16)
                sp.wait_ge(stored, 16 * UNITS)

        @block.tensor
        def _(pe):
            pe.sem_inc(turned, 1)
            pe.sem_inc(h_made, 2 * K)
            pe.sem_inc(y_made, 2 * T)

            def turn(m, u):
                pe.wait_ge(ln_step, LN_STEPS * m + LN_STEPS + 1)
                pe.wait_ge(xlo_done, m + 1)
                for i in range(T):
                    last = nc.tensor.transpose(k.ps[:, 6, i * P:(i + 1) * P], xn[:, i, :], k.ident[:])
                last.then_inc(turned, 1)

            def hidden(m, u, j):
                if j == 0:
                    pe.wait_ge(xlo_done, m + 2)
                pe.wait_ge(h32_done, K * m + j + 1)
                for n, (wp, xp) in enumerate(((0, 0), (0, 1), (1, 0))):
                    last = nc.tensor.matmul(k.ps[:, 4 + j % 2, :], w1[:, wp, j * P:(j + 1) * P], xT[:, u, xp, :],
                                            start=(n == 0), stop=(n == SCORES - 1))
                last.then_inc(h_made, 1)

            def logits(m, u):
                pe.wait_ge(gate_step, GATE_STEPS * m + 1)
                if ex.layer == 1:
                    pe.wait_ge(lo_done, K * m + K + 2)
                for i in range(T):
                    n = 0
                    for j in range(LOGIT_CHUNKS):
                        for ap, wp in ((0, 0), (0, 1), (1, 0)):
                            src = h[:, u, ap, j, :] if ex.layer == 1 else xT[:, u, ap, :]
                            last = nc.tensor.matmul(k.ps[:, 7, i * E:(i + 1) * E], src[:, i * P:(i + 1) * P], wg[:, wp, j, :],
                                                    start=(n == 0), stop=(n == SCORES * LOGIT_CHUNKS - 1))
                            n += 1
                last.then_inc(logits_done, 1)

            def outputs(m, u, i, quarter):
                bank = 2 * (i % 2)
                if quarter == 0:
                    if i == 0:
                        pe.wait_ge(lo_done, K * m + K + 2)
                    pe.wait_ge(prod_done, T * m + i + 1)
                    for half in range(2):
                        nc.tensor.matmul(k.ps[:, bank + half, :], pick_rows, halves(b2)[half],
                                         start=True, stop=False, skip_group_check=True)
                for j in range(quarter * K // 4, (quarter + 1) * K // 4):
                    for hp, wp in ((0, 0), (0, 1), (1, 0)):
                        for piece in range(max(1, CHUNK_COLS // 512)):
                            n = min(512, CHUNK_COLS)
                            at_col = piece * n if ex.layer == 1 else (j * E // K) * D
                            last = nc.tensor.matmul(k.bank2(bank)[:, at_col:at_col + n], h[:, u, hp, j, i * P:(i + 1) * P],
                                                    w2[:, wp, j, piece * n:(piece + 1) * n],
                                                    start=False, stop=True, skip_group_check=True)
                if quarter == 3:
                    last.then_inc(y_made, 1)

            def body(n, u, do_outputs, do_hidden, do_norm):
                if do_hidden and not do_outputs:
                    pe.wait_ge(w_ready, 5)
                for s in range(STEPS):
                    if do_hidden and s % EVERY == 0:
                        hidden(n + 1, 1 - u, s // EVERY)
                    if do_outputs:
                        outputs(n, u, s // 4, s % 4)
                    if do_norm and s == 8:
                        turn(n + 2, u)
                    if do_hidden and s == (1, STEPS - 1)[ex.layer]:
                        logits(n + 1, 1 - u)

            run(pe, body)

        @block.scalar
        def _(act):
            act.sem_inc(h32_done, 2)
            act.wait_ge(w_loaded, 16 * len(loads))
            for dst, src in ((w1[:, 0, :], w1_32), (wg[:, 0], wg32), (b2_high, b2_32),
                             (w2[:, 0].rearrange("p k c -> p (k c)"), w32)):
                nc.scalar.activation(dst, src, ACT.Identity, scale=WS).then_inc(w_high, 1)

            def body(n, u, do_outputs, do_hidden, do_norm):
                if do_outputs:
                    act.wait_ge(gate_step, GATE_STEPS * n + GATE_STEPS + DIFF_READY)
                    if ex.layer == 0:
                        nc.scalar.activation(q[:, 1, :], pick, ACT.Exp).then_inc(exp_done, 1)
                    else:
                        nc.scalar.activation(expl, l, ACT.Exp).then_inc(exp_done, 1)
                m, v = n + 1, 1 - u
                for s in range(STEPS):
                    if do_hidden and s % EVERY == 0:
                        j = s // EVERY
                        act.wait_ge(lo_done, K * m + j + 1)
                        act.wait_ge(h_made, K * m + j + 1 + 2 * K)
                        nc.scalar.activation(h32[:, j % 2, :], k.ps[:, 4 + j % 2, :], (ACT.Relu, ACT.Gelu)[ex.layer],
                                             bias=b1[:, j:j + 1], scale=1.0 / WS).then_inc(h32_done, 1)
                        if j == 0:
                            act.wait_ge(y_made, T * m + T)
                        act.wait_ge(h32_done, K * m + j + 3)
                        nc.scalar.copy(h[:, v, 0, j, :], h32[:, j % 2, :]).then_inc(hi_done, 1)
                    if do_norm and s == 9:
                        act.wait_ge(h_made, K * (n + 2) + K)
                        act.wait_ge(turned, n + 2 + 2)
                        nc.scalar.copy(xT[:, u, 0, :], k.ps[:, 6, :]).then_inc(xhi_done, 1)

            run(act, body)

        @block.vector
        def _(dve):
            tt, stt, ts = nc.vector.tensor_tensor, nc.vector.scalar_tensor_tensor, nc.vector.tensor_scalar
            red = nc.vector.tensor_reduce
            dve.sem_inc(ln_step, 1)
            dve.sem_inc(xlo_done, 1)
            dve.sem_inc(lo_done, 2)
            dve.sem_inc(prod_done, 2)
            dve.sem_inc(gate_step, GATE_STEPS)

            def statistics(m):
                base = LN_STEPS * m + 1
                dve.wait_ge(ln_step, base)
                x = rows(m)
                for i in range(T):
                    nc.vector.bn_stats(stats[:, i, :], x[i]).then_inc(ln_step, 1)
                dve.wait_ge(ln_step, base + T)
                combine_stats(nc, Steps(dve, ln_step, base + T), stats, mean, ve, tmp)

            def normalise(m):
                dve.wait_ge(pow_done, m + 1)
                dve.wait_ge(turned, m + 1)
                x = rows(m)
                for i in range(T):
                    ts(xn[:, i, :], x[i], mean[:, i:i + 1], rs[:, i:i + 1], ALU.subtract, ALU.mult).then_inc(ln_step, 1)

            def gate(m):
                s = Steps(dve, gate_step, GATE_STEPS * m + GATE_STEPS)
                dve.wait_ge(logits_done, m + 1)
                dve.wait_ge(prod_done, T * m + 2)
                s.did(stt(out=l, in0=k.ps[:, 7, 0:T * E].rearrange("p (n e) -> p n e", e=E), scalar=1.0 / WS,
                          in1=lane(bg[:, 0, :]), op0=ALU.mult, op1=ALU.add))
                s.wait()
                if ex.layer == 0:
                    s.did(tt(l, l, lane(bg[:, 1, :]), ALU.add))
                    for j in range(2):
                        s.wait()
                        s.did(red(top[:, j, :], l, AX.X, ALU.max))
                        s.wait()
                        s.did(tt(at, l, per(top[:, j, :]), ALU.is_equal))
                        s.wait()
                        s.did(tt(at, at, lane(key), ALU.mult))
                        s.wait()
                        s.did(red(pick, at, AX.X, ALU.max))
                        s.wait()
                        s.did(tt(hot[:, j], at, per(pick), ALU.is_equal))
                        if j == 0:
                            s.wait()
                            s.did(stt(out=l, in0=hot[:, 0], scalar=-3e38, in1=l, op0=ALU.mult, op1=ALU.add))
                    s.wait()
                    s.did(tt(pick, top[:, 1, :], top[:, 0, :], ALU.subtract))
                    assert s.n == DIFF_READY
                    dve.wait_ge(exp_done, m + 1)
                    s.did(ts(q[:, 0, :], q[:, 1, :], 1.0, WS, ALU.add, ALU.mult))
                    s.wait()
                    s.did(nc.vector.reciprocal(q[:, 0, :], q[:, 0, :]))
                    s.wait()
                    s.did(tt(q[:, 1, :], q[:, 1, :], q[:, 0, :], ALU.mult))
                    s.did(tt(w, hot[:, 0], per(q[:, 0, :]), ALU.mult))
                    s.wait()
                    s.did(tt(at, hot[:, 1], per(q[:, 1, :]), ALU.mult))
                    s.wait()
                    s.did(tt(w, w, at, ALU.add))
                else:
                    s.did(red(pick, l, AX.X, ALU.max))
                    s.wait()
                    s.did(tt(l, l, per(pick), ALU.subtract))
                    assert s.n == DIFF_READY
                    s.wait()
                    s.did(ts(at, l, 0.0, None, ALU.is_ge))
                    s.wait()
                    s.did(tt(at, at, lane(key), ALU.mult))
                    s.wait()
                    s.did(red(pick, at, AX.X, ALU.max))
                    s.wait()
                    s.did(tt(hot[:, 0], at, per(pick), ALU.is_equal))
                    dve.wait_ge(exp_done, m + 1)
                    s.did(red(q[:, 0, :], expl, AX.X, ALU.add))
                    s.wait()
                    s.did(nc.vector.reciprocal(q[:, 0, :], q[:, 0, :]))
                    s.wait()
                    s.did(stt(out=w, in0=hot[:, 0], scalar=1.0 / WS, in1=per(q[:, 0, :]), op0=ALU.mult, op1=ALU.mult))
                assert s.n == GATE_STEPS
                s.wait()

            def body(n, u, do_outputs, do_hidden, do_norm):
                if do_hidden and not do_outputs:
                    dve.wait_ge(consts, 4)
                    for i, (dst, src, high) in enumerate((
                            (w1[:, 1, :], w1_32, w1[:, 0, :]), (wg[:, 1], wg32, wg[:, 0]),
                            (b2[HS:2 * HS, :], b2_32[HS:2 * HS, :], b2_high[HS:2 * HS, :]),
                            (w2[:, 1].rearrange("p k c -> p (k c)"), w32, w2[:, 0].rearrange("p k c -> p (k c)")))):
                        dve.wait_ge(w_high, i + 1)
                        stt(out=dst, in0=src, scalar=WS, in1=high, op0=ALU.mult, op1=ALU.subtract).then_inc(w_ready, 1)
                    nc.vector.tensor_copy(b2[0:HS, :], b2_high[0:HS, :]).then_inc(w_ready, 1)
                if do_outputs:
                    gate(n)
                m, v = n + 1, 1 - u
                for s in range(STEPS):
                    if do_norm and s == 0:
                        statistics(n + 2)
                    if do_norm and s == 4:
                        normalise(n + 2)
                    if do_norm and s == 10:
                        dve.wait_ge(xhi_done, n + 2 + 1)
                        tt(xT[:, u, 1, :], k.ps[:, 6, :], xT[:, u, 0, :], ALU.subtract).then_inc(xlo_done, 1)
                    if do_outputs and s % 4 == 3:
                        i = s // 4
                        dve.wait_ge(y_made, T * n + i + 1 + 2 * T)
                        dve.wait_ge(sum_step, SUM_STEPS * (T * n + i) + SUM_STEPS)
                        tt(prod[:, i % 2, :].rearrange("p (e d) -> p e d", e=E),
                           k.bank2(2 * (i % 2)).rearrange("p (e d) -> p e d", e=E),
                           w[:, i, :].unsqueeze(2).to_broadcast([P, E, D]), ALU.mult).then_inc(prod_done, 1)
                    if do_hidden and s % EVERY == 0:
                        j = s // EVERY
                        dve.wait_ge(hi_done, K * m + j + 1)
                        tt(h[:, v, 1, j, :], h32[:, j % 2, :], h[:, v, 0, j, :], ALU.subtract).then_inc(lo_done, 1)

            run(dve, body)

        @block.gpsimd
        def _(pool):
            pool.sem_inc(sum_step, 2 * SUM_STEPS)
            for e in range(E):
                nc.gpsimd.memset(key[:, e:e + 1], float(E - e))
            nc.gpsimd.memset(b2, 0.0).then_inc(consts, 1)
            nc.gpsimd.memset(pick_rows, 0.0).then_inc(consts, 1)
            pool.wait_ge(consts, 2)
            for row in (0, HS):
                nc.gpsimd.memset(pick_rows[row:row + 1, :], 1.0).then_inc(consts, 1)
            pool.wait_ge(consts, 4)
            tt = nc.gpsimd.tensor_tensor

            def body(n, u, do_outputs, do_hidden, do_norm):
                if do_norm:
                    m = n + 2
                    pool.wait_ge(ln_step, LN_STEPS * m + 1 + T + COMBINE)
                    tt(rs, ve, k.minus_half[:, 0:T], ALU.pow).then_inc(pow_done, 1)
                if do_outputs:
                    x = rows(n)
                    for i in range(T):
                        base = SUM_STEPS * (T * n + i) + 2 * SUM_STEPS
                        pool.wait_ge(prod_done, T * n + i + 3)
                        for step, width in enumerate((ED // 2, ED // 4, ED // 8)):
                            if step:
                                pool.wait_ge(sum_step, base + step)
                            y = prod[:, i % 2, 0:width]
                            tt(y, y, prod[:, i % 2, width:2 * width], ALU.add).then_inc(sum_step, 1)
                        pool.wait_ge(sum_step, base + 3)
                        tt(x[i], x[i], y, ALU.add).then_inc(sum_step, 1)

            run(pool, body)


def ffn0(k):
    t = k.t
    row = lambda v: v.rearrange("(o e) -> o e", o=1).to_broadcast([P, E])
    experts(k, ExpertWeights(
        0, E * 256, t["L0_ffn_W1p"], t["L0_ffn_b1T"], t["L0_ffn_Wg"].rearrange("(j p) e -> p j e", p=P),
        [row(t["L0_ffn_bg"]), row(t["L0_ffn_bias"])],
        lambda dst: [(dst.rearrange("p (k d) -> p k d", d=D), t["L0_ffn_W2"].rearrange("e (j p) d -> p (e j) d", p=P))],
        t["L0_ffn_b2"].rearrange("(o e) d -> o (e d)", o=1).to_broadcast([P, E * D])))


def ffn1(k, out):
    t = k.t
    K = 4
    experts(k, ExpertWeights(
        1, K * P, t["L1_ffn_W1"], t["L1_ffn_b1T"], t["L1_ffn_Wg"].rearrange("(j p) e -> p j e", p=P),
        [t["L1_ffn_bg"].rearrange("(o e) -> o e", o=1).to_broadcast([P, E])],
        lambda dst: [(dst.rearrange("p (k c) -> p k c", k=K)[:, :, e * D:(e + 1) * D],
                      t["L1_ffn_Wd"][e].rearrange("(j p) d -> p j d", p=P)) for e in range(E)],
        t["L1_ffn_bd"].rearrange("(o e) d -> o (e d)", o=1).to_broadcast([P, E * D])), out)


def build(nc, t, out):
    with ExitStack() as ctx:
        k = Core(nc, ctx, t)
        scr = Scratch(k)
        setup(k, scr)
        qkv(k, scr)
        attention0(k, scr)
        ffn0(k)
        layer_norm(k, scr, "n3")
        gat_factors(k, scr)
        attention1(k, scr)
        ffn1(k, out)


def layouts(inputs):
    a = {n: np.ascontiguousarray(np.asarray(v)) for n, v in inputs.items()}
    for n in ("L0_gnn_Wq", "L0_gnn_Wk", "L0_gnn_Wv", "L0_gnn_Wo"):
        a[n + "T"] = np.ascontiguousarray(a.pop(n).T)
    a["L1_gnn_Wc"] = np.ascontiguousarray(a.pop("L1_gnn_W").transpose(1, 0, 2).reshape(D, D))
    a["L0_ffn_W1p"] = np.ascontiguousarray(a.pop("L0_ffn_W1").transpose(1, 0, 2).reshape(D, -1))
    a["L0_ffn_b1T"] = np.ascontiguousarray(a.pop("L0_ffn_b1").reshape(-1, P).T)
    a["L1_ffn_b1T"] = np.ascontiguousarray(a.pop("L1_ffn_b1").reshape(-1, P).T)
    a["ident"] = np.eye(P, dtype=np.float32)
    return a


def kernel(**inputs):
    import concourse.bacc as bacc
    from concourse.bass_utils import run_bass_kernel_spmd

    nc = bacc.Bacc("TRN2", target_bir_lowering=False, num_devices=1)
    arrays = layouts(inputs)
    t = {n: nc.dram_tensor(n, a.shape, mybir.dt.from_np(a.dtype), kind="ExternalInput").ap() for n, a in arrays.items()}
    out = nc.dram_tensor("out", (B, N, D), F32, kind="ExternalOutput").ap()
    build(nc, t, out)
    r = run_bass_kernel_spmd(nc, [arrays], core_ids=[0])
    return r.results[0]["out"]
```

```python
from contextlib import ExitStack

import concourse.bass as bass
from concourse import mybir
import numpy as np

ALU = mybir.AluOpType
ACT = mybir.ActivationFunctionType
AX = mybir.AxisListType
F32 = mybir.dt.float32
F16 = mybir.dt.float16
BF16 = mybir.dt.bfloat16
I32 = mybir.dt.int32

P = 128
B, N, D = 8, 1024, 128
H, HS = 4, 32
E = 8
C = N // P
EPS = 1e-5
CLIP = 10.0
E_HI = float(np.float32(np.exp(CLIP)))
E_LO = float(np.float32(np.exp(-CLIP)))
SCALE = float(HS) ** -0.5
SLOPE = 0.2


class Steps:

    def __init__(self, eng, sem, base=0):
        self.eng, self.sem, self.base, self.n = eng, sem, base, 0

    def did(self, ins):
        self.n += 1
        ins.then_inc(self.sem, 1)
        return ins

    def wait(self):
        self.eng.wait_ge(self.sem, self.base + self.n)


def halves(ap):
    return [ap[:, 0:512], ap[:, 512:1024]]


COMBINE = 7


def combine_stats(nc, steps, stats, mean, var_eps, tmp):
    ms, ds, vs = tmp[:, 0], tmp[:, 1], tmp[:, 2]
    tt, stt = nc.vector.tensor_tensor, nc.vector.scalar_tensor_tensor
    steps.did(tt(ms, stats[:, :, 1], stats[:, :, 4], ALU.add))
    steps.did(tt(ds, stats[:, :, 1], stats[:, :, 4], ALU.subtract))
    steps.did(tt(vs, stats[:, :, 2], stats[:, :, 5], ALU.add))
    steps.wait()
    steps.did(nc.vector.tensor_scalar(mean, ms, 0.5, None, ALU.mult))
    steps.did(stt(out=ds, in0=ds, scalar=0.25, in1=ds, op0=ALU.mult, op1=ALU.mult))
    steps.did(nc.vector.tensor_scalar(vs, vs, 1.0 / D, EPS, ALU.mult, ALU.add))
    steps.wait()
    steps.did(tt(var_eps, vs, ds, ALU.add))


class Core:

    def __init__(self, nc, ctx, t):
        self.nc, self.ctx, self.t = nc, ctx, t
        sb = self.sb
        self.x = sb("x_res", [P, B * C, D], F32)
        self.bound = sb("bound", [P, C, N], F32)
        self.lone = sb("lone", [P, N], BF16)
        self.ident = sb("ident_sb", [P, P], F32)
        self.ident16 = sb("ident16", [P, P], BF16)
        self.ones = sb("ones", [P, HS], F32)
        self.minus_half = sb("minus_half", [P, C], F32)
        self.wo_bias = sb("wo_bias", [P, D], F32)
        self.rows3 = sb("rows3", [P, 3, D], F32)
        self.gamma, self.beta = self.rows3[:, 1, :], self.rows3[:, 2, :]
        self.w0 = sb("w0", [P, 4, D], F32)
        self.bqkv = sb("bqkv", [P, 3], F32)
        self.arena = sb("arena", [P, ARENA // 4], F32)
        self.ps = ctx.enter_context(nc.psum_tensor("ps", [P, 8, 512], F32))

    def sb(self, name, shape, dt):
        return self.ctx.enter_context(self.nc.sbuf_tensor(name, shape, dt))

    def sem(self, name):
        return self.ctx.enter_context(self.nc.semaphore(name))

    def dram(self, name, shape, dt):
        return self.nc.dram_tensor(name, shape, dt).ap()

    def bank2(self, k):
        return self.ps[:, k:k + 2, :].rearrange("p a n -> p (a n)")


class Arena:

    def __init__(self, core):
        self.core, self.at = core, 0

    def take(self, shape, dt=F32):
        size = 2 if dt in (F16, BF16) else 4
        words = int(np.prod(shape)) * size // 4
        ap = self.core.arena[:, self.at:self.at + words]
        self.at += words
        assert self.at * 4 <= ARENA, self.at * 4
        if dt != F32:
            ap = ap.bitcast(dt)
        if len(shape) == 1:
            return ap
        names = "abcd"[:len(shape)]
        sizes = {n: s for n, s in zip(names, shape)}
        return ap.rearrange(f"p ({' '.join(names)}) -> p {' '.join(names)}", **sizes)


ARENA = 133 * 1024 + 768


def tile_rows(dram):
    return dram.rearrange("(n p) f -> p n f", p=P)


class Scratch:

    def __init__(self, k):
        self.parts = k.dram("qk_parts", [B, 4, P, N], F16)
        self.v = k.dram("v_rows", [B, P, N], F32)
        self.xb = k.dram("x_bias", [B, P, N], F32)
        self.den = k.dram("den_rows", [2, H, N], F32)
        self.rec = k.dram("rec_rows", [2, H, N], F32)
        self.edge = k.dram("edge_rows", [P, C, N], BF16)
        self.gv = k.dram("gat_values", [B, 2, P, N], F32)
        self.gs = k.dram("gat_small", [B, P, C * H + D], F32)
        self.grow = k.dram("gat_rows", [B, H * N], F32)
        self.gden = k.dram("gat_den", [2, H, N], F32)
        self.grec = k.dram("gat_rec", [2, H, N], F32)


def prepare(k, scr):
    nc, t = k.nc, k.t
    a = Arena(k)
    adj = a.take([C, N], I32)
    sign = a.take([C, N], BF16)
    edge = a.take([C, N], BF16)
    ones16 = a.take([P], BF16)
    bv_cols = a.take([P])
    stats = a.take([C, 6])
    tmp = a.take([3, C])
    mean, ve, rs = a.take([2, C]), a.take([2, C]), a.take([2, C])
    xn = a.take([2, C, D])
    xnT = a.take([2, N])
    xb = a.take([C, D])
    parts = a.take([2, 4, N], F16)
    v = a.take([2, N])

    adj_loaded = [k.sem(f"adj_loaded{i}") for i in range(C)]
    x_loaded = [k.sem(f"x_loaded{b}") for b in range(B)]
    (weights_loaded, consts_ready, bias_made, bias_ready, start_ready, sign_ready, flags_turned, bound_made, edge_made,
     counted, edge_stored, stat_step, xn_done, pow_done, turned, xnT_done, proj_done, high_done, low_done, v_copied,
     xb_done) = [
        k.sem(f"q_{s}") for s in (
            "weights_loaded", "consts_ready", "bias_made", "bias_ready", "start_ready", "sign_ready", "flags_turned",
            "bound_made", "edge_made", "counted", "edge_stored", "stat_step", "xn_done", "pow_done", "turned", "xnT_done",
            "proj_done", "high_done", "low_done", "v_copied", "xb_done")]
    stored = [k.sem(f"q_stored{u}") for u in range(2)]
    xb_stored = k.sem("q_xb_stored")
    STAT_STEPS = C + COMBINE
    xt = tile_rows(t["x"].rearrange("b n f -> (b n) f"))
    adj_t = tile_rows(t["adj"])
    loads = [(k.ident[:], t["ident"]), (k.w0[:], t["L0_gnn_W4"]), (k.bqkv[:], t["L0_gnn_bqkv"]),
             (k.rows3[:], t["L0_gnn_rows"].rearrange("(o r) f -> o r f", o=1).to_broadcast([P, 3, D]))]

    def run(eng, body):
        body(-2, 0, -1, False, False, True)
        body(-1, 1, -1, False, True, True)
        with eng.Fori(0, B // 2 - 1) as pair:
            body(2 * pair, 0, pair, True, True, True)
            body(2 * pair + 1, 1, pair, True, True, True)
        body(B - 2, 0, B // 2 - 1, True, True, False)
        body(B - 1, 1, B // 2 - 1, True, False, False)

    with nc.Block() as block:
        @block.sync
        def _(sp):
            for b in range(B):
                sp.dma_start(k.x[:, b * C:(b + 1) * C, :], xt[:, b * C:(b + 1) * C, :]).then_inc(x_loaded[b], 16)
            for i in range(C):
                sp.dma_start(adj[:, i, :], adj_t[:, i, :]).then_inc(adj_loaded[i], 16)
            for u in range(2):
                sp.sem_inc(stored[u], 32)
            sp.sem_inc(xb_stored, 16)
            with sp.Fori(0, B // 2) as pair:
                for u in range(2):
                    b = 2 * pair + u
                    at = bass.ds(b, 1)
                    sp.wait_ge(low_done, 2 * b + 4)
                    sp.dma_start(scr.parts[at].rearrange("o r p t -> p (o r) t"), parts[:, u]).then_inc(stored[u], 16)
                    sp.wait_ge(v_copied, b + 2)
                    sp.dma_start(scr.v[at].rearrange("o p t -> (o p) t"), v[:, u, :]).then_inc(stored[u], 16)
                    sp.wait_ge(xb_done, b + 3)
                    sp.dma_start(scr.xb[at].rearrange("o p t -> (o p) t"),
                                 xb.rearrange("p c f -> p (c f)")).then_inc(xb_stored, 16)
            sp.wait_ge(edge_made, C)
            sp.dma_start(scr.edge, edge).then_inc(edge_stored, 16)
            sp.wait_ge(edge_stored, 16)
            sp.wait_ge(xb_stored, 16 * (B + 1))
            for u in range(2):
                sp.wait_ge(stored[u], 16 * (B + 2))

        @block.scalar
        def _(act):
            for dst, src in loads:
                act.dma_start(dst, src).then_inc(weights_loaded, 16)
            act.sem_inc(xnT_done, 1)
            act.sem_inc(v_copied, 1)
            act.wait_ge(weights_loaded, 16 * len(loads))

            def body(n, u, pair, products, norm, stats_next):
                if products:
                    act.wait_ge(stored[u], 32 * pair + 32)
                    for j in range(2):
                        act.wait_ge(proj_done, 3 * n + 7 + j)
                        nc.scalar.activation(parts[:, u, 2 * j, :], k.bank2(2 + 2 * j), ACT.Identity,
                                             bias=k.bqkv[:, j:j + 1]).then_inc(high_done, 1)
                if norm:
                    act.wait_ge(turned, n + 1 + 3)
                    act.wait_ge(proj_done, 3 * n + 6)
                    nc.scalar.copy(xnT[:, 1 - u, :], k.bank2(0)).then_inc(xnT_done, 1)
                if products:
                    act.wait_ge(proj_done, 3 * n + 9)
                    nc.scalar.copy(v[:, u, :], k.bank2(6)).then_inc(v_copied, 1)

            run(act, body)

            for i in range(C):
                act.wait_ge(adj_loaded[i], 16)
                nc.scalar.activation(sign[:, i, :], adj[:, i, :], ACT.Sign).then_inc(sign_ready, 1)
            for c in range(C):
                act.wait_ge(flags_turned, c + 1)
                act.wait_ge(bound_made, c + 1)
                nc.scalar.activation(edge[:, c, :], k.ps[:, c % 4, :].bitcast(BF16), ACT.Relu).then_inc(edge_made, 1)

        @block.gpsimd
        def _(pool):
            nc.gpsimd.memset(k.ones[:], 1.0).then_inc(consts_ready, 1)
            nc.gpsimd.memset(ones16, 1.0).then_inc(consts_ready, 1)
            nc.gpsimd.memset(k.minus_half[:], -0.5).then_inc(consts_ready, 1)
            pool.wait_ge(consts_ready, 3)
            pool.sem_inc(xb_done, 2)
            bias = k.wo_bias[:].unsqueeze(1).to_broadcast([P, C, D])

            def body(n, u, pair, products, norm, stats_next):
                if stats_next:
                    pool.wait_ge(stat_step, STAT_STEPS * (n + 2) + STAT_STEPS + 1)
                    nc.gpsimd.tensor_tensor(rs[:, u, :], ve[:, u, :], k.minus_half[:, 0:C], ALU.pow).then_inc(pow_done, 1)
                if norm:
                    b = n + 1
                    if not products:
                        pool.wait_ge(bias_ready, 1)
                    pool.wait_ge(xn_done, C * b + C)
                    pool.wait_ge(xb_stored, 16 * b + 16)
                    nc.gpsimd.tensor_tensor(xb, xn[:, 1 - u], bias, ALU.add).then_inc(xb_done, 1)

            run(pool, body)

        @block.vector
        def _(dve):
            stt, ts = nc.vector.scalar_tensor_tensor, nc.vector.tensor_scalar
            dve.sem_inc(stat_step, 1)
            dve.sem_inc(low_done, 2)
            dve.wait_ge(weights_loaded, 16 * len(loads))
            nc.vector.tensor_copy(k.ident16[:], k.ident[:]).then_inc(start_ready, 1)
            nc.vector.tensor_copy(bv_cols, k.bqkv[:, 2:3].to_broadcast([P, P])).then_inc(start_ready, 1)

            dve.wait_ge(bias_made, 1)
            stt(out=k.wo_bias[:], in0=k.ps[:, 4, 0:D], scalar=float(C), in1=k.rows3[:, 0, :],
                op0=ALU.mult, op1=ALU.add).then_inc(bias_ready, 1)

            def statistics(b, v):
                base = STAT_STEPS * b + 1
                dve.wait_ge(stat_step, base)
                x = rows_of(k, b)
                for i in range(C):
                    nc.vector.bn_stats(stats[:, i, :], x[i]).then_inc(stat_step, 1)
                dve.wait_ge(stat_step, base + C)
                combine_stats(nc, Steps(dve, stat_step, base + C), stats, mean[:, v, :], ve[:, v, :], tmp)

            def normalise(b, v):
                x = rows_of(k, b)
                dve.wait_ge(pow_done, b + 1)
                dve.wait_ge(turned, b + 1)
                dve.wait_ge(xb_done, b + 1)
                for i in range(C):
                    ts(xn[:, v, i, :], x[i], mean[:, v, i:i + 1], rs[:, v, i:i + 1],
                       ALU.subtract, ALU.mult).then_inc(xn_done, 1)

            def body(n, u, pair, products, norm, stats_next):
                if norm:
                    normalise(n + 1, 1 - u)
                if stats_next:
                    if not products:
                        dve.wait_ge(x_loaded[n + 2], 16)
                    statistics(n + 2, u)
                if norm and not products:
                    for b in range(2, B):
                        dve.wait_ge(x_loaded[b], 16)
                if products:
                    for j in range(2):
                        dve.wait_ge(high_done, 2 * n + j + 1)
                        stt(out=parts[:, u, 2 * j + 1, :], in0=k.bank2(2 + 2 * j), scalar=k.bqkv[:, j:j + 1],
                            in1=parts[:, u, 2 * j, :], op0=ALU.add, op1=ALU.subtract).then_inc(low_done, 1)

            run(dve, body)

            for c in range(C):
                dve.wait_ge(flags_turned, c + 1)
                ts(k.bound[:, c, :], k.ps[:, c % 4, :].bitcast(BF16), 0.0, E_HI, ALU.not_equal, ALU.mult).then_inc(bound_made, 1)
            for c in range(C):
                dve.wait_ge(bound_made, c + 1)
                ts(k.bound[:, c, :], k.bound[:, c, :], E_LO, None, ALU.max)
            dve.wait_ge(counted, 1)
            ts(k.lone[:], k.bank2(6), 0.0, None, ALU.is_equal)

        @block.tensor
        def _(pe):
            pe.sem_inc(turned, 2)
            pe.sem_inc(proj_done, 6)
            pe.wait_ge(start_ready, 2)
            nc.tensor.matmul(k.ps[:, 4, 0:D], bv_cols, k.w0[:, 3, :], start=True, stop=True).then_inc(bias_made, 1)
            pe.wait_ge(bias_ready, 1)

            def body(n, u, pair, products, norm, stats_next):
                if products:
                    pe.wait_ge(xnT_done, n + 2)
                    for j in range(2):
                        pe.wait_ge(low_done, 2 * n + j + 1)
                        for half in range(2):
                            last = nc.tensor.matmul(k.ps[:, 2 + 2 * j + half, :], k.w0[:, j, :],
                                                    halves(xnT[:, u, :])[half], start=True, stop=True)
                        last.then_inc(proj_done, 1)
                if norm:
                    turn(n + 1, 1 - u)
                if products:
                    pe.wait_ge(v_copied, n + 1)
                    for i in range(C):
                        last = nc.tensor.matmul(k.bank2(6)[:, i * P:(i + 1) * P], xnT[:, u, i * P:(i + 1) * P],
                                                k.w0[:, 2, :], start=True, stop=True)
                    last.then_inc(proj_done, 1)

            def turn(b, v):
                pe.wait_ge(xn_done, C * b + C)
                pe.wait_ge(xnT_done, b + 1)
                for i in range(C):
                    last = nc.tensor.transpose(k.bank2(0)[:, i * P:(i + 1) * P], xn[:, v, i, :], k.ident[:])
                last.then_inc(turned, 1)

            run(pe, body)

            pe.wait_ge(sign_ready, C)
            pe.wait_ge(v_copied, B + 1)
            pe.wait_ge(low_done, 2 * B + 2)
            for c in range(C):
                if c >= 4:
                    pe.wait_ge(edge_made, c - 3)
                flags = k.ps[:, c % 4, :].bitcast(BF16)
                for i in range(C):
                    last = nc.tensor.transpose(flags[:, i * P:(i + 1) * P], sign[:, i, c * P:(c + 1) * P], k.ident16[:])
                last.then_inc(flags_turned, 1)
            pe.wait_ge(edge_made, C)
            for half in range(2):
                for c in range(C):
                    last = nc.tensor.matmul(k.ps[:, 6 + half, :], ones16, edge[:, c, half * 512:(half + 1) * 512],
                                            start=(c == 0), stop=(c == C - 1))
            last.then_inc(counted, 1)


def rows_of(k, b):
    return [k.x[:, bass.ds(b * C + i, 1), :].rearrange("p o f -> p (o f)") for i in range(C)]


class Peeled:

    @staticmethod
    def run(eng, body, last):
        body(0, 0, 0)
        with eng.Fori(0, (B - 2) // 2) as pair:
            body(2 * pair + 1, 1, pair)
            body(2 * pair + 2, 0, pair + 1)
        body(B - 1, (B - 1) % 2, (B - 1) // 2)
        last()

    @staticmethod
    def back(b, u, c, lag):
        if c >= lag:
            return b, u, c - lag
        return None if is_first(b) else (b - 1, 1 - u, c - lag + C)

    @staticmethod
    def tail(lag):
        return [(B - 1, (B - 1) % 2, c) for c in range(C - lag, C)]


def is_first(b):
    return isinstance(b, int) and b == 0


def attention0(k, scr, experts_next):
    nc = k.nc
    a = Arena(k)
    qs = a.take([2, H, N], F16)
    ks = a.take([2, H, N], F16)
    v = a.take([2, N])
    xb = a.take([N])
    e = a.take([H, N])
    pm = a.take([8, N])
    ctx = a.take([4, N])
    den = a.take([N])
    r_in = a.take([HS])
    r_out = a.take([HS])
    r_rows = a.take([2, N])
    ctx_sum = a.take([2, N])
    y = a.take([C, D])
    stats = a.take([C, 6])
    mean = a.take([C])
    tmp = a.take([3, C])
    ve = a.take([C])
    rs = a.take([C])

    loaded = [k.sem(f"a_loaded{u}") for u in range(2)]
    (score_done, exp_done, clip_done, pv_done, copied, recip_done, summed, o_done, den_stored, den_loaded,
     rec_stored, rec_loaded, xb_loaded, y_added, y_done, pow_done, res_done) = [
        k.sem(f"a_{s}") for s in ("score_done", "exp_done", "clip_done", "pv_done", "copied", "recip_done", "summed",
                                  "o_done", "den_stored", "den_loaded", "rec_stored", "rec_loaded", "xb_loaded",
                                  "y_added", "y_done", "pow_done", "res_done")]
    LOADS = 4 + 4 + 1
    RECIP_LAG = 2
    PROJECT_AT = 5
    VAR = C + COMBINE
    Y_STEPS = VAR + C
    back, tail = Peeled.back, Peeled.tail

    gamma, beta = [w.unsqueeze(1).to_broadcast([P, C, D]) for w in (k.gamma, k.beta)]

    def residual(ops, eng, b):
        eng.wait_ge(y_done, Y_STEPS * b + Y_STEPS)
        ops.tensor_tensor(y[:, :, :], y[:, :, :], gamma, ALU.mult).then_inc(res_done, 1)
        eng.wait_ge(res_done, 3 * b + 4)
        ops.tensor_tensor(y[:, :, :], y[:, :, :], beta, ALU.add).then_inc(res_done, 1)
        eng.wait_ge(res_done, 3 * b + 5)
        x = k.x[:, bass.ds(b * C, C), :]
        ops.tensor_tensor(x, x, y[:, :, :], ALU.add).then_inc(res_done, 1)

    with nc.Block() as block:
        @block.sync
        def _(sp):
            sp.sem_inc(den_stored, 16)

            def load(b, u, r):
                at = bass.ds(b, 1)
                if r == H:
                    sp.dma_start(v[:, u, :], scr.v[at].rearrange("o p t -> (o p) t")).then_inc(loaded[u], 16)
                    return
                for dst, j in ((qs, r // 2), (ks, 2 + r % 2)):
                    sp.dma_start(dst[r * HS:(r + 1) * HS, u, :, :],
                                 scr.parts[at, j].rearrange("o (h d) t -> d (o h) t", h=H)).then_inc(loaded[u], 16)

            def store_den(b, u, c):
                g = C * b + c
                sp.wait_ge(copied, 2 * g + 3)
                sp.dma_start(scr.den[c % 2], den[0:P:HS, :]).then_inc(den_stored, 16)

            def load_den(b, u, c):
                g = C * b + c
                sp.wait_ge(den_stored, 16 * g + 32)
                sp.dma_start(r_in[:], scr.den[c % 2].rearrange("h (a t) -> (h a) t", t=HS)).then_inc(den_loaded, 16)

            def store_rec(b, u, c):
                g = C * b + c
                sp.wait_ge(recip_done, g + 1)
                sp.dma_start(scr.rec[c % 2].rearrange("h (a t) -> (h a) t", t=HS), r_out[:]).then_inc(rec_stored, 16)

            def load_rec(b, u, c):
                g = C * b + c
                sp.wait_ge(rec_stored, 16 * g + 16)
                for h in range(H):
                    sp.dma_start(r_rows[h * HS:(h + 1) * HS, c % 2, :],
                                 scr.rec[c % 2, h:h + 1, :].to_broadcast([HS, N])).then_inc(rec_loaded, 16)

            def round_trip(g, before):
                if g:
                    store_den(*g)
                if before:
                    store_rec(*before)
                if g:
                    load_den(*g)
                if before:
                    load_rec(*before)

            def body(b, u, _):
                if is_first(b):
                    for u_next in range(2):
                        for r in range(H + 1):
                            load(u_next, u_next, r)
                for c in range(C):
                    round_trip(back(b, u, c, 1), back(b, u, c, 2))
                    if 1 <= c <= H + 1 and not isinstance(b, int):
                        if c == 1:
                            sp.wait_ge(pv_done, 2 * C * b + 4)
                        load(b + 1, 1 - u, c - 1)
                    if c == 1 and not is_first(b):
                        sp.wait_ge(y_added, b)
                        sp.dma_start(xb[:, :], scr.xb[bass.ds(b - 1, 1)].rearrange("o p t -> (o p) t")).then_inc(xb_loaded, 16)

            def last():
                g6, g7 = tail(2)
                round_trip(g7, g6)
                round_trip(None, g7)
                sp.wait_ge(y_added, B)
                sp.dma_start(xb[:, :], scr.xb[B - 1]).then_inc(xb_loaded, 16)
                sp.wait_ge(pv_done, 2 * C * B + 4)
                experts_next.load(sp)

            Peeled.run(sp, body, last)

        @block.tensor
        def _(pe):
            pe.sem_inc(o_done, 2)
            pe.sem_inc(pv_done, 4)

            def scores(b, u, half_b, c, h):
                if c == 0 and h == 0:
                    pe.wait_ge(loaded[u], 16 * LOADS * (half_b + 1))
                pe.wait_ge(exp_done, 4 * (C * b + c) + h + 1)
                for half in range(2):
                    last = nc.tensor.matmul(k.ps[:, 6 * (h % 2) + half, :], ks[:, u, h, c * P:(c + 1) * P],
                                            halves(qs[:, u, h, :])[half], start=True, stop=True)
                last.then_inc(score_done, 1)

            def values(b, u, c, part):
                g = C * b + c
                pe.wait_ge(copied, 2 * g + 1 + part)
                if part == 1 and c == PROJECT_AT - 1 and not is_first(b):
                    pe.wait_ge(y_added, b + 1)
                if part == 0:
                    pe.wait_ge(clip_done, 4 * g + 8)
                for half in range(2):
                    for h in range(H):
                        lhsT = k.ones[:] if part == 0 else v[:, u, c * P + h * HS:c * P + (h + 1) * HS]
                        last = nc.tensor.matmul(
                            k.ps[h * HS:(h + 1) * HS, 4 - 2 * part + half, :], lhsT,
                            halves(pm[:, 4 * (c % 2) + h, :])[half], start=True, stop=True)
                last.then_inc(pv_done, 1)

            def project(b, u):
                pe.wait_ge(summed, 2 * C * b + 2 * C + 8)
                for i in range(C):
                    last = nc.tensor.matmul(k.bank2(2)[:, i * P:(i + 1) * P], ctx_sum[:, u, i * P:(i + 1) * P],
                                            k.w0[:, 3, :], start=True, stop=True)
                last.then_inc(o_done, 1)

            def body(b, u, half_b):
                for c in range(C):
                    scores(b, u, half_b, c, 0)
                    scores(b, u, half_b, c, 1)
                    if g := back(b, u, c, 1):
                        values(*g, 0)
                    if c == PROJECT_AT and not is_first(b):
                        pe.wait_ge(copied, 2 * C * b + 2 * PROJECT_AT)
                        project(b - 1, 1 - u)
                    scores(b, u, half_b, c, 2)
                    scores(b, u, half_b, c, 3)
                    if g := back(b, u, c, 1):
                        values(*g, 1)

            def last():
                for part in range(2):
                    values(*tail(1)[0], part)
                pe.wait_ge(copied, 2 * C * B + 2)
                project(B - 1, (B - 1) % 2)

            Peeled.run(pe, body, last)

        @block.scalar
        def _(act):
            act.sem_inc(exp_done, 2)
            act.sem_inc(copied, 2)

            def copy_den(b, u, c):
                g = C * b + c
                act.wait_ge(pv_done, 2 * g + 5)
                act.wait_ge(den_stored, 16 * g + 16)
                nc.scalar.copy(den[:, :], k.bank2(4)).then_inc(copied, 1)

            def copy_ctx(b, u, c):
                g = C * b + c
                act.wait_ge(pv_done, 2 * g + 6)
                act.wait_ge(summed, 2 * g + 2)
                nc.scalar.copy(ctx[:, c % 4, :], k.bank2(2)).then_inc(copied, 1)

            def body(b, u, _):
                for c in range(C):
                    for h in range(H):
                        if h == 2 and (g := back(b, u, c, 2)):
                            copy_ctx(*g)
                        at = 4 * (C * b + c) + h
                        act.wait_ge(clip_done, at + 1)
                        act.wait_ge(score_done, at + 1)
                        nc.scalar.activation(e[:, h, :], k.bank2(6 * (h % 2)), ACT.Exp, scale=SCALE).then_inc(exp_done, 1)
                    if g := back(b, u, c, 1):
                        copy_den(*g)

            def last():
                g6, g7 = tail(2)
                copy_ctx(*g6)
                copy_den(*g7)
                copy_ctx(*g7)

            Peeled.run(act, body, last)

        @block.vector
        def _(dve):
            dve.sem_inc(clip_done, 4)
            dve.sem_inc(y_added, 1)

            def clip(b, u, c, h):
                if h == 0:
                    dve.wait_ge(pv_done, 2 * (C * b + c) + 2)
                dve.wait_ge(exp_done, 4 * (C * b + c) + h + 3)
                nc.vector.scalar_tensor_tensor(out=pm[:, 4 * (c % 2) + h, :], in0=e[:, h, :], scalar=E_LO,
                                               in1=k.bound[:, c, :], op0=ALU.max, op1=ALU.min).then_inc(clip_done, 1)

            def reciprocal(b, u, c):
                dve.wait_ge(summed, 2 * (C * b + c) + 5)
                dve.wait_ge(den_loaded, 16 * (C * b + c) + 16)
                nc.vector.reciprocal(r_out[:], r_in[:]).then_inc(recip_done, 1)

            def add(b):
                dve.wait_ge(xb_loaded, 16 * b + 16)
                dve.wait_ge(res_done, 3 * b + 3)
                dve.wait_ge(o_done, b + 3)
                nc.vector.tensor_tensor(y[:, :, :].rearrange("p c f -> p (c f)"), k.bank2(2), xb[:, :],
                                        ALU.add).then_inc(y_added, 1)

            def statistics(b, h):
                if h == 0:
                    dve.wait_ge(y_added, b + 2)
                for i in range(2 * h, 2 * h + 2):
                    nc.vector.bn_stats(stats[:, i, :], y[:, i, :]).then_inc(y_done, 1)
                if h == H - 1:
                    dve.wait_ge(y_done, Y_STEPS * b + C)
                    combine_stats(nc, Steps(dve, y_done, Y_STEPS * b + C), stats, mean, ve, tmp)

            def normalise(b, h):
                if h == 0:
                    dve.wait_ge(pow_done, b + 1)
                for i in range(2 * h, 2 * h + 2):
                    nc.vector.tensor_scalar(y[:, i, :], y[:, i, :], mean[:, i:i + 1], rs[:, i:i + 1],
                                            ALU.subtract, ALU.mult).then_inc(y_done, 1)

            def body(b, u, _):
                for c in range(C):
                    for h in range(H):
                        clip(b, u, c, h)
                        if h == 2 and (g := back(b, u, c, RECIP_LAG)):
                            reciprocal(*g)
                        if not is_first(b):
                            if c == PROJECT_AT and h == 1:
                                add(b - 1)
                            if c == PROJECT_AT + 1:
                                statistics(b - 1, h)
                            if c == PROJECT_AT + 2:
                                normalise(b - 1, h)

            def last():
                for g in tail(RECIP_LAG):
                    reciprocal(*g)
                add(B - 1)
                for h in range(H):
                    statistics(B - 1, h)
                for h in range(H):
                    normalise(B - 1, h)
                residual(nc.vector, dve, B - 1)

            Peeled.run(dve, body, last)

        @block.gpsimd
        def _(pool):
            pool.sem_inc(summed, 8)
            pool.sem_inc(res_done, 3)

            def quotient(b, u, c):
                g = C * b + c
                pool.wait_ge(rec_loaded, 64 * g + 64)
                pool.wait_ge(copied, 2 * g + 4)
                if c == 0:
                    pool.wait_ge(o_done, b + 1)
                    nc.gpsimd.tensor_tensor(ctx_sum[:, u, :], ctx[:, 0, :], r_rows[:, 0, :], ALU.mult).then_inc(summed, 2)
                    return
                nc.gpsimd.tensor_tensor(ctx[:, c % 4, :], ctx[:, c % 4, :], r_rows[:, c % 2, :], ALU.mult).then_inc(summed, 1)
                pool.wait_ge(summed, 2 * g + 9)
                nc.gpsimd.tensor_tensor(ctx_sum[:, u, :], ctx_sum[:, u, :], ctx[:, c % 4, :], ALU.add).then_inc(summed, 1)

            def power(b):
                pool.wait_ge(y_done, Y_STEPS * b + VAR)
                nc.gpsimd.tensor_tensor(rs[:], ve[:], k.minus_half[:, 0:C], ALU.pow).then_inc(pow_done, 1)

            def body(b, u, _):
                for c in range(C):
                    quotient(b, u, c)
                    if c == 2 and not is_first(b):
                        power(b - 1)
                    if c == 4 and not is_first(b):
                        residual(nc.gpsimd, pool, b - 1)

            def last():
                power(B - 1)

            Peeled.run(pool, body, last)


class Attention1Buffers:

    def __init__(self, k, scr):
        self.scr = scr
        a = Arena(k)
        self.pm = a.take([8, N])
        self.ctx, self.den, self.r_rows, self.low, self.lone32 = [a.take([N]) for _ in range(5)]
        self.r_in, self.r_out = a.take([HS]), a.take([HS])
        self.tens = a.take([P], BF16)
        self.begin = a.at
        self.rows = a.take([2, H, N])
        self.v = a.take([2, N])
        self.fb = a.take([2, N])
        self.small = a.take([2, C * H + D])
        self.edge = k.bound[:, 0:C // 2, :].bitcast(BF16).rearrange("p a n -> p (a n)").rearrange("p (c n) -> p c n", c=C)
        self.edge_loaded = k.sem("h_edge_loaded")
        self.loaded = [k.sem(f"h_loaded{u}") for u in range(2)]

    LOADS = 4

    def load_edge(self, sp):
        sp.dma_start(self.edge, self.scr.edge).then_inc(self.edge_loaded, 16)

    def load(self, sp, b, u):
        scr, at, loaded = self.scr, bass.ds(b, 1), self.loaded[u]
        sp.dma_start(self.rows[:, u, :, :].rearrange("p h n -> p (h n)"),
                     scr.grow[at].to_broadcast([P, H * N])).then_inc(loaded, 16)
        sp.dma_start(self.v[:, u, :], scr.gv[at, 0].rearrange("o p n -> (o p) n")).then_inc(loaded, 16)
        sp.dma_start(self.fb[:, u, :], scr.gv[at, 1].rearrange("o p n -> (o p) n")).then_inc(loaded, 16)
        sp.dma_start(self.small[:, u, :], scr.gs[at].rearrange("o p n -> (o p) n")).then_inc(loaded, 16)


def gat_factors(k, scr, buffers):
    nc, t = k.nc, k.t
    a = Arena(k)
    stats = a.take([C, 6])
    tmp = a.take([3, C])
    mean, ve, rs = a.take([2, C]), a.take([2, C]), a.take([2, C])
    xn = a.take([2, C, D])
    xnT = a.take([2, N])
    wide = a.take([D + 2 * H])
    prod = a.take([2, D])
    a12 = a.take([2, D])
    e = a.take([C, 3 * H])
    top = a.take([2 * H])
    tops = a.take([2 * H])
    u8 = a.take([C, 2 * H])
    spread = a.take([H])
    r1 = a.take([C, H])
    f = a.take([2, C * H])
    r = a.take([H, C])
    rT = a.take([2, P])
    xsum = a.take([1])
    small = a.take([2, C * H + D])
    v = a.take([2, N])
    fb = a.take([2, N])
    assert a.at <= buffers.begin

    (w_loaded, w_ready, stat_step, pow_done, xn_done, turned, xnT_done, e_made, wh_done, step, top_seen, reduced, exp_done, v_done,
     r_turned, r_copied, fb_done) = [
        k.sem(f"g_{s}") for s in (
            "w_loaded", "w_ready", "stat_step", "pow_done", "xn_done", "turned", "xnT_done", "e_made", "wh_done", "step", "top_seen",
            "reduced", "exp_done", "v_done", "r_turned", "r_copied", "fb_done")]
    stored = [k.sem(f"g_stored{u}") for u in range(2)]
    STORES = 4
    STAT_STEPS = C + COMBINE
    E_READY, U_READY, R_READY = 4, 6, 9
    STEPS = 11
    E_BANK, R_BANK = 6, 7

    def run(eng, body):
        body(-2, 0, -1, False, False, True)
        body(-1, 1, -1, False, True, True)
        with eng.Fori(0, B // 2 - 1) as pair:
            body(2 * pair, 0, pair, True, True, True)
            body(2 * pair + 1, 1, pair, True, True, True)
        body(B - 2, 0, B // 2 - 1, True, True, False)
        body(B - 1, 1, B // 2 - 1, True, False, False)

    with nc.Block() as block:
        @block.sync
        def _(sp):
            for u in range(2):
                sp.sem_inc(stored[u], 16 * STORES)
            sp.dma_start(wide[:, 0:D], t["L1_gnn_Wc"]).then_inc(w_loaded, 16)
            for i in range(2):
                sp.dma_start(a12[:, i, :].rearrange("p (h d) -> p h d", h=H),
                             t["L1_gnn_a"][:, HS * (1 - i):HS * (2 - i)].rearrange("(o h) d -> o h d", o=1)
                             .to_broadcast([P, H, HS])).then_inc(w_loaded, 16)
            buffers.load_edge(sp)

            def store(b, u):
                at = bass.ds(b, 1)
                sp.wait_ge(v_done, b + 3)
                sp.dma_start(scr.gv[at, 0].rearrange("o p n -> (o p) n"), v[:, u, :]).then_inc(stored[u], 16)
                sp.wait_ge(fb_done, b + 1)
                sp.dma_start(scr.gv[at, 1].rearrange("o p n -> (o p) n"), fb[:, u, :]).then_inc(stored[u], 16)
                sp.wait_ge(r_copied, b + 2)
                sp.dma_start(scr.gs[at].rearrange("o p n -> (o p) n"), small[:, u, :]).then_inc(stored[u], 16)
                sp.dma_start(scr.grow[at].rearrange("o (q t) -> (o q) t", t=P), rT[0:C * H, u, :]).then_inc(stored[u], 16)

            with sp.Fori(0, B // 2 - 1) as pair:
                for u in range(2):
                    store(2 * pair + u, u)
            for u in range(2):
                sp.wait_ge(stored[u], 16 * STORES * (B // 2))
                buffers.load(sp, u, u)
            for u in range(2):
                store(B - 2 + u, u)
            for u in range(2):
                sp.wait_ge(stored[u], 16 * STORES * (B // 2 + 1))

        @block.tensor
        def _(pe):
            pe.sem_inc(turned, 2)
            pe.sem_inc(wh_done, 2)
            pe.wait_ge(w_ready, 4)

            def body(n, u, pair, products, norm, stats_next):
                if products:
                    pe.wait_ge(xnT_done, n + 2)
                    pe.wait_ge(step, STEPS * n + 3)
                    for i in range(C):
                        last = nc.tensor.matmul(k.ps[:, E_BANK, i * 2 * H:(i + 1) * 2 * H], xnT[:, u, i * P:(i + 1) * P],
                                                wide[:, D:D + 2 * H], start=True, stop=True)
                    last.then_inc(e_made, 1)
                    pe.wait_ge(v_done, n + 1)
                    for i in range(C):
                        last = nc.tensor.matmul(k.bank2(2 * u)[:, i * P:(i + 1) * P], xnT[:, u, i * P:(i + 1) * P],
                                                wide[:, 0:D], start=True, stop=True)
                    last.then_inc(wh_done, 1)
                if norm:
                    b = n + 1
                    pe.wait_ge(xn_done, C * b + C)
                    pe.wait_ge(xnT_done, b + 1)
                    for i in range(C):
                        last = nc.tensor.transpose(k.bank2(4)[:, i * P:(i + 1) * P], xn[:, 1 - u, i, :], k.ident[:])
                    last.then_inc(turned, 1)
                if products:
                    pe.wait_ge(exp_done, 3 * n + 3)
                    pe.wait_ge(r_copied, n + 1)
                    nc.tensor.transpose(k.ps[0:C * H, R_BANK, 0:P],
                                        r.rearrange("p h c -> p (h c)"), k.ident[:]).then_inc(r_turned, 1)

            run(pe, body)

        @block.vector
        def _(dve):
            tt, ts, stt, red = (nc.vector.tensor_tensor, nc.vector.tensor_scalar, nc.vector.scalar_tensor_tensor,
                                nc.vector.tensor_reduce)
            dve.sem_inc(v_done, 2)
            dve.sem_inc(stat_step, 1)
            dve.sem_inc(step, STEPS)
            dve.wait_ge(w_loaded, 48)
            for i in range(2):
                tt(prod[:, i, :], wide[:, 0:D], a12[:, i, :], ALU.mult).then_inc(w_ready, 1)
            for i in range(2):
                dve.wait_ge(w_ready, i + 1)
                red(wide[:, D + i * H:D + (i + 1) * H], prod[:, i, :].rearrange("p (h d) -> p h d", h=H),
                    AX.X, ALU.add).then_inc(w_ready, 1)

            def body(n, u, pair, products, norm, stats_next):
                s = Steps(dve, step, STEPS * n + STEPS)
                if norm:
                    b, v1 = n + 1, 1 - u
                    x = rows_of(k, b)
                    dve.wait_ge(pow_done, b + 1)
                    dve.wait_ge(turned, b + 1)
                    for i in range(C):
                        ts(xn[:, v1, i, :], x[i], mean[:, v1, i:i + 1], rs[:, v1, i:i + 1],
                           ALU.subtract, ALU.mult).then_inc(xn_done, 1)
                if products:
                    ps_e = k.ps[:, E_BANK, 0:2 * H * C].rearrange("p (c q) -> p c q", q=2 * H)
                    dve.wait_ge(e_made, n + 1)
                    dve.wait_ge(r_copied, n + 1)
                    s.did(nc.vector.tensor_copy(e[:, :, 0:H], ps_e[:, :, 0:H]))
                    s.did(nc.vector.tensor_copy(e[:, :, 2 * H:3 * H], ps_e[:, :, H:2 * H]))
                    s.did(ts(e[:, :, H:2 * H], ps_e[:, :, 0:H], -1.0, None, ALU.mult))
                    s.wait()
                    s.did(red(top, e[:, :, 0:2 * H].rearrange("p c q -> p q c"), AX.X, ALU.max))
                    assert s.n == E_READY
                if stats_next:
                    b = n + 2
                    base = STAT_STEPS * b + 1
                    x = rows_of(k, b)
                    dve.wait_ge(stat_step, base)
                    for i in range(C):
                        nc.vector.bn_stats(stats[:, i, :], x[i]).then_inc(stat_step, 1)
                    dve.wait_ge(stat_step, base + C)
                    combine_stats(nc, Steps(dve, stat_step, base + C), stats, mean[:, u, :], ve[:, u, :], tmp)
                if products:
                    dve.wait_ge(reduced, n + 1)
                    s.did(tt(u8, e[:, :, 0:2 * H], tops.unsqueeze(1).to_broadcast([P, C, 2 * H]), ALU.subtract))
                    s.did(tt(spread, tops[:, 0:H], tops[:, H:2 * H], ALU.add))
                    assert s.n == U_READY
                    s.did(tt(r1, e[:, :, 2 * H:3 * H], tops[:, 0:H].unsqueeze(1).to_broadcast([P, C, H]), ALU.add))
                    s.wait()
                    s.did(stt(out=r1, in0=r1, scalar=0.0, in1=spread.unsqueeze(1).to_broadcast([P, C, H]),
                              op0=ALU.max, op1=ALU.subtract))
                    s.wait()
                    s.did(ts(r1, r1, 0.0, None, ALU.min))
                    assert s.n == R_READY
                    dve.wait_ge(stored[u], 16 * STORES * (pair + 1))
                    s.did(red(xsum, xnT[:, u, :], AX.X, ALU.add))
                    s.wait()
                    s.did(ts(small[:, u, C * H:C * H + D], wide[:, 0:D], xsum[:, 0:1], None, ALU.mult))
                    assert s.n == STEPS
                    dve.wait_ge(wh_done, n + 3)
                    dve.wait_ge(exp_done, 3 * n + 1)
                    tt(v[:, u, :].rearrange("p (c h d) -> p c h d", c=C, h=H),
                       k.bank2(2 * u).rearrange("p (c h d) -> p c h d", c=C, h=H),
                       f[:, u, :].rearrange("p (c h) -> p c h", h=H).unsqueeze(3).to_broadcast([P, C, H, HS]),
                       ALU.mult).then_inc(v_done, 1)

            run(dve, body)

        @block.gpsimd
        def _(pool):
            def body(n, u, pair, products, norm, stats_next):
                if products:
                    pool.wait_ge(step, STEPS * n + STEPS + E_READY)
                    pool.sem_inc(top_seen, 1)
                    nc.gpsimd.partition_all_reduce(tops, top, P, bass.bass_isa.ReduceOp.max).then_inc(reduced, 1)
                if stats_next:
                    pool.wait_ge(stat_step, STAT_STEPS * (n + 2) + STAT_STEPS + 1)
                    nc.gpsimd.tensor_tensor(rs[:, u, :], ve[:, u, :], k.minus_half[:, 0:C], ALU.pow).then_inc(pow_done, 1)

            run(pool, body)

        @block.scalar
        def _(act):
            act.sem_inc(xnT_done, 1)
            act.sem_inc(r_copied, 1)

            def body(n, u, pair, products, norm, stats_next):
                if products:
                    c_h = lambda ap: ap.rearrange("p (c h) -> p c h", h=H)
                    act.wait_ge(stored[u], 16 * STORES * (pair + 1))
                    act.wait_ge(step, STEPS * n + STEPS + U_READY)
                    nc.scalar.activation(c_h(f[:, u, :]), u8[:, :, 0:H], ACT.Exp).then_inc(exp_done, 1)
                    nc.scalar.activation(c_h(small[:, u, 0:C * H]), u8[:, :, H:2 * H], ACT.Exp,
                                         scale=1.0 - SLOPE).then_inc(exp_done, 1)
                    act.wait_ge(step, STEPS * n + STEPS + R_READY)
                    nc.scalar.activation(r.rearrange("p h c -> p c h"), r1, ACT.Exp, scale=1.0 - SLOPE).then_inc(exp_done, 1)
                if norm:
                    act.wait_ge(turned, n + 1 + 3)
                    act.wait_ge(wh_done, n + 2)
                    if products:
                        act.wait_ge(step, STEPS * n + STEPS)
                    nc.scalar.copy(xnT[:, 1 - u, :], k.bank2(4)).then_inc(xnT_done, 1)
                if products:
                    act.wait_ge(exp_done, 3 * n + 1)
                    nc.scalar.copy(fb[:, u, :].rearrange("p (q d) -> p q d", d=HS),
                                   f[:, u, :].unsqueeze(2).to_broadcast([P, C * H, HS])).then_inc(fb_done, 1)
                    act.wait_ge(step, STEPS * n + 2 * STEPS)
                    act.wait_ge(r_turned, n + 1)
                    nc.scalar.copy(rT[0:C * H, u, :], k.ps[0:C * H, R_BANK, 0:P]).then_inc(r_copied, 1)

            run(act, body)


def attention1(k, scr, buffers, experts_next):
    nc = k.nc
    pm, ctx, den, r_rows, low, lone32 = buffers.pm, buffers.ctx, buffers.den, buffers.r_rows, buffers.low, buffers.lone32
    r_in, r_out, tens = buffers.r_in, buffers.r_out, buffers.tens
    rows, v, fb, small, edge = buffers.rows, buffers.v, buffers.fb, buffers.small, buffers.edge
    edge_loaded, loaded, LOADS = buffers.edge_loaded, buffers.loaded, buffers.LOADS

    tens_ready, masked = k.sem("h_tens_ready"), k.sem("h_masked")
    (w_done, pv_done, copied, recip_done, quot_done, low_done, exp_done, elu_done, turned, added,
     den_stored, den_loaded, rec_stored, rec_loaded) = [
        k.sem(f"h_{s}") for s in ("w_done", "pv_done", "copied", "recip_done", "quot_done", "low_done", "exp_done",
                                  "elu_done", "turned", "added", "den_stored", "den_loaded", "rec_stored", "rec_loaded")]
    U_LAST = (B - 1) % 2
    BY_POOL = H - 1
    RECIP_AT, QUOT_AT, ELU_AT, ADD_AT = 3, 5, 6, 7

    with nc.Block() as block:
        @block.sync
        def _(sp):
            sp.sem_inc(den_stored, 16)
            def reciprocals(b, u):
                sp.wait_ge(copied, 2 * b + 1)
                sp.dma_start(scr.gden[u], den[0:P:HS, :]).then_inc(den_stored, 16)
                sp.wait_ge(den_stored, 16 * b + 32)
                sp.dma_start(r_in[:], scr.gden[u].rearrange("h (a t) -> (h a) t", t=HS)).then_inc(den_loaded, 16)
                sp.wait_ge(recip_done, b + 1)
                sp.dma_start(scr.grec[u].rearrange("h (a t) -> (h a) t", t=HS), r_out[:]).then_inc(rec_stored, 16)
                sp.wait_ge(rec_stored, 16 * b + 16)
                for h in range(H):
                    sp.dma_start(r_rows[h * HS:(h + 1) * HS, :],
                                 scr.grec[u, h:h + 1, :].to_broadcast([HS, N])).then_inc(rec_loaded, 16)

            def body(b, u, _):
                if is_first(b):
                    return
                if not isinstance(b, int):
                    sp.wait_ge(pv_done, C * b + 2)
                    buffers.load(sp, b + 1, 1 - u)
                reciprocals(b - 1, 1 - u)

            def last():
                reciprocals(B - 1, U_LAST)
                sp.wait_ge(pv_done, C * B + 2)
                experts_next.load(sp)

            Peeled.run(sp, body, last)

        @block.gpsimd
        def _(pool):
            nc.gpsimd.tensor_copy(lone32, k.lone[:])
            nc.gpsimd.memset(tens, float(C)).then_inc(tens_ready, 1)
            pool.wait_ge(tens_ready, 1)
            pool.wait_ge(edge_loaded, 16)

            def quotient(b):
                pool.wait_ge(copied, 2 * b + 2)
                pool.wait_ge(rec_loaded, 64 * b + 64)
                nc.gpsimd.tensor_tensor(ctx[:], ctx[:], r_rows[:], ALU.mult).then_inc(quot_done, 1)

            def body(b, u, _):
                for c in range(C):
                    pool.wait_ge(w_done, 4 * (C * b + c) + 1)
                    w = pm[:, 4 * (c % 2) + BY_POOL, :]
                    nc.gpsimd.tensor_tensor(w, w, edge[:, c, :], ALU.mult).then_inc(masked, 1)
                    if c == QUOT_AT and not is_first(b):
                        quotient(b - 1)

            Peeled.run(pool, body, lambda: quotient(B - 1))

        @block.tensor
        def _(pe):
            pe.sem_inc(pv_done, 2)
            pe.sem_inc(turned, 1)
            pe.wait_ge(tens_ready, 1)

            def values(b, u, half_b, c):
                if c == 0:
                    pe.wait_ge(loaded[u], 16 * LOADS * (half_b + 1))
                    pe.wait_ge(added, b + 1)
                    for half in range(2):
                        nc.tensor.matmul(k.ps[:, 4 * u + half, :], small[:, u, C * H:C * H + D], halves(lone32)[half],
                                         start=True, stop=False, skip_group_check=True)
                        nc.tensor.matmul(k.ps[:, 4 * u + 2 + half, :], tens, halves(k.lone[:])[half],
                                         start=True, stop=False, skip_group_check=True)
                pe.wait_ge(w_done, 4 * (C * b + c) + 4)
                pe.wait_ge(masked, C * b + c + 1)
                for half in range(2):
                    for bank, w in ((0, v), (2, fb)):
                        for h in range(H):
                            last = nc.tensor.matmul(
                                k.ps[h * HS:(h + 1) * HS, 4 * u + bank + half, :],
                                w[:, u, c * P + h * HS:c * P + (h + 1) * HS], halves(pm[:, 4 * (c % 2) + h, :])[half],
                                start=False, stop=(c == C - 1), skip_group_check=True)
                last.then_inc(pv_done, 1)

            def turn(b, u):
                pe.wait_ge(elu_done, b + 2)
                for i in range(C):
                    last = nc.tensor.transpose(k.bank2(4 * u)[:, i * P:(i + 1) * P], ctx[:, i * P:(i + 1) * P], k.ident[:])
                last.then_inc(turned, 1)

            def body(b, u, half_b):
                for c in range(C):
                    values(b, u, half_b, c)
                    if c == ELU_AT and not is_first(b):
                        turn(b - 1, 1 - u)

            Peeled.run(pe, body, lambda: turn(B - 1, U_LAST))

        @block.vector
        def _(dve):
            dve.sem_inc(added, 2)
            dve.sem_inc(elu_done, 1)
            dve.wait_ge(edge_loaded, 16)

            def weights(b, u, half_b, c):
                if c == 0:
                    dve.wait_ge(loaded[u], 16 * LOADS * (half_b + 1))
                dve.wait_ge(pv_done, C * b + c + 1)
                nc.vector.tensor_scalar(pm[:, 4 * (c % 2) + BY_POOL, :], rows[:, u, BY_POOL, :],
                                        small[:, u, c * H + BY_POOL:c * H + BY_POOL + 1], None, ALU.max).then_inc(w_done, 1)
                for h in range(BY_POOL):
                    nc.vector.scalar_tensor_tensor(out=pm[:, 4 * (c % 2) + h, :], in0=rows[:, u, h, :],
                                                   scalar=small[:, u, c * H + h:c * H + h + 1], in1=edge[:, c, :],
                                                   op0=ALU.max, op1=ALU.mult).then_inc(w_done, 1)

            def reciprocal(b):
                dve.wait_ge(den_loaded, 16 * b + 16)
                nc.vector.reciprocal(r_out[:], r_in[:]).then_inc(recip_done, 1)

            def elu(b):
                dve.wait_ge(exp_done, b + 1)
                nc.vector.scalar_tensor_tensor(out=ctx[:], in0=low[:], scalar=-1.0, in1=ctx[:],
                                               op0=ALU.add, op1=ALU.max).then_inc(elu_done, 1)

            def add(b, u):
                dve.wait_ge(turned, b + 2)
                x = k.x[:, bass.ds(b * C, C), :].rearrange("p c f -> p (c f)")
                nc.vector.tensor_tensor(x, k.bank2(4 * u), x, ALU.add).then_inc(added, 1)

            def body(b, u, half_b):
                for c in range(C):
                    weights(b, u, half_b, c)
                    if not is_first(b):
                        if c == RECIP_AT:
                            reciprocal(b - 1)
                        if c == ELU_AT:
                            elu(b - 1)
                        if c == ADD_AT:
                            add(b - 1, 1 - u)

            def last():
                reciprocal(B - 1)
                elu(B - 1)
                add(B - 1, U_LAST)

            Peeled.run(dve, body, last)

        @block.scalar
        def _(act):
            def finish(b, u):
                act.wait_ge(pv_done, C * b + C + 2)
                act.wait_ge(den_stored, 16 * b + 16)
                nc.scalar.copy(den[:], k.bank2(4 * u + 2)).then_inc(copied, 1)
                act.wait_ge(turned, b + 1)
                nc.scalar.copy(ctx[:], k.bank2(4 * u)).then_inc(copied, 1)
                act.wait_ge(quot_done, b + 1)
                act.wait_ge(elu_done, b + 1)
                nc.scalar.activation(low[:], ctx[:], ACT.Relu, scale=-1.0).then_inc(low_done, 1)
                act.wait_ge(low_done, b + 1)
                nc.scalar.activation(low[:], low[:], ACT.Exp, scale=-1.0).then_inc(exp_done, 1)

            with act.Fori(0, B // 2) as pair:
                for u in range(2):
                    finish(2 * pair + u, u)


class ExpertWeights:

    def __init__(self, k, layer, hidden, w1, b1, wg, gate_biases, w2, b2):
        self.layer = layer
        self.arena = a = Arena(k)
        self.K = hidden // P
        self.chunk_cols = D if layer == 0 else E * D
        self.logit_chunks = 1 if layer == 0 else self.K
        self.w1 = a.take([self.K * P])
        self.b1 = a.take([self.K])
        self.wg = a.take([self.logit_chunks, E])
        self.w2 = a.take([self.K * self.chunk_cols])
        self.b2 = a.take([E * D])
        self.bg = a.take([len(gate_biases), E])
        row = lambda v: v.rearrange("(o e) -> o e", o=1).to_broadcast([P, E])
        self.loads = [(self.w1, w1), (self.b1, b1), (self.wg, wg.rearrange("(j p) e -> p j e", p=P)),
                      (self.b2, b2.rearrange("(o e) d -> o (e d)", o=1).to_broadcast([P, E * D]))]
        self.loads += [(self.bg[:, i, :], row(v)) for i, v in enumerate(gate_biases)]
        if layer == 0:
            self.loads.append((self.w2.rearrange("p (k d) -> p k d", d=D), w2.rearrange("e (j p) d -> p (e j) d", p=P)))
        else:
            self.loads += [(self.w2.rearrange("p (k c) -> p k c", k=self.K)[:, :, e * D:(e + 1) * D],
                            w2[e].rearrange("(j p) d -> p j d", p=P)) for e in range(E)]
        self.loaded = k.sem(f"w{layer}_loaded")

    def load(self, sp):
        for dst, src in self.loads:
            sp.dma_start(dst, src).then_inc(self.loaded, 16)


def experts(k, ex, out=None):
    nc, t = k.nc, k.t
    a = ex.arena
    T = 4
    TOK = T * P
    UNITS = B * C // T
    K = ex.K
    ED = E * D
    WS = 64.0
    CHUNK_COLS, LOGIT_CHUNKS = ex.chunk_cols, ex.logit_chunks
    w1_32, b1, wg32, w32, b2_32, bg = ex.w1, ex.b1, ex.wg, ex.w2, ex.b2, ex.bg
    PASSES = 3

    w1 = a.take([2, K * P], F16)
    wg = a.take([2, LOGIT_CHUNKS, E], F16)
    w2 = a.take([2, K, CHUNK_COLS], F16)
    b2 = a.take([ED], F16)
    b2_high = a.take([ED], F16)
    b2_scaled = a.take([ED])
    pick_rows = a.take([P], F16)
    key = a.take([E])

    stats = a.take([T, 6])
    tmp = a.take([3, T])
    mean, ve, rs = a.take([T]), a.take([T]), a.take([T])
    xn = a.take([T, D])
    xT = a.take([2, 2, TOK], F16)
    h32 = a.take([2, TOK])
    h = a.take([2, 2, K, TOK], F16)
    prod = a.take([2, ED])

    l = a.take([T, E])
    expl = a.take([T, E])
    at = a.take([T, E])
    hot = a.take([2, T, E])
    top = a.take([2, T])
    pick = a.take([T])
    q = a.take([2, T])
    w = a.take([2, T, E])

    (w_high, w_ready, consts, ln_step, pow_done, turned, xhi_done, xlo_done, h_made, h32_done, hi_done, lo_done,
     y_made, biased, prod_done, sum_step, logits_done, gate_step, exp_done, stored) = [
        k.sem(f"m{ex.layer}_{s}") for s in (
            "w_high", "w_ready", "consts", "ln_step", "pow_done", "turned", "xhi_done", "xlo_done", "h_made",
            "h32_done", "hi_done", "lo_done", "y_made", "biased", "prod_done", "sum_step", "logits_done", "gate_step", "exp_done",
            "stored")]
    LN_STEPS = T + COMBINE + T
    DIFF_READY, GATE_STEPS = ((14, 20), (3, 10))[ex.layer]
    SUM_STEPS = 4
    GATE_AT = (3, 4, 5, 6, 12, 13)
    STEPS = 16
    EVERY = STEPS // K
    lane = lambda ap: ap.unsqueeze(1).to_broadcast([P, T, E])
    per = lambda ap: ap.unsqueeze(2).to_broadcast([P, T, E])

    def rows(m):
        return [k.x[:, bass.ds(T * m + i, 1), :].rearrange("p o f -> p (o f)") for i in range(T)]

    def run(eng, body):
        body(-2, 0, False, False, True)
        body(-1, 1, False, True, True)
        with eng.Fori(0, UNITS // 2 - 1) as pair:
            body(2 * pair, 0, True, True, True)
            body(2 * pair + 1, 1, True, True, True)
        body(UNITS - 2, 0, True, True, False)
        body(UNITS - 1, 1, True, False, False)

    with nc.Block() as block:
        @block.sync
        def _(sp):
            if out is not None:
                out_rows = tile_rows(out.rearrange("b n f -> (b n) f"))
                with sp.Fori(0, UNITS) as m:
                    sp.wait_ge(sum_step, SUM_STEPS * T * m + SUM_STEPS * (T + 2))
                    sp.dma_start(out_rows[:, bass.ds(T * m, T), :], k.x[:, bass.ds(T * m, T), :]).then_inc(stored, 16)
                sp.wait_ge(stored, 16 * UNITS)

        @block.tensor
        def _(pe):
            pe.sem_inc(turned, 1)
            pe.sem_inc(h_made, 2 * K)
            pe.sem_inc(y_made, 2 * T)

            def turn(m, u):
                pe.wait_ge(ln_step, LN_STEPS * m + LN_STEPS + 1)
                pe.wait_ge(xlo_done, m + 1)
                for i in range(T):
                    last = nc.tensor.transpose(k.ps[:, 6, i * P:(i + 1) * P], xn[:, i, :], k.ident[:])
                last.then_inc(turned, 1)

            def hidden(m, u, j):
                if j == 0:
                    pe.wait_ge(xlo_done, m + 2)
                pe.wait_ge(h32_done, K * m + j + 1)
                for n, (wp, xp) in enumerate(((0, 0), (0, 1), (1, 0))):
                    last = nc.tensor.matmul(k.ps[:, 4 + j % 2, :], w1[:, wp, j * P:(j + 1) * P], xT[:, u, xp, :],
                                            start=(n == 0), stop=(n == PASSES - 1))
                last.then_inc(h_made, 1)

            def logits(m, u):
                pe.wait_ge(gate_step, GATE_STEPS * m + 1)
                if ex.layer == 1:
                    pe.wait_ge(lo_done, K * m + K + 2)
                for i in range(T):
                    n = 0
                    for j in range(LOGIT_CHUNKS):
                        for ap, wp in ((0, 0), (0, 1), (1, 0)):
                            src = h[:, u, ap, j, :] if ex.layer == 1 else xT[:, u, ap, :]
                            last = nc.tensor.matmul(k.ps[:, 7, i * E:(i + 1) * E], src[:, i * P:(i + 1) * P], wg[:, wp, j, :],
                                                    start=(n == 0), stop=(n == PASSES * LOGIT_CHUNKS - 1))
                            n += 1
                last.then_inc(logits_done, 1)

            def outputs(m, u, i, quarter):
                bank = 2 * (i % 2)
                if quarter == 0:
                    if i == 0:
                        pe.wait_ge(lo_done, K * m + K + 2)
                    pe.wait_ge(prod_done, T * (m + 1) + i + 1)
                    if ex.layer == 0:
                        for half in range(2):
                            nc.tensor.matmul(k.ps[:, bank + half, :], pick_rows, halves(b2)[half],
                                             start=True, stop=False, skip_group_check=True)
                for j in range(quarter * K // 4, (quarter + 1) * K // 4):
                    for hp, wp in ((0, 0), (0, 1), (1, 0)):
                        for piece in range(max(1, CHUNK_COLS // 512)):
                            n = min(512, CHUNK_COLS)
                            at_col = piece * n if ex.layer == 1 else (j * E // K) * D
                            last = nc.tensor.matmul(k.bank2(bank)[:, at_col:at_col + n], h[:, u, hp, j, i * P:(i + 1) * P],
                                                    w2[:, wp, j, piece * n:(piece + 1) * n],
                                                    start=(ex.layer == 1 and j == 0 and (hp, wp) == (0, 0)), stop=True,
                                                    skip_group_check=True)
                if quarter == 3:
                    last.then_inc(y_made, 1)

            def body(n, u, do_outputs, do_hidden, do_norm):
                if do_hidden and not do_outputs:
                    pe.wait_ge(w_ready, 5)
                for s in range(STEPS):
                    if do_hidden and s % EVERY == 0:
                        hidden(n + 1, 1 - u, s // EVERY)
                    if do_outputs:
                        outputs(n, u, s // 4, s % 4)
                    if do_norm and s == 8:
                        turn(n + 2, u)
                    if do_hidden and s == (1, STEPS - 1)[ex.layer]:
                        logits(n + 1, 1 - u)

            run(pe, body)

        @block.scalar
        def _(act):
            act.sem_inc(h32_done, 2)
            act.wait_ge(ex.loaded, 16 * len(ex.loads))
            for dst, src in ((w1[:, 0, :], w1_32), (wg[:, 0], wg32), (b2_high, b2_32),
                             (w2[:, 0].rearrange("p k c -> p (k c)"), w32)):
                nc.scalar.activation(dst, src, ACT.Identity, scale=WS).then_inc(w_high, 1)
            if ex.layer == 1:
                nc.scalar.activation(b2_scaled, b2_32, ACT.Identity, scale=WS).then_inc(w_high, 1)

            def body(n, u, do_outputs, do_hidden, do_norm):
                if ex.layer == 1 and do_outputs:
                    act.wait_ge(gate_step, GATE_STEPS * n + GATE_STEPS + DIFF_READY)
                    nc.scalar.activation(expl, l, ACT.Exp).then_inc(exp_done, 1)
                m, v = n + 1, 1 - u
                for s in range(STEPS):
                    if do_hidden and s % EVERY == 0:
                        j = s // EVERY
                        act.wait_ge(lo_done, K * m + j + 1)
                        act.wait_ge(h_made, K * m + j + 1 + 2 * K)
                        nc.scalar.activation(h32[:, j % 2, :], k.ps[:, 4 + j % 2, :], (ACT.Relu, ACT.Gelu)[ex.layer],
                                             bias=b1[:, j:j + 1], scale=1.0 / WS).then_inc(h32_done, 1)
                        if j == 0:
                            act.wait_ge(y_made, T * m + T)
                        act.wait_ge(h32_done, K * m + j + 3)
                        nc.scalar.copy(h[:, v, 0, j, :], h32[:, j % 2, :]).then_inc(hi_done, 1)
                    if ex.layer == 0 and do_hidden and s == 8:
                        act.wait_ge(gate_step, GATE_STEPS * m + GATE_STEPS + DIFF_READY)
                        nc.scalar.activation(q[:, 1, :], pick, ACT.Exp).then_inc(exp_done, 1)
                    if do_norm and s == 9:
                        act.wait_ge(h_made, K * (n + 2) + K)
                        act.wait_ge(turned, n + 2 + 2)
                        nc.scalar.copy(xT[:, u, 0, :], k.ps[:, 6, :]).then_inc(xhi_done, 1)

            run(act, body)

        @block.vector
        def _(dve):
            tt, stt, ts = nc.vector.tensor_tensor, nc.vector.scalar_tensor_tensor, nc.vector.tensor_scalar
            red = nc.vector.tensor_reduce
            dve.sem_inc(ln_step, 1)
            dve.sem_inc(xlo_done, 1)
            dve.sem_inc(lo_done, 2)
            dve.sem_inc(prod_done, T + 2)
            dve.sem_inc(gate_step, GATE_STEPS)

            def statistics(m):
                base = LN_STEPS * m + 1
                dve.wait_ge(ln_step, base)
                x = rows(m)
                for i in range(T):
                    nc.vector.bn_stats(stats[:, i, :], x[i]).then_inc(ln_step, 1)
                dve.wait_ge(ln_step, base + T)
                combine_stats(nc, Steps(dve, ln_step, base + T), stats, mean, ve, tmp)

            def normalise(m):
                dve.wait_ge(pow_done, m + 1)
                dve.wait_ge(turned, m + 1)
                x = rows(m)
                for i in range(T):
                    ts(xn[:, i, :], x[i], mean[:, i:i + 1], rs[:, i:i + 1], ALU.subtract, ALU.mult).then_inc(ln_step, 1)

            def gate(m, v):
                s = Steps(dve, gate_step, GATE_STEPS * m + GATE_STEPS)
                dve.wait_ge(logits_done, m + 1)
                dve.wait_ge(prod_done, T * m + 2)
                s.did(stt(out=l, in0=k.ps[:, 7, 0:T * E].rearrange("p (n e) -> p n e", e=E), scalar=1.0 / WS,
                          in1=lane(bg[:, 0, :]), op0=ALU.mult, op1=ALU.add))
                s.wait()
                if ex.layer == 0:
                    s.did(tt(l, l, lane(bg[:, 1, :]), ALU.add))
                    for j in range(2):
                        s.wait()
                        s.did(red(top[:, j, :], l, AX.X, ALU.max))
                        s.wait()
                        s.did(tt(at, l, per(top[:, j, :]), ALU.is_equal))
                        yield
                        s.wait()
                        s.did(tt(at, at, lane(key), ALU.mult))
                        s.wait()
                        s.did(red(pick, at, AX.X, ALU.max))
                        s.wait()
                        s.did(tt(hot[:, j], at, per(pick), ALU.is_equal))
                        if j == 0:
                            s.wait()
                            s.did(stt(out=l, in0=hot[:, 0], scalar=-3e38, in1=l, op0=ALU.mult, op1=ALU.add))
                            yield
                    s.wait()
                    s.did(tt(pick, top[:, 1, :], top[:, 0, :], ALU.subtract))
                    assert s.n == DIFF_READY
                    yield
                    dve.wait_ge(exp_done, m + 1)
                    s.did(ts(q[:, 0, :], q[:, 1, :], 1.0, WS, ALU.add, ALU.mult))
                    s.wait()
                    s.did(nc.vector.reciprocal(q[:, 0, :], q[:, 0, :]))
                    s.wait()
                    s.did(tt(q[:, 1, :], q[:, 1, :], q[:, 0, :], ALU.mult))
                    s.did(tt(w[:, v], hot[:, 0], per(q[:, 0, :]), ALU.mult))
                    yield
                    s.wait()
                    s.did(tt(at, hot[:, 1], per(q[:, 1, :]), ALU.mult))
                    s.wait()
                    s.did(tt(w[:, v], w[:, v], at, ALU.add))
                else:
                    s.did(red(pick, l, AX.X, ALU.max))
                    s.wait()
                    s.did(tt(l, l, per(pick), ALU.subtract))
                    assert s.n == DIFF_READY
                    s.wait()
                    s.did(ts(at, l, 0.0, None, ALU.is_ge))
                    s.wait()
                    s.did(tt(at, at, lane(key), ALU.mult))
                    s.wait()
                    s.did(red(pick, at, AX.X, ALU.max))
                    s.wait()
                    s.did(tt(hot[:, 0], at, per(pick), ALU.is_equal))
                    dve.wait_ge(exp_done, m + 1)
                    s.did(red(q[:, 0, :], expl, AX.X, ALU.add))
                    s.wait()
                    s.did(nc.vector.reciprocal(q[:, 0, :], q[:, 0, :]))
                    s.wait()
                    s.did(stt(out=w[:, v], in0=hot[:, 0], scalar=1.0 / WS, in1=per(q[:, 0, :]), op0=ALU.mult, op1=ALU.mult))
                assert s.n == GATE_STEPS
                s.wait()

            def body(n, u, do_outputs, do_hidden, do_norm):
                if do_hidden and not do_outputs:
                    dve.wait_ge(consts, 4)
                    for i, (dst, src, high) in enumerate((
                            (w1[:, 1, :], w1_32, w1[:, 0, :]), (wg[:, 1], wg32, wg[:, 0]),
                            (b2[HS:2 * HS, :], b2_32[HS:2 * HS, :], b2_high[HS:2 * HS, :]),
                            (w2[:, 1].rearrange("p k c -> p (k c)"), w32, w2[:, 0].rearrange("p k c -> p (k c)")))):
                        dve.wait_ge(w_high, i + 1)
                        stt(out=dst, in0=src, scalar=WS, in1=high, op0=ALU.mult, op1=ALU.subtract).then_inc(w_ready, 1)
                    nc.vector.tensor_copy(b2[0:HS, :], b2_high[0:HS, :]).then_inc(w_ready, 1)
                    if ex.layer == 1:
                        dve.wait_ge(w_high, 5)
                m, v = n + 1, 1 - u
                if ex.layer == 1 and do_outputs:
                    for _ in gate(n, u):
                        pass
                pieces = gate(m, v) if ex.layer == 0 and do_hidden else ()
                for s in range(STEPS):
                    if do_hidden and s % EVERY == 0:
                        j = s // EVERY
                        dve.wait_ge(hi_done, K * m + j + 1)
                        tt(h[:, v, 1, j, :], h32[:, j % 2, :], h[:, v, 0, j, :], ALU.subtract).then_inc(lo_done, 1)
                    if pieces and s in GATE_AT:
                        next(pieces, None)
                    if do_norm and s == 0:
                        statistics(n + 2)
                    if do_norm and s == 4:
                        normalise(n + 2)
                    if do_norm and s == 10:
                        dve.wait_ge(xhi_done, n + 2 + 1)
                        tt(xT[:, u, 1, :], k.ps[:, 6, :], xT[:, u, 0, :], ALU.subtract).then_inc(xlo_done, 1)
                    if do_outputs and s % 4 == 3:
                        i = s // 4
                        dve.wait_ge(y_made, T * n + i + 1 + 2 * T)
                        dve.wait_ge(sum_step, SUM_STEPS * (T * n + i) + SUM_STEPS)
                        y = k.bank2(2 * (i % 2))
                        if ex.layer == 1:
                            tt(prod[:, i % 2, :], y, b2_scaled, ALU.add).then_inc(biased, 1)
                            dve.wait_ge(biased, T * n + i + 1)
                            y = prod[:, i % 2, :]
                        tt(prod[:, i % 2, :].rearrange("p (e d) -> p e d", e=E), y.rearrange("p (e d) -> p e d", e=E),
                           w[:, u, i, :].unsqueeze(2).to_broadcast([P, E, D]), ALU.mult).then_inc(prod_done, 1)

            run(dve, body)

        @block.gpsimd
        def _(pool):
            pool.sem_inc(sum_step, 2 * SUM_STEPS)
            for e in range(E):
                nc.gpsimd.memset(key[:, e:e + 1], float(E - e))
            nc.gpsimd.memset(b2, 0.0).then_inc(consts, 1)
            nc.gpsimd.memset(pick_rows, 0.0).then_inc(consts, 1)
            pool.wait_ge(consts, 2)
            for row in (0, HS):
                nc.gpsimd.memset(pick_rows[row:row + 1, :], 1.0).then_inc(consts, 1)
            pool.wait_ge(consts, 4)
            tt = nc.gpsimd.tensor_tensor

            def body(n, u, do_outputs, do_hidden, do_norm):
                if do_norm:
                    m = n + 2
                    pool.wait_ge(ln_step, LN_STEPS * m + 1 + T + COMBINE)
                    tt(rs, ve, k.minus_half[:, 0:T], ALU.pow).then_inc(pow_done, 1)
                if do_outputs:
                    x = rows(n)
                    for i in range(T):
                        base = SUM_STEPS * (T * n + i) + 2 * SUM_STEPS
                        pool.wait_ge(prod_done, T * (n + 1) + i + 3)
                        for step, width in enumerate((ED // 2, ED // 4, ED // 8)):
                            if step:
                                pool.wait_ge(sum_step, base + step)
                            y = prod[:, i % 2, 0:width]
                            tt(y, y, prod[:, i % 2, width:2 * width], ALU.add).then_inc(sum_step, 1)
                        pool.wait_ge(sum_step, base + 3)
                        tt(x[i], x[i], y, ALU.add).then_inc(sum_step, 1)

            run(pool, body)


def weights0(k):
    t = k.t
    return ExpertWeights(k, 0, E * 256, t["L0_ffn_W1p"], t["L0_ffn_b1T"], t["L0_ffn_Wg"], [t["L0_ffn_bg"], t["L0_ffn_bias"]],
                         t["L0_ffn_W2"], t["L0_ffn_b2"])


def weights1(k):
    t = k.t
    return ExpertWeights(k, 1, 512, t["L1_ffn_W1"], t["L1_ffn_b1T"], t["L1_ffn_Wg"], [t["L1_ffn_bg"]],
                         t["L1_ffn_Wd"], t["L1_ffn_bd"])


def build(nc, t, out):
    with ExitStack() as ctx:
        k = Core(nc, ctx, t)
        scr = Scratch(k)
        prepare(k, scr)
        experts0, experts1 = weights0(k), weights1(k)
        attention0(k, scr, experts0)
        experts(k, experts0)
        buffers = Attention1Buffers(k, scr)
        gat_factors(k, scr, buffers)
        attention1(k, scr, buffers, experts1)
        experts(k, experts1, out)


def layouts(inputs):
    a = {n: np.ascontiguousarray(np.asarray(v)) for n, v in inputs.items()}
    a["L0_gnn_W4"] = np.ascontiguousarray(np.stack([a.pop("L0_gnn_W" + c).T for c in "qkvo"], axis=1))
    a["L0_gnn_bqkv"] = np.ascontiguousarray(np.stack([a.pop("L0_gnn_b" + c) for c in "qkv"], axis=1))
    a["L0_gnn_rows"] = np.stack([a.pop("L0_gnn_" + c) for c in ("bo", "gamma", "beta")])
    a["L1_gnn_Wc"] = np.ascontiguousarray(a.pop("L1_gnn_W").transpose(1, 0, 2).reshape(D, D))
    a["L0_ffn_W1p"] = np.ascontiguousarray(a.pop("L0_ffn_W1").transpose(1, 0, 2).reshape(D, -1))
    a["L0_ffn_b1T"] = np.ascontiguousarray(a.pop("L0_ffn_b1").reshape(-1, P).T)
    a["L1_ffn_b1T"] = np.ascontiguousarray(a.pop("L1_ffn_b1").reshape(-1, P).T)
    a["ident"] = np.eye(P, dtype=np.float32)
    return a


def kernel(**inputs):
    import concourse.bacc as bacc
    from concourse.bass_utils import run_bass_kernel_spmd

    nc = bacc.Bacc("TRN2", target_bir_lowering=False, num_devices=1)
    arrays = layouts(inputs)
    t = {n: nc.dram_tensor(n, a.shape, mybir.dt.from_np(a.dtype), kind="ExternalInput").ap() for n, a in arrays.items()}
    out = nc.dram_tensor("out", (B, N, D), F32, kind="ExternalOutput").ap()
    build(nc, t, out)
    r = run_bass_kernel_spmd(nc, [arrays], core_ids=[0])
    return r.results[0]["out"]
```
